# Optimizing a Trainium2 kernel written in Bass

```python
import numpy as np
import jax
import jax.numpy as jnp

def _softmax(x, axis=-1):
    return jax.nn.softmax(x, axis=axis)

def _gelu(x):
    return jax.nn.gelu(x, approximate=True)

def _silu(x):
    return jax.nn.silu(x)

def _sigmoid(x):
    return jax.nn.sigmoid(x)

def _layernorm(x, axis=-1, eps=1e-05):
    m = jnp.mean(x, axis=axis, keepdims=True)
    v = jnp.var(x, axis=axis, keepdims=True)
    return (x - m) / jnp.sqrt(v + eps)

def _scatter_add(tgt, idx, src, axis=0):
    return tgt.at[idx].add(src)

def _segment_sum(src, seg, n):
    return jax.ops.segment_sum(src, seg, n)
kernel_name = 'mk_perceiver_d1_seqx_r8_52bae2'

def setup_inputs(seed: int=0):
    np.random.seed(seed)
    _w = jnp.asarray

    def _rec_inputs():
        import jax
        import jax.numpy as jnp
        _rk = jax.random.key(seed)
        x = -0.0003929 + 0.9999 * jax.random.normal(jax.random.fold_in(_rk, 1), (64, 32, 256), jnp.float32)
        _lenS = 32 - jax.random.randint(jax.random.fold_in(_rk, 7), (64,), 0, max(1, 32 // 4) + 1, jnp.int32)
        _lenS2 = 257 - jax.random.randint(jax.random.fold_in(_rk, 8), (64,), 0, max(1, 257 // 4) + 1, jnp.int32)
        _ctx_2048P = jax.random.normal(jax.random.fold_in(_rk, 11), (64, 16, 256), jnp.float32)
        _ctx_2048c = jax.random.dirichlet(jax.random.fold_in(_rk, 511), 0.3 * jnp.ones((16,), jnp.float32), (64, 257))
        _ctx_2048t = jnp.einsum('bsk,bkd->bsd', _ctx_2048c, _ctx_2048P)
        _ctx_2048t = _ctx_2048t * jax.lax.rsqrt(jnp.mean(jnp.square(_ctx_2048t)) + 1e-12) * 0.953939
        ctx_2048 = -0.000514642 + 1.00011 * (_ctx_2048t + 0.3 * jax.random.normal(jax.random.fold_in(_rk, 611), (64, 257, 256), jnp.float32))
        return (x, ctx_2048)
    x, ctx_2048 = _rec_inputs()

    def _L0_xattn_setup():
        import jax, jax.numpy as jnp
        import numpy as np
        NUM_HEADS = 16

        def _qdq(x):
            s = jnp.maximum(jnp.max(jnp.abs(x), axis=-1, keepdims=True) / 127.0, 1e-08)
            return jnp.clip(jnp.round(x / s), -127.0, 127.0) * s
        key = jax.random.key(seed)
        ks = jax.random.split(key, 8)
        B, N, M, D = (2, 512, 64, 256)
        w_std = 0.02
        return {'x': jax.random.normal(ks[0], (B, N, D), jnp.float32), 'cond': jax.random.normal(ks[1], (B, M, D), jnp.float32), 'wq': jax.random.normal(ks[2], (D, D), jnp.float32) * w_std, 'bq': jax.random.normal(ks[3], (D,), jnp.float32) * w_std, 'wkv': jax.random.normal(ks[4], (2 * D, D), jnp.float32) * w_std, 'bkv': jax.random.normal(ks[5], (2 * D,), jnp.float32) * w_std, 'wp': jax.random.normal(ks[6], (D, D), jnp.float32) * w_std, 'bp': jax.random.normal(ks[7], (D,), jnp.float32) * w_std}
    _L0_xattn_all = _L0_xattn_setup()
    _L0_xattn_in = {k: v for k, v in _L0_xattn_all.items() if k in ('wq', 'bq', 'wkv', 'bkv', 'wp', 'bp')}
    del _L0_xattn_all

    def _L0_attn_setup():
        import jax, jax.numpy as jnp
        import numpy as np
        B, S, D = (2, 256, 256)
        H, DH, GROUPS = (16, 128, 4)
        KV = H // GROUPS
        G = GROUPS
        key = jax.random.key(seed)
        ks = jax.random.split(key, 5)
        sd = 1.0 / np.sqrt(D)
        return {'x': jax.random.normal(ks[0], (B, S, D), dtype=jnp.float32), 'Wq': jax.random.normal(ks[1], (D, H * DH), dtype=jnp.float32) * sd, 'bq': jnp.zeros((H * DH,), dtype=jnp.float32), 'Wk': jax.random.normal(ks[2], (D, KV * DH), dtype=jnp.float32) * sd, 'bk': jnp.zeros((KV * DH,), dtype=jnp.float32), 'Wv': jax.random.normal(ks[3], (D, KV * DH), dtype=jnp.float32) * sd, 'bv': jnp.zeros((KV * DH,), dtype=jnp.float32), 'Wo': jax.random.normal(ks[4], (H * DH, D), dtype=jnp.float32) * (1.0 / np.sqrt(H * DH)), 'bo': jnp.zeros((D,), dtype=jnp.float32)}
    _L0_attn_all = _L0_attn_setup()
    _L0_attn_in = {k: v for k, v in _L0_attn_all.items() if k in ('Wq', 'bq', 'Wk', 'bk', 'Wv', 'bv', 'Wo', 'bo')}
    del _L0_attn_all

    def _L0_ffn_setup():
        import jax, jax.numpy as jnp
        import numpy as np
        HIDDEN = 256
        NUM_EXPERTS = 32
        TOP_K = 4
        MOE_INTER = 96
        GROUP = 2
        NUM_CHUNK = NUM_EXPERTS // GROUP
        CHUNK_INTER = 128
        SMALL_SCALE = 0.05

        def _routing(x2d, gate_w):
            logits = x2d @ gate_w.T
            rw = jax.nn.softmax(logits.astype(jnp.float32), axis=-1)
            scores = jax.nn.sigmoid(logits.astype(jnp.float32))
            _, sel = jax.lax.top_k(scores, TOP_K)
            w = jnp.take_along_axis(rw, sel, axis=-1)
            w = w / w.sum(axis=-1, keepdims=True)
            return (w.astype(x2d.dtype), sel)

        def _moe(x2d, Wg, Wu, Wd, cw):
            g = jnp.einsum('th,ehi->eti', x2d, Wg)
            u = jnp.einsum('th,ehi->eti', x2d, Wu)
            a = jax.nn.silu(g) * u * cw.T[:, :, None]
            return jnp.einsum('eti,eih->th', a, Wd)
        key = jax.random.key(seed)
        ks = jax.random.split(key, 8)
        s = 0.02
        B, S = (2, 256)
        return {'hidden_states': jax.random.normal(ks[0], (B, S, HIDDEN), jnp.float32), 'gate_w': jax.random.normal(ks[1], (NUM_EXPERTS, HIDDEN), jnp.float32) * s, 'Wg': jax.random.normal(ks[2], (NUM_EXPERTS, HIDDEN, MOE_INTER), jnp.float32) * s, 'Wu': jax.random.normal(ks[3], (NUM_EXPERTS, HIDDEN, MOE_INTER), jnp.float32) * s, 'Wd': jax.random.normal(ks[4], (NUM_EXPERTS, MOE_INTER, HIDDEN), jnp.float32) * s, 'cWg': jax.random.normal(ks[5], (NUM_CHUNK, HIDDEN, CHUNK_INTER), jnp.float32) * s, 'cWu': jax.random.normal(ks[6], (NUM_CHUNK, HIDDEN, CHUNK_INTER), jnp.float32) * s, 'cWd': jax.random.normal(ks[7], (NUM_CHUNK, CHUNK_INTER, HIDDEN), jnp.float32) * s}
    _L0_ffn_all = _L0_ffn_setup()
    _L0_ffn_in = {k: v for k, v in _L0_ffn_all.items() if k in ('gate_w', 'Wg', 'Wu', 'Wd', 'cWg', 'cWu', 'cWd')}
    del _L0_ffn_all
    return {'x': x, 'ctx_2048': ctx_2048, 'L0_xattn_wq': _L0_xattn_in['wq'], 'L0_xattn_bq': _L0_xattn_in['bq'], 'L0_xattn_wkv': _L0_xattn_in['wkv'], 'L0_xattn_bkv': _L0_xattn_in['bkv'], 'L0_xattn_wp': _L0_xattn_in['wp'], 'L0_xattn_bp': _L0_xattn_in['bp'], 'L0_attn_Wq': _L0_attn_in['Wq'], 'L0_attn_bq': _L0_attn_in['bq'], 'L0_attn_Wk': _L0_attn_in['Wk'], 'L0_attn_bk': _L0_attn_in['bk'], 'L0_attn_Wv': _L0_attn_in['Wv'], 'L0_attn_bv': _L0_attn_in['bv'], 'L0_attn_Wo': _L0_attn_in['Wo'], 'L0_attn_bo': _L0_attn_in['bo'], 'L0_ffn_gate_w': _L0_ffn_in['gate_w'], 'L0_ffn_Wg': _L0_ffn_in['Wg'], 'L0_ffn_Wu': _L0_ffn_in['Wu'], 'L0_ffn_Wd': _L0_ffn_in['Wd'], 'L0_ffn_cWg': _L0_ffn_in['cWg'], 'L0_ffn_cWu': _L0_ffn_in['cWu'], 'L0_ffn_cWd': _L0_ffn_in['cWd']}

def reference(x, ctx_2048, L0_xattn_wq, L0_xattn_bq, L0_xattn_wkv, L0_xattn_bkv, L0_xattn_wp, L0_xattn_bp, L0_attn_Wq, L0_attn_bq, L0_attn_Wk, L0_attn_bk, L0_attn_Wv, L0_attn_bv, L0_attn_Wo, L0_attn_bo, L0_ffn_gate_w, L0_ffn_Wg, L0_ffn_Wu, L0_ffn_Wd, L0_ffn_cWg, L0_ffn_cWu, L0_ffn_cWd):
    import jax
    import jax.numpy as jnp

    def _L0_xattn_ref(x, cond, wq, bq, wkv, bkv, wp, bp):
        import jax, jax.numpy as jnp
        import numpy as np
        NUM_HEADS = 16

        def _qdq(x):
            s = jnp.maximum(jnp.max(jnp.abs(x), axis=-1, keepdims=True) / 127.0, 1e-08)
            return jnp.clip(jnp.round(x / s), -127.0, 127.0) * s
        B, N, C = x.shape
        M = cond.shape[1]
        H = NUM_HEADS
        Dh = C // H
        q = _qdq(x) @ _qdq(wq).T + bq
        kv = cond @ wkv.T + bkv
        k, v = jnp.split(kv, 2, axis=-1)
        q = q.reshape(B, N, H, Dh)
        k = k.reshape(B, M, H, Dh)
        v = v.reshape(B, M, H, Dh)
        scale = 1.0 / np.sqrt(Dh)
        attn = jax.nn.softmax(jnp.einsum('bnhd,bmhd->bhnm', q, k) * scale, axis=-1)
        o = jnp.einsum('bhnm,bmhd->bnhd', attn, v).reshape(B, N, C)
        out = _qdq(o) @ _qdq(wp).T + bp
        return out

    def _L0_attn_ref(x, Wq, bq, Wk, bk, Wv, bv, Wo, bo):
        import jax, jax.numpy as jnp
        import numpy as np
        B, S, D = (2, 256, 256)
        H, DH, GROUPS = (16, 128, 4)
        KV = H // GROUPS
        G = GROUPS
        b, s, _ = x.shape
        Q = (x @ Wq + bq).reshape(b, s, KV, G, DH)
        K = (x @ Wk + bk).reshape(b, s, KV, DH)
        V = (x @ Wv + bv).reshape(b, s, KV, DH)
        scale = 1.0 / np.sqrt(DH).astype(np.float32)
        scores = jnp.einsum('bqkgd,bpkd->bkgqp', Q, K) * scale
        attn = jax.nn.softmax(scores, axis=-1)
        out = jnp.einsum('bkgqp,bpkd->bqkgd', attn, V)
        out = out.reshape(b, s, H * DH)
        return out @ Wo + bo

    def _L0_ffn_ref(hidden_states, gate_w, Wg, Wu, Wd, cWg, cWu, cWd):
        import jax, jax.numpy as jnp
        import numpy as np
        HIDDEN = 256
        NUM_EXPERTS = 32
        TOP_K = 4
        MOE_INTER = 96
        GROUP = 2
        NUM_CHUNK = NUM_EXPERTS // GROUP
        CHUNK_INTER = 128
        SMALL_SCALE = 0.05

        def _routing(x2d, gate_w):
            logits = x2d @ gate_w.T
            rw = jax.nn.softmax(logits.astype(jnp.float32), axis=-1)
            scores = jax.nn.sigmoid(logits.astype(jnp.float32))
            _, sel = jax.lax.top_k(scores, TOP_K)
            w = jnp.take_along_axis(rw, sel, axis=-1)
            w = w / w.sum(axis=-1, keepdims=True)
            return (w.astype(x2d.dtype), sel)

        def _moe(x2d, Wg, Wu, Wd, cw):
            g = jnp.einsum('th,ehi->eti', x2d, Wg)
            u = jnp.einsum('th,ehi->eti', x2d, Wu)
            a = jax.nn.silu(g) * u * cw.T[:, :, None]
            return jnp.einsum('eti,eih->th', a, Wd)
        B, S, H = hidden_states.shape
        T = B * S
        x = hidden_states.reshape(T, H)
        w, sel = _routing(x, gate_w)
        rows = jnp.arange(T)[:, None]
        cw_large = jnp.zeros((T, NUM_EXPERTS), x.dtype).at[rows, sel].add(w)
        cw_small = jnp.zeros((T, NUM_CHUNK), x.dtype).at[rows, sel // GROUP].add(w)
        large = _moe(x, Wg, Wu, Wd, cw_large)
        small = _moe(x, cWg, cWu, cWd, cw_small)
        return (large + SMALL_SCALE * small).reshape(B, S, H)
    x = x + _L0_xattn_ref(_layernorm(x, axis=-1), ctx_2048, L0_xattn_wq, L0_xattn_bq, L0_xattn_wkv, L0_xattn_bkv, L0_xattn_wp, L0_xattn_bp)
    x = x + _L0_attn_ref(_layernorm(x, axis=-1), L0_attn_Wq, L0_attn_bq, L0_attn_Wk, L0_attn_bk, L0_attn_Wv, L0_attn_bv, L0_attn_Wo, L0_attn_bo)
    x = x + _L0_ffn_ref(_layernorm(x, axis=-1), L0_ffn_gate_w, L0_ffn_Wg, L0_ffn_Wu, L0_ffn_Wd, L0_ffn_cWg, L0_ffn_cWu, L0_ffn_cWd)
    return x

_drawn_inputs = setup_inputs


def setup_inputs(seed=0):
    import zlib

    import numpy as np

    out = dict(_drawn_inputs(seed))
    spreads = {'L0_attn_bq': (0.0, 0.354),
     'L0_attn_bk': (0.0, 2.0),
     'L0_attn_bv': (0.0, 0.1),
     'L0_attn_bo': (0.0, 0.1)}
    factors = {'L0_xattn_wq': 8.0,
     'L0_xattn_bq': 59.383,
     'L0_xattn_bkv': 7.315,
     'L0_ffn_gate_w': 8.0,
     'L0_ffn_Wg': 8.0,
     'L0_ffn_Wu': 8.0,
     'L0_ffn_Wd': 8.0,
     'L0_ffn_cWg': 8.0,
     'L0_ffn_cWu': 8.0,
     'L0_ffn_cWd': 8.0}
    for name, (base, spread) in spreads.items():
        noise = np.random.default_rng([zlib.crc32(name.encode()), seed]).standard_normal(out[name].shape)
        drawn = base * np.exp(spread * noise) if base else spread * noise
        out[name] = jnp.asarray(drawn.astype(out[name].dtype))
    for name, factor in factors.items():
        out[name] = (out[name] * factor).astype(out[name].dtype)
    return out
```

```python
import concourse.bass as bass
from concourse import mybir
from contextlib import ExitStack

F32 = mybir.dt.float32
F32R = mybir.dt.float32r
ALU = mybir.AluOpType
ACT = mybir.ActivationFunctionType
AX = mybir.AxisListType.X

P = 128
D = 256
DC = D // P
NB, NQ, NK = 64, 32, 257
T = NB * NQ
NT = T // P
BT = P // NQ
XH, XD = 16, 16
RB = XH // 4
RW = D // RB
KP = NK + 1
SH, SD, KV = 16, 128, 4
SG = SH // KV
GT = 4
GW = GT * P
NG = NT // GT
NE, EI = 32, 96
NC, CI = 16, 128
INTER = NE * EI + NC * CI
SB = 4
BW = SB * P
NBLK = INTER // BW
CWR = 2 * NE + 2 * NC
EPS = 1e-5
ROUND = 12582912.0
QMAX = 127.0
SMALL_SCALE = 0.05
SATURATED = 16.6355


def f32(ap):
    return ap.bitcast(F32)


class Steps:

    def __init__(self, eng, sem):
        self.eng, self.sem, self.base, self.n = eng, sem, 0, 0

    def begin(self, i, per_round, before=0):
        self.base, self.n, self.per_round = i * per_round + before, 0, per_round

    def end(self):
        assert self.n == self.per_round, (self.n, self.per_round)

    def then(self, ins):
        self.n += 1
        ins.then_inc(self.sem, 1)
        self.eng.wait_ge(self.sem, self.base + self.n)


def program(nc, t, out):
    vlast_dram = nc.dram_tensor("vlast_scratch", (NB, RB, D), F32, kind="Internal").ap()
    ctx = ExitStack()
    with ctx:
        X = ctx.enter_context(nc.sbuf_tensor("resid", [P, NT, D], F32))
        otok = ctx.enter_context(nc.sbuf_tensor("otok", [P, NT, D], F32))
        wpT_h = ctx.enter_context(nc.sbuf_tensor("wpT_h", [P, DC, D], F32R))
        wpT_l = ctx.enter_context(nc.sbuf_tensor("wpT_l", [P, DC, D], F32R))
        ident = ctx.enter_context(nc.sbuf_tensor("ident", [P, P], F32))
        mv = ctx.enter_context(nc.sbuf_tensor("mv", [P, NT, 2], F32))
        rstd = ctx.enter_context(nc.sbuf_tensor("rstd", [P, NT], F32))
        ps = ctx.enter_context(nc.psum_tensor("ps", [P, 8, 512], F32))
        with ExitStack() as cross:
            qT = [cross.enter_context(nc.sbuf_tensor(f"qT_{x}", [P, DC, T], F32R)) for x in ("hi", "lo")]
            phase_queries(nc, t, X, wpT_h, wpT_l, ident, mv, rstd, ps, qT, vlast_dram)
            phase_cross(nc, t, X, otok, ps, qT, ident, vlast_dram)
        phase_self(nc, t, X, otok, wpT_h, wpT_l, ident, mv, rstd, ps)
        phase_experts(nc, t, X, ident, mv, rstd, ps)
        phase_store(nc, X, out)


def phase_store(nc, X, out):
    with nc.semaphore("stored") as stored, nc.Block() as block:
        @block.sync
        def _(sp):
            sp.dma_start(out.rearrange("(n p) d -> p n d", p=P), X[:, :, :]).then_inc(stored, 16)
            sp.wait_ge(stored, 16)


def quantise(nc, steps, src, amax, s, rs, tmp, tmp2, ints):
    steps.then(nc.vector.tensor_reduce(amax, src, AX, ALU.max, apply_absolute_value=True))
    steps.then(nc.vector.tensor_scalar(s, amax, 1.0 / QMAX, 1e-8, ALU.mult, ALU.max))
    steps.then(nc.vector.reciprocal(rs, s))
    steps.then(nc.vector.tensor_scalar(tmp, src, rs, ROUND, ALU.mult, ALU.add))
    steps.then(nc.vector.tensor_scalar(tmp2, tmp, ROUND, QMAX, ALU.subtract, ALU.min))
    return nc.vector.tensor_scalar(ints, tmp2, -QMAX, None, ALU.max)


def phase_queries(nc, t, X, wpT_h, wpT_l, ident, mv, rstd, ps, qT, vlast_dram):
    ctx = ExitStack()
    with ctx:
        sb = lambda n, s, d=F32: ctx.enter_context(nc.sbuf_tensor(n, s, d))
        sem = lambda n: ctx.enter_context(nc.semaphore(n))
        wraw = sb("wraw", [P, 2, DC, D])
        wamax = sb("wamax", [P, 2, DC])
        wscale = sb("wscale", [P, 2, DC])
        wrs = sb("wrs", [P, 2, DC])
        wtmp = sb("wtmp", [P, 2, DC, D])
        wtmp2 = sb("wtmp2", [P, 2, DC, D])
        wints = sb("wints", [P, 2, DC, D])
        wdeq = sb("wdeq", [P, 2, DC, D])
        wqT_h = sb("wqT_h", [P, DC, D], F32R)
        wqT_l = sb("wqT_l", [P, DC, D], F32R)
        bq_b = sb("bq_b", [P, D])
        bv_b = sb("bv_b", [P, D])
        clast = sb("clast", [P, DC, NB])
        wv32 = sb("wv32", [P, DC, D])
        vlast = sb("vlast", [NB, RB, D])
        stats = sb("stats", [P, 2, 6])
        std = sb("std", [P, NT])
        xn = sb("xn", [P, 2, D])
        amax = sb("amax", [P, 2])
        sx = sb("sx", [P, 2])
        rs = sb("rs", [P, 2])
        tmp = sb("tmp", [P, 2, D])
        tmp2 = sb("tmp2", [P, 2, D])
        ints = sb("ints", [P, 2, D])
        intsT = sb("intsT", [P, 2, DC, P], F32R)
        q = sb("q", [P, 2, D])
        x_loaded, w_loaded, v_loaded, b_loaded = sem("x_loaded"), sem("w_loaded"), sem("v_loaded"), sem("b_loaded")
        ident_zero, ident_ready = sem("ident_zero"), sem("ident_ready")
        dve_step = sem("dve_step")
        w_deq, w_turned, w_hi, w_split = sem("w_deq"), sem("w_turned"), sem("w_hi"), sem("w_split")
        var_ready, std_ready = sem("var_ready"), sem("std_ready")
        ints_ready, ints_turned, ints_copied = sem("ints_ready"), sem("ints_turned"), sem("ints_copied")
        q_mm, q_ready, q_turned, q_copied, q_split = (sem(n) for n in (
            "q_mm", "q_ready", "q_turned", "q_copied", "q_split"))
        vlast_mm, vlast_ready, vlast_stored = sem("vlast_mm"), sem("vlast_ready"), sem("vlast_stored")
        block = ctx.enter_context(nc.Block())

        @block.sync
        def _(sp):
            sp.dma_start(wraw[:, 0], t["xwq"].rearrange("(c p) i -> p c i", p=P)).then_inc(w_loaded, 16)
            sp.dma_start(wraw[:, 1], t["xwp"].rearrange("(c p) i -> p c i", p=P)).then_inc(w_loaded, 16)
            for g in range(NG):
                sp.dma_start(X[:, g * GT:(g + 1) * GT, :],
                             t["x"][g * GW:(g + 1) * GW, :].rearrange("(n p) d -> p n d", p=P)).then_inc(x_loaded, 16)
            sp.wait_ge(vlast_ready, 1)
            sp.dma_start(vlast_dram, vlast[:, :, :]).then_inc(vlast_stored, 16)
            sp.wait_ge(vlast_stored, 16)

        @block.gpsimd
        def _(pool):
            nc.gpsimd.memset(ident[:, :], 0.0).then_inc(ident_zero, 1)
            pool.wait_ge(ident_zero, 1)
            nc.gpsimd.affine_select(out=ident[:, :], in_=ident[:, :], compare_op=ALU.not_equal, fill=1.0, base=0,
                                    pattern=[[-1, P]], channel_multiplier=1).then_inc(ident_ready, 1)

        @block.scalar
        def _(act):
            act.dma_start(bq_b[:, :], t["xbq"].partition_broadcast(P)).then_inc(b_loaded, 16)
            act.dma_start(bv_b[:, :], t["xbv"].partition_broadcast(P)).then_inc(b_loaded, 16)
            act.dma_start(clast[:, :, :], t["clast"].rearrange("(c p) b -> p c b", p=P)).then_inc(v_loaded, 16)
            act.dma_start(wv32[:, :, :], t["wvT"].rearrange("(c p) o -> p c o", p=P)).then_inc(v_loaded, 16)
            act.wait_ge(w_turned, 1)
            for dst, bank in ((wqT_h, 0), (wpT_h, 1)):
                act.activation(dst[:, :, :], ps[:, bank, :].rearrange("p (c o) -> p c o", c=DC), ACT.Copy).then_inc(w_hi, 1)
            act.wait_ge(var_ready, 1)
            act.activation(std[:, :], rstd[:, :], ACT.Sqrt).then_inc(std_ready, 1)
            with act.Fori(0, NT // 2) as it:
                for u in range(2):
                    act.wait_ge(ints_turned, it * 2 + u + 1)
                    act.activation(intsT[:, u], ps[:, 2 + u, 0:D].rearrange("p (c n) -> p c n", c=DC), ACT.Copy).then_inc(ints_copied, 1)
                for u in range(2):
                    act.wait_ge(q_turned, it * 2 + u + 1)
                    act.activation(qT[0][:, :, bass.ds((it * 2 + u) * P, P)], ps[:, 6 + u, 0:D].rearrange("p (c n) -> p c n", c=DC),
                                   ACT.Copy, scale=float(XD) ** -0.5).then_inc(q_copied, 1)

        @block.vector
        def _(dve):
            steps = Steps(dve, dve_step)
            dve.wait_ge(w_loaded, 32)
            steps.then(nc.vector.tensor_reduce(wamax[:, :, :], wraw[:, :, :, :], AX, ALU.max, apply_absolute_value=True))
            steps.then(nc.vector.tensor_scalar(wscale[:, :, :], wamax[:, :, :], 1.0 / QMAX, 1e-8, ALU.mult, ALU.max))
            steps.then(nc.vector.reciprocal(wrs[:, :, :], wscale[:, :, :]))
            merged = lambda a: a[:, :, :, :].rearrange("p w c i -> p (w c) i")
            rows = lambda a: a[:, :, :].rearrange("p w c -> p (w c)").unsqueeze(2).broadcast_to([P, 2 * DC, D])
            steps.then(nc.vector.tensor_tensor(merged(wtmp), merged(wraw), rows(wrs), ALU.mult))
            steps.then(nc.vector.tensor_scalar(wtmp2[:, :, :, :], wtmp[:, :, :, :], ROUND, ROUND, ALU.add, ALU.subtract))
            steps.then(nc.vector.tensor_scalar(wints[:, :, :, :], wtmp2[:, :, :, :], QMAX, -QMAX, ALU.min, ALU.max))
            nc.vector.tensor_tensor(merged(wdeq), merged(wints), rows(wscale), ALU.mult).then_inc(w_deq, 1)
            for n, (lo, hi, bank) in enumerate(((wqT_l, wqT_h, 0), (wpT_l, wpT_h, 1))):
                dve.wait_ge(w_hi, n + 1)
                nc.vector.tensor_tensor(lo[:, :, :], ps[:, bank, :].rearrange("p (c o) -> p c o", c=DC), f32(hi[:, :, :]),
                                        ALU.subtract).then_inc(w_split, 1)
            dve.wait_ge(vlast_mm, 1)
            dve.wait_ge(b_loaded, 32)
            steps.then(nc.vector.memset(vlast[:, :, :], 0.0))
            for b in range(RB):
                cols = slice(b * RW, (b + 1) * RW)
                last = nc.vector.tensor_tensor(vlast[:, b, cols], ps[0:NB, 7, cols], bv_b[0:NB, cols], ALU.add)
            last.then_inc(vlast_ready, 1)
            dve.wait_ge(x_loaded, 16 * NG)
            token_stats(nc, steps, X, stats, mv)
            nc.vector.tensor_scalar(rstd[:, :], mv[:, :, 1], EPS, None, ALU.add).then_inc(var_ready, 1)
            dve.wait_ge(std_ready, 1)
            steps.then(nc.vector.reciprocal(rstd[:, :], std[:, :]))
            before = steps.n
            with dve.Fori(0, NT // 2) as it:
                steps.begin(it, 12, before)
                for u in range(2):
                    at = it * 2 + u
                    steps.then(nc.vector.tensor_scalar(xn[:, u, :], X[:, bass.ds(at, 1), :].rearrange("p n d -> p (n d)"),
                                                       mv[:, bass.ds(at, 1), 0], rstd[:, bass.ds(at, 1)], ALU.subtract, ALU.mult))
                    quantise(nc, steps, xn[:, u, :], amax[:, u:u + 1], sx[:, u:u + 1], rs[:, u:u + 1], tmp[:, u, :],
                             tmp2[:, u, :], ints[:, u, :]).then_inc(ints_ready, 1)
                for u in range(2):
                    dve.wait_ge(q_mm, it * 2 + u + 1)
                    nc.vector.scalar_tensor_tensor(out=q[:, u, :], in0=ps[:, 4 + u, 0:D], scalar=sx[:, u:u + 1],
                                                   in1=bq_b[:, :], op0=ALU.mult, op1=ALU.add).then_inc(q_ready, 1)
                for u in range(2):
                    dve.wait_ge(q_copied, it * 2 + u + 1)
                    cols = bass.ds((it * 2 + u) * P, P)
                    nc.vector.scalar_tensor_tensor(out=qT[1][:, :, cols], in0=ps[:, 6 + u, 0:D].rearrange("p (c n) -> p c n", c=DC),
                                                   scalar=float(XD) ** -0.5, in1=f32(qT[0][:, :, cols]), op0=ALU.mult,
                                                   op1=ALU.subtract).then_inc(q_split, 1)
                steps.end()

        @block.tensor
        def _(pe):
            pe.wait_ge(ident_ready, 1)
            pe.wait_ge(w_deq, 1)
            for w in range(2):
                for c in range(DC):
                    for o in range(DC):
                        last = nc.tensor.transpose(ps[:, w, c * D + o * P:c * D + (o + 1) * P], wdeq[:, w, o, c * P:(c + 1) * P], ident[:, :])
            last.then_inc(w_turned, 1)
            pe.wait_ge(v_loaded, 32)
            for c in range(DC):
                last = nc.tensor.matmul(ps[0:NB, 7, 0:D], clast[:, c, :], wv32[:, c, :], start=c == 0, stop=c == DC - 1)
            last.then_inc(vlast_mm, 1)
            pe.wait_ge(vlast_ready, 1)
            pe.wait_ge(w_split, 2)
            with pe.Fori(0, NT // 2) as it:
                for u in range(2):
                    pe.wait_ge(ints_ready, it * 2 + u + 1)
                    for c in range(DC):
                        last = nc.tensor.transpose(ps[:, 2 + u, c * P:(c + 1) * P], ints[:, u, c * P:(c + 1) * P], ident[:, :])
                    last.then_inc(ints_turned, 1)
                for u in range(2):
                    pe.wait_ge(ints_copied, it * 2 + u + 1)
                    for n, (c, w) in enumerate((c, w) for c in range(DC) for w in (wqT_h, wqT_l)):
                        last = nc.tensor.matmul(ps[:, 4 + u, 0:D], intsT[:, u, c, :], w[:, c, :], start=n == 0, stop=n == 2 * DC - 1)
                    last.then_inc(q_mm, 1)
                for u in range(2):
                    pe.wait_ge(q_ready, it * 2 + u + 1)
                    for c in range(DC):
                        last = nc.tensor.transpose(ps[:, 6 + u, c * P:(c + 1) * P], q[:, u, c * P:(c + 1) * P], ident[:, :])
                    last.then_inc(q_turned, 1)


THREE = ((0, 0), (0, 1), (1, 0))


def phase_cross(nc, t, X, otok, ps, qT, ident, vlast_dram):
    LASTP = slice(D, D + P)
    ctx = ExitStack()
    with ctx:
        sb = lambda n, s, d=F32: ctx.enter_context(nc.sbuf_tensor(n, s, d))
        sem = lambda n: ctx.enter_context(nc.semaphore(n))
        wraw = sb("wkv_raw", [P, DC, 2 * D])
        wkv_h = sb("wkv_h", [P, DC, 2 * D], F32R)
        wkv_l = sb("wkv_l", [P, DC, 2 * D], F32R)
        bk = sb("bk", [P, DC])
        bv_b = sb("bv_bc", [P, D])
        craw = sb("craw", [P, BT, DC, NK])
        ch = sb("ch", [P, 2, DC, KP], F32R)
        cl = sb("cl", [P, 2, DC, KP], F32R)
        kh = sb("kh", [P, 2, DC, KP], F32R)
        kl = sb("kl", [P, 2, DC, KP], F32R)
        mask = sb("mask", [P, 8, NQ])
        qh = sb("qh", [P, 2, DC, 8, NQ], F32R)
        ql = sb("ql", [P, 2, DC, 8, NQ], F32R)
        v = sb("v", [P, 2, 2, D])
        vl = sb("vl", [RB, BT, D])
        probs = sb("probs", [P, RB, KP])
        nmax = sb("nmax", [P, 2, RB])
        rsum = sb("rsum", [P, 2, RB])
        rinv = sb("rinv", [P, 2, RB])
        pT = sb("pT", [P, 2, 512])
        pT_last = sb("pT_last", [RB, P])
        w_loaded, b_loaded, w_hi, w_split = sem("w_loaded"), sem("b_loaded"), sem("w_hi"), sem("w_split")
        ctx_loaded = [sem(f"ctx_loaded{b}") for b in range(BT)]
        vl_loaded = [sem(f"vl_loaded{b}") for b in range(BT)]
        mask_step, pad_ready = sem("mask_step"), sem("pad_ready")
        ctx_hi, ctx_split = sem("ctx_hi"), sem("ctx_split")
        k_mm, k_hi, k_split, q_masked = sem("k_mm"), sem("k_hi"), sem("k_split"), sem("q_masked")
        s_mm, nmax_ready, exp_done = sem("s_mm"), sem("nmax_ready"), sem("exp_done")
        v_mm, v_ready = sem("v_mm"), sem("v_ready")
        p_turned, pT_dve, pT_act = sem("p_turned"), sem("pT_dve"), sem("pT_act")
        rinv_ready, o_mm, o_ready = sem("rinv_ready"), sem("o_mm"), sem("o_ready")
        block = ctx.enter_context(nc.Block())

        O_CREDIT = 1

        def rounds(eng, one):
            with eng.Fori(0, NT - 1) as it:
                for b in range(BT):
                    one(it, b, 2)
            for b in range(BT):
                one(NT - 1, b, min(2, BT - 1 - b))

        @block.sync
        def _(sp):
            sp.dma_start(wraw[:, :, :], t["wkvT"].rearrange("(c p) o -> p c o", p=P)).then_inc(w_loaded, 16)
            sp.dma_start(bk[:, :], t["xbk"]).then_inc(b_loaded, 16)
            sp.dma_start(bv_b[:, :], t["xbv"].partition_broadcast(P)).then_inc(b_loaded, 16)
            for b in range(BT):
                sp.dma_start(craw[:, b], t["ctxT"][b].rearrange("(c p) k -> p c k", p=P)).then_inc(ctx_loaded[b], 16)
                sp.dma_start(vl[:, b, :], vlast_dram[b]).then_inc(vl_loaded[b], 16)
            with sp.Fori(0, NT - 1) as it:
                for b in range(BT):
                    sp.wait_ge(ctx_split, it * BT + b + 1)
                    sp.dma_start(craw[:, b], t["ctxT"][bass.ds(it * BT + BT + b, 1)].rearrange("a (c p) k -> p (a c) k", p=P)) \
                        .then_inc(ctx_loaded[b], 16)
                    sp.wait_ge(o_mm, it * BT + b + 1)
                    sp.dma_start(vl[:, b, :], vlast_dram[bass.ds(it * BT + BT + b, 1)].rearrange("a r d -> r (a d)")).then_inc(vl_loaded[b], 16)

        @block.gpsimd
        def _(pool):
            for s in (ch, cl):
                nc.gpsimd.memset(f32(s[:, :, :, NK:KP]), 0.0).then_inc(pad_ready, 1)
            nc.gpsimd.memset(mask[:, :, :], 1.0).then_inc(mask_step, 1)
            pool.wait_ge(mask_step, 1)
            nc.gpsimd.affine_select(out=mask[:, :, :], in_=mask[:, :, :], compare_op=ALU.is_ge, fill=0.0, base=0,
                                    pattern=[[-XD, 8], [0, NQ]], channel_multiplier=1).then_inc(mask_step, 1)
            pool.wait_ge(mask_step, 2)
            nc.gpsimd.affine_select(out=mask[:, :, :], in_=mask[:, :, :], compare_op=ALU.is_ge, fill=0.0, base=XD - 1,
                                    pattern=[[XD, 8], [0, NQ]], channel_multiplier=-1).then_inc(mask_step, 1)
            pool.wait_ge(mask_step, 3)
            pool.wait_ge(w_hi, 1)
            nc.gpsimd.tensor_tensor(wkv_l[:, :, :], wraw[:, :, :], f32(wkv_h[:, :, :]), ALU.subtract).then_inc(w_split, 1)
            pool.sem_inc(o_ready, O_CREDIT)

            def prepare(n, slot):
                u = slot % 2
                pool.wait_ge(ctx_hi, n + 1)
                nc.gpsimd.tensor_tensor(cl[:, u, :, 0:NK], craw[:, slot], f32(ch[:, u, :, 0:NK]), ALU.subtract).then_inc(ctx_split, 1)
                for dst, src in ((qh, qT[0]), (ql, qT[1])):
                    for c in range(DC):
                        last = nc.gpsimd.tensor_tensor(dst[:, u, c], f32(src[:, c, bass.ds(n * NQ, NQ)]).unsqueeze(1).broadcast_to([P, 8, NQ]),
                                                       mask[:, :, :], ALU.mult)
                last.then_inc(q_masked, 1)

            def one(it, b, more):
                if more == 2:
                    pool.wait_ge(s_mm, (it * BT + b + 1) * RB)
                    prepare(it * BT + b + 2, (b + 2) % BT)

            prepare(0, 0)
            prepare(1, 1)
            rounds(pool, one)

        @block.scalar
        def _(act):
            act.wait_ge(w_loaded, 16)
            act.activation(wkv_h[:, :, :], wraw[:, :, :], ACT.Copy).then_inc(w_hi, 1)
            act.wait_ge(b_loaded, 32)

            def context_hi(n, slot, loads):
                act.wait_ge(ctx_loaded[slot], loads * 16)
                act.activation(ch[:, slot % 2, :, 0:NK], craw[:, slot], ACT.Copy).then_inc(ctx_hi, 1)

            def keys_hi(n, u):
                for c in range(DC):
                    act.wait_ge(k_mm, n * DC + c + 1)
                    act.activation(kh[:, u, c, :], ps[:, 4 + c, 0:KP], ACT.Identity, bias=bk[:, c:c + 1]).then_inc(k_hi, 1)

            def exps(n, u):
                for r in range(RB):
                    act.wait_ge(nmax_ready, n * 2 + r // 2 + 1)
                    act.activation(probs[:, r, 0:NK], ps[:, r, 0:NK], ACT.Exp, bias=nmax[:, u, r:r + 1],
                                   accum_out=rsum[:, u, r:r + 1]).then_inc(exp_done, 1)

            def one(it, b, more):
                n = it * BT + b
                if more >= 2:
                    act.wait_ge(v_mm, n + 1)
                    context_hi(n + 2, (b + 2) % BT, it + 1 + (b + 2) // BT)
                if more >= 1:
                    keys_hi(n + 1, (b + 1) % 2)
                act.wait_ge(p_turned, n * 3 + 2)
                act.activation(pT[:, 1, :], ps[:, 5, :], ACT.Copy).then_inc(pT_act, 1)
                act.wait_ge(p_turned, n * 3 + 3)
                act.activation(pT_last[:, :], ps[0:RB, 7, LASTP], ACT.Copy).then_inc(pT_act, 1)
                if more >= 1:
                    exps(n + 1, (b + 1) % 2)

            context_hi(0, 0, 1)
            context_hi(1, 1, 1)
            keys_hi(0, 0)
            exps(0, 0)
            rounds(act, one)

        @block.vector
        def _(dve):
            dve.wait_ge(b_loaded, 32)

            def keys_lo(n, u):
                for c in range(DC):
                    dve.wait_ge(k_hi, n * DC + c + 1)
                    nc.vector.scalar_tensor_tensor(out=kl[:, u, c, :], in0=ps[:, 4 + c, 0:KP], scalar=bk[:, c:c + 1],
                                                   in1=f32(kh[:, u, c, :]), op0=ALU.add, op1=ALU.subtract).then_inc(k_split, 1)

            def values(n, u):
                dve.wait_ge(v_mm, n + 1)
                nc.vector.tensor_tensor(v[:, u], ps[:, 6, :].rearrange("p (k d) -> p k d", k=2),
                                        bv_b[:, :].unsqueeze(1).broadcast_to([P, 2, D]), ALU.add).then_inc(v_ready, 1)

            def maxima(n, u):
                for half in range(2):
                    dve.wait_ge(s_mm, n * RB + 2 * half + 2)
                    nc.vector.tensor_reduce(nmax[:, u, 2 * half:2 * half + 2], ps[:, 2 * half:2 * half + 2, 0:NK], AX, ALU.max,
                                            negate=True).then_inc(nmax_ready, 1)

            def one(it, b, more):
                n, u = it * BT + b, b % 2
                if more >= 1:
                    keys_lo(n + 1, 1 - u)
                    values(n + 1, 1 - u)
                dve.wait_ge(exp_done, (n + 1) * RB)
                nc.vector.reciprocal(rinv[:, u, :], rsum[:, u, :]).then_inc(rinv_ready, 1)
                dve.wait_ge(p_turned, n * 3 + 1)
                nc.vector.tensor_copy(pT[:, 0, :], ps[:, 4, :]).then_inc(pT_dve, 1)
                if more >= 1:
                    maxima(n + 1, 1 - u)
                dve.wait_ge(rinv_ready, n + 1)
                dve.wait_ge(o_mm, n + 1)
                for h in range(4):
                    rows = slice(h * NQ, (h + 1) * NQ)
                    dst = otok[b * NQ:(b + 1) * NQ, bass.ds(it, 1), :].rearrange("p n (r h d) -> p (n r) h d", r=RB, h=4)[:, :, h, :]
                    src = ps[rows, 7, 0:D].rearrange("p (r h d) -> p r h d", r=RB, h=4)[:, :, h, :]
                    last = nc.vector.tensor_tensor(dst, src, rinv[rows, u, :].unsqueeze(2).broadcast_to([NQ, RB, XD]), ALU.mult)
                last.then_inc(o_ready, 1)

            keys_lo(0, 0)
            values(0, 0)
            maxima(0, 0)
            rounds(dve, one)

        @block.tensor
        def _(pe):
            pe.wait_ge(w_split, 1)
            pe.wait_ge(pad_ready, 2)
            w2, c2, k2, q2 = (wkv_h, wkv_l), (ch, cl), (kh, kl), (qh, ql)

            def keys(n, u):
                pe.wait_ge(ctx_split, n + 1)
                for o in range(DC):
                    for m, (c, (i, j)) in enumerate((c, x) for c in range(DC) for x in THREE):
                        last = nc.tensor.matmul(ps[:, 4 + o, 0:KP], w2[i][:, c, o * P:(o + 1) * P], c2[j][:, u, c, :],
                                                start=m == 0, stop=m == 3 * DC - 1)
                    last.then_inc(k_mm, 1)

            def values(n, u):
                for kb in range(2):
                    for m, (c, (i, j)) in enumerate((c, x) for c in range(DC) for x in THREE):
                        last = nc.tensor.matmul(ps[:, 6, kb * D:(kb + 1) * D], c2[i][:, u, c, kb * P:(kb + 1) * P],
                                                w2[j][:, c, D:2 * D], start=m == 0, stop=m == 3 * DC - 1)
                last.then_inc(v_mm, 1)

            def scores(n, u):
                pe.wait_ge(k_split, (n + 1) * DC)
                pe.wait_ge(q_masked, n + 1)
                for r in range(RB):
                    rows = slice(r % 2 * 4, r % 2 * 4 + 4)
                    for m, (i, j) in enumerate(THREE):
                        last = nc.tensor.matmul(ps[:, r, 0:KP], q2[i][:, u, r // 2, rows, :].rearrange("p h n -> p (h n)"),
                                                k2[j][:, u, r // 2, :], start=m == 0, stop=m == 2)
                    last.then_inc(s_mm, 1)

            def one(it, b, more):
                n, u = it * BT + b, b % 2
                if more >= 1:
                    keys(n + 1, 1 - u)
                    pe.wait_ge(v_ready, n + 1)
                    values(n + 1, 1 - u)
                pe.wait_ge(exp_done, (n + 1) * RB)
                for kb in range(2):
                    if more >= 1:
                        pe.wait_ge(k_split, (n + 1) * DC + kb + 1)
                    for r in range(RB):
                        last = nc.tensor.transpose(ps[:, 4 + kb, r * P:(r + 1) * P], probs[:, r, kb * P:(kb + 1) * P], ident[:, :])
                    last.then_inc(p_turned, 1)
                pe.wait_ge(o_ready, n + O_CREDIT)
                nc.tensor.transpose(ps[0:RB, 7, LASTP], probs[:, :, NK - 1], ident[:, :]).then_inc(p_turned, 1)
                if more >= 1:
                    scores(n + 1, 1 - u)
                else:
                    pe.wait_ge(v_ready, n + 1)
                pe.wait_ge(vl_loaded[b], it * 16 + 16)
                pe.wait_ge(pT_act, 2 * n + 2)
                nc.tensor.matmul(ps[:, 7, 0:D], pT_last[:, :], vl[:, b, :], start=True, stop=False)
                pe.wait_ge(pT_dve, n + 1)
                for r in range(RB):
                    cols = slice(r * RW, (r + 1) * RW)
                    for kb in range(2):
                        last = nc.tensor.matmul(ps[:, 7, cols], pT[:, kb, r * P:(r + 1) * P], v[:, u, kb, cols],
                                                start=False, stop=r == RB - 1 and kb == 1)
                last.then_inc(o_mm, 1)

            keys(0, 0)
            values(0, 0)
            scores(0, 0)
            rounds(pe, one)


def token_stats(nc, steps, X, stats, mv):
    for n in range(NT):
        steps.then(nc.vector.bn_stats(stats[:, n % 2, :], X[:, n, :]))
        steps.then(nc.vector.bn_aggr(mv[:, n, :], stats[:, n % 2, :]))


def phase_project(nc, t, X, otok, wpT_h, wpT_l, ident, mv, rstd, ps, xT, W):
    CH = 2048
    ctx = ExitStack()
    with ctx:
        sb = lambda n, s, d=F32: ctx.enter_context(nc.sbuf_tensor(n, s, d))
        sem = lambda n: ctx.enter_context(nc.semaphore(n))
        wraw = sb("self_wraw", [P, 2, CH])
        bp_b = sb("bp_b", [P, D])
        bo_b = sb("bo_b", [P, D])
        stats = sb("stats_p", [P, 2, 6])
        std = sb("std_p", [P, NT])
        amax = sb("amax_p", [P, 2])
        so = sb("so_p", [P, 2])
        rs = sb("rs_p", [P, 2])
        tmp = sb("tmp_p", [P, 2, D])
        tmp2 = sb("tmp2_p", [P, 2, D])
        ints = sb("ints_p", [P, 2, D])
        intsT = sb("intsT_p", [P, 2, DC, P], F32R)
        y = sb("y_p", [P, 2, D])
        xn = sb("xn_p", [P, 2, D])
        b_loaded = sem("b_loaded")
        w_loaded = [sem("w_loaded0"), sem("w_loaded1")]
        w_hi, w_split = sem("w_hi"), sem("w_split")
        dve_step = sem("dve_step")
        ints_ready, ints_turned, ints_copied, y_mm = sem("ints_ready"), sem("ints_turned"), sem("ints_copied"), sem("y_mm")
        var_ready, std_ready = sem("var_ready"), sem("std_ready")
        xn_ready, xn_turned, xn_copied = sem("xn_ready"), sem("xn_turned"), sem("xn_copied")
        block = ctx.enter_context(nc.Block())

        chunks = []
        for c in range(DC):
            chunks.append((t["sWq"][c * P:(c + 1) * P, :], [w[:, c, :] for w in W["q"]], SH * SD))
        for name in ("k", "v"):
            for c in range(DC):
                chunks.append((t["sW" + name][c * P:(c + 1) * P, :], [w[:, c, :] for w in W[name]], KV * SD))
        for c in range(2):
            h = SH // 2
            chunks.append((t["sWo"][c * h * SD:(c + 1) * h * SD, :].rearrange("(h p) o -> p h o", p=P),
                           [w[:, c * h:(c + 1) * h, :].rearrange("p h o -> p (h o)") for w in W["o"]], h * D))

        @block.sync
        def _(sp):
            sp.dma_start(bp_b[:, :], t["xbp"].partition_broadcast(P)).then_inc(b_loaded, 16)
            sp.dma_start(bo_b[:, :], t["sbo"].partition_broadcast(P)).then_inc(b_loaded, 16)
            for n, (src, _, w) in enumerate(chunks):
                if n >= 2:
                    sp.wait_ge(w_split, n - 1)
                dst = wraw[:, n % 2, 0:w]
                if len(src.shape) == 3:
                    dst = dst.rearrange("p (h o) -> p h o", o=D)
                sp.dma_start(dst, src).then_inc(w_loaded[n % 2], 16)

        @block.gpsimd
        def _(pool):
            for n, (_, (hi, lo), w) in enumerate(chunks):
                pool.wait_ge(w_loaded[n % 2], 16 * (n // 2 + 1))
                nc.gpsimd.tensor_copy(hi, wraw[:, n % 2, 0:w]).then_inc(w_hi, 1)
                pool.wait_ge(w_hi, n + 1)
                nc.gpsimd.tensor_tensor(lo, wraw[:, n % 2, 0:w], f32(hi), ALU.subtract).then_inc(w_split, 1)

        @block.scalar
        def _(act):
            with act.Fori(0, NT // 2) as it:
                for u in range(2):
                    act.wait_ge(ints_turned, it * 2 + u + 1)
                    act.activation(intsT[:, u], ps[:, 2 + u, 0:D].rearrange("p (c n) -> p c n", c=DC), ACT.Copy).then_inc(ints_copied, 1)
            act.wait_ge(var_ready, 1)
            act.activation(std[:, :], rstd[:, :], ACT.Sqrt).then_inc(std_ready, 1)
            with act.Fori(0, NT // 2) as it:
                for u in range(2):
                    act.wait_ge(xn_turned, it * 2 + u + 1)
                    act.activation(xT[:, :, bass.ds((it * 2 + u) * P, P)], ps[:, 6 + u, 0:D].rearrange("p (c n) -> p c n", c=DC),
                                   ACT.Copy).then_inc(xn_copied, 1)

        @block.vector
        def _(dve):
            steps = Steps(dve, dve_step)
            dve.wait_ge(b_loaded, 32)
            with dve.Fori(0, NT // 2) as it:
                steps.begin(it, 14)
                tile = lambda a, u: a[:, bass.ds(it * 2 + u, 1), :].rearrange("p n d -> p (n d)")
                for u in range(2):
                    quantise(nc, steps, tile(otok, u), amax[:, u:u + 1], so[:, u:u + 1], rs[:, u:u + 1], tmp[:, u, :],
                             tmp2[:, u, :], ints[:, u, :]).then_inc(ints_ready, 1)
                for u in range(2):
                    dve.wait_ge(y_mm, it * 2 + u + 1)
                    steps.then(nc.vector.scalar_tensor_tensor(out=y[:, u, :], in0=ps[:, 4 + u, 0:D], scalar=so[:, u:u + 1],
                                                              in1=bp_b[:, :], op0=ALU.mult, op1=ALU.add))
                    steps.then(nc.vector.tensor_tensor(tile(X, u), tile(X, u), y[:, u, :], ALU.add))
                steps.end()
            done = 14 * (NT // 2)
            steps.begin(0, 2 * NT, done)
            token_stats(nc, steps, X, stats, mv)
            steps.end()
            done += 2 * NT
            nc.vector.tensor_scalar(rstd[:, :], mv[:, :, 1], EPS, None, ALU.add).then_inc(var_ready, 1)
            dve.wait_ge(std_ready, 1)
            steps.begin(0, 1, done)
            steps.then(nc.vector.reciprocal(rstd[:, :], std[:, :]))
            with dve.Fori(0, NT // 2) as it:
                steps.begin(it, 2, done + 1)
                tile = lambda a, u: a[:, bass.ds(it * 2 + u, 1), :].rearrange("p n d -> p (n d)")
                for u in range(2):
                    nc.vector.tensor_scalar(xn[:, u, :], tile(X, u), mv[:, bass.ds(it * 2 + u, 1), 0], rstd[:, bass.ds(it * 2 + u, 1)],
                                            ALU.subtract, ALU.mult).then_inc(xn_ready, 1)
                for u in range(2):
                    dve.wait_ge(xn_copied, it * 2 + u + 1)
                    steps.then(nc.vector.tensor_tensor(tile(X, u), tile(X, u), bo_b[:, :], ALU.add))
                steps.end()

        @block.tensor
        def _(pe):
            with pe.Fori(0, NT // 2) as it:
                for u in range(2):
                    pe.wait_ge(ints_ready, it * 2 + u + 1)
                    for c in range(DC):
                        last = nc.tensor.transpose(ps[:, 2 + u, c * P:(c + 1) * P], ints[:, u, c * P:(c + 1) * P], ident[:, :])
                    last.then_inc(ints_turned, 1)
                for u in range(2):
                    pe.wait_ge(ints_copied, it * 2 + u + 1)
                    for n, (c, w) in enumerate((c, w) for c in range(DC) for w in (wpT_h, wpT_l)):
                        last = nc.tensor.matmul(ps[:, 4 + u, 0:D], intsT[:, u, c, :], w[:, c, :], start=n == 0, stop=n == 2 * DC - 1)
                    last.then_inc(y_mm, 1)
            with pe.Fori(0, NT // 2) as it:
                for u in range(2):
                    pe.wait_ge(xn_ready, it * 2 + u + 1)
                    for c in range(DC):
                        last = nc.tensor.transpose(ps[:, 6 + u, c * P:(c + 1) * P], xn[:, u, c * P:(c + 1) * P], ident[:, :])
                    last.then_inc(xn_turned, 1)


def phase_self(nc, t, X, otok, wpT_h, wpT_l, ident, mv, rstd, ps):
    with ExitStack() as outer:
        sb = lambda n, s, d=F32: outer.enter_context(nc.sbuf_tensor(n, s, d))
        W = {n: [sb(f"sW{n}_{x}", s, F32R) for x in ("hi", "lo")] for n, s in (
            ("q", [P, DC, SH * SD]), ("k", [P, DC, KV * SD]), ("v", [P, DC, KV * SD]), ("o", [P, SH, D]))}
        xT = sb("xT_self", [P, DC, T])
        phase_project(nc, t, X, otok, wpT_h, wpT_l, ident, mv, rstd, ps, xT, W)
        phase_attend(nc, t, X, ident, ps, xT, W)


def phase_attend(nc, t, X, ident, ps, xT, W):
    GB = GW // NQ
    NPROJ = GT + KV * (SG + 1)
    ctx = ExitStack()
    with ctx:
        sb = lambda n, s, d=F32: ctx.enter_context(nc.sbuf_tensor(n, s, d))
        sem = lambda n: ctx.enter_context(nc.semaphore(n))
        x_h, x_l = sb("x_h", [P, DC, GW], F32R), sb("x_l", [P, DC, GW], F32R)
        q = sb("q_self", [P, GB, SG, NQ])
        k = sb("k_self", [P, GW])
        o_h, o_l = sb("o_h", [P, SG, GW], F32R), sb("o_l", [P, SG, GW], F32R)
        v = sb("v_self", [P, GT, KV * SD])
        bq, bk = sb("sbq", [P, SH]), sb("sbk", [P, KV])
        bv_b = sb("sbv_b", [P, KV * SD])
        smax = sb("smax", [P, GB])
        shifted = sb("shifted", [P, GB, NQ])
        probs = sb("probs_self", [P, GB, NQ])
        psum_, pinv = sb("prob_sum", [P, GB]), sb("prob_inv", [P, GB])
        pdiag = sb("pdiag", [P, GT, BT, P])
        b_loaded = sem("b_loaded")
        x_hi, x_split = sem("x_hi"), sem("x_split")
        proj_mm, proj_act, proj_dve = sem("proj_mm"), sem("proj_act"), sem("proj_dve")
        s_mm, s_max, s_shifted, s_exp, s_sum, s_inv, probs_ready = (sem(n) for n in (
            "s_mm", "s_max", "s_shifted", "s_exp", "s_sum", "s_inv", "probs_ready"))
        p_turned, pdiag_zero, pdiag_act, pdiag_dve = sem("p_turned"), sem("pdiag_zero"), sem("pdiag_act"), sem("pdiag_dve")
        o_mm, o_hi, o_split = sem("o_mm"), sem("o_hi"), sem("o_split")
        y_mm, y_added = sem("y_mm"), sem("y_added")
        block = ctx.enter_context(nc.Block())
        O_CREDIT = 2
        Y_CREDIT = 2

        def copies(n):
            on_act = sum((m - GT) % (SG + 1) % 2 == 0 for m in range(GT, n))
            return on_act, n - on_act

        def by_batch(a):
            return a.rearrange("p (b n) -> p b n", b=GB)

        def proj_index(kv, j):
            return GT + kv * (SG + 1) + j

        @block.sync
        def _(sp):
            sp.dma_start(bq[:, :], t["sbq"]).then_inc(b_loaded, 16)
            sp.dma_start(bk[:, :], t["sbk"]).then_inc(b_loaded, 16)
            sp.dma_start(bv_b[:, :], t["sbv"].partition_broadcast(P)).then_inc(b_loaded, 16)

        @block.gpsimd
        def _(pool):
            nc.gpsimd.memset(pdiag[:, :, :, :], 0.0).then_inc(pdiag_zero, 1)
            pool.sem_inc(o_split, O_CREDIT)
            pool.sem_inc(y_added, Y_CREDIT)

        @block.scalar
        def _(act):
            act.wait_ge(b_loaded, 48)
            act.wait_ge(pdiag_zero, 1)
            with act.Fori(0, NG) as g:

                def project_copy(kv, j):
                    if j % 2 == 0:
                        act.wait_ge(proj_mm, g * NPROJ + proj_index(kv, j) + 1)
                        dst, bias = (q[:, :, j, :], bq[:, kv * SG + j:kv * SG + j + 1]) if j < SG else (by_batch(k[:, :]), bk[:, kv:kv + 1])
                        act.activation(dst, by_batch(ps[:, proj_index(kv, j) % 2, :]), ACT.Identity, bias=bias).then_inc(proj_act, 1)

                act.activation(x_h[:, :, :], xT[:, :, bass.ds(g * GW, GW)], ACT.Copy).then_inc(x_hi, 1)
                for j in range(SG + 1):
                    project_copy(0, j)
                for kv in range(KV):
                    act.wait_ge(s_shifted, g * KV + kv + 1)
                    act.activation(probs[:, :, :], shifted[:, :, :], ACT.Exp, scale=float(SD) ** -0.5).then_inc(s_exp, 1)
                    if kv + 1 < KV:
                        for j in range(SG + 1):
                            project_copy(kv + 1, j)
                    act.wait_ge(p_turned, g * KV + kv + 1)
                    for b in range(2):
                        rows = slice(b * NQ, (b + 1) * NQ)
                        last = act.activation(pdiag[rows, :, b, :], ps[rows, 5, :].rearrange("p (j n) -> p j n", j=GT), ACT.Copy)
                    last.then_inc(pdiag_act, 1)
                    for j in range(GT):
                        act.wait_ge(o_mm, (g * KV + kv) * GT + j + 1)
                        dst = o_h[:, :, j * P:(j + 1) * P].rearrange("p h (b n) -> p b h n", b=BT)
                        act.activation(dst, ps[:, 2 + j % 2, :].rearrange("p (b h n) -> p b h n", b=BT, h=SG), ACT.Copy).then_inc(o_hi, 1)

        @block.vector
        def _(dve):
            dve.wait_ge(b_loaded, 48)
            dve.wait_ge(pdiag_zero, 1)
            with dve.Fori(0, NG) as g:

                def project_copy(kv, j):
                    if j % 2:
                        n = proj_index(kv, j)
                        dve.wait_ge(proj_mm, g * NPROJ + n + 1)
                        nc.vector.tensor_scalar(q[:, :, j, :], by_batch(ps[:, n % 2, :]), bq[:, kv * SG + j:kv * SG + j + 1], None,
                                                ALU.add).then_inc(proj_dve, 1)

                def add_output(kv):
                    for half in range(2):
                        dve.wait_ge(y_mm, (g * KV + kv) * 2 + half + 1)
                        x = X[:, bass.ds(g * GT + 2 * half, 2), :].rearrange("p n d -> p (n d)")
                        nc.vector.tensor_tensor(x, x, ps[:, 6 + half, :], ALU.add).then_inc(y_added, 1)

                dve.wait_ge(x_hi, g + 1)
                nc.vector.tensor_tensor(x_l[:, :, :], xT[:, :, bass.ds(g * GW, GW)], f32(x_h[:, :, :]), ALU.subtract).then_inc(x_split, 1)
                for j in range(GT):
                    dve.wait_ge(proj_mm, g * NPROJ + j + 1)
                    nc.vector.tensor_tensor(v[:, j, :], ps[:, j % 2, :], bv_b[:, :], ALU.add).then_inc(proj_dve, 1)
                for j in range(SG + 1):
                    project_copy(0, j)
                for kv in range(KV):
                    n = g * KV + kv + 1
                    scores = ps[:, 4, :].rearrange("p (b k) -> p b k", b=GB)
                    dve.wait_ge(s_mm, n)
                    nc.vector.tensor_reduce(smax[:, :], scores, AX, ALU.max).then_inc(s_max, 1)
                    dve.wait_ge(s_max, n)
                    nc.vector.tensor_tensor(shifted[:, :, :], scores, smax[:, :].unsqueeze(2).broadcast_to([P, GB, NQ]),
                                            ALU.subtract).then_inc(s_shifted, 1)
                    if kv + 1 < KV:
                        for j in range(2):
                            project_copy(kv + 1, j)
                    dve.wait_ge(s_exp, n)
                    nc.vector.tensor_reduce(psum_[:, :], probs[:, :, :], AX, ALU.add).then_inc(s_sum, 1)
                    dve.wait_ge(s_sum, n)
                    nc.vector.reciprocal(pinv[:, :], psum_[:, :]).then_inc(s_inv, 1)
                    dve.wait_ge(s_inv, n)
                    nc.vector.tensor_tensor(probs[:, :, :], probs[:, :, :], pinv[:, :].unsqueeze(2).broadcast_to([P, GB, NQ]),
                                            ALU.mult).then_inc(probs_ready, 1)
                    if kv + 1 < KV:
                        for j in range(2, SG + 1):
                            project_copy(kv + 1, j)
                    dve.wait_ge(p_turned, n)
                    dve.wait_ge(pdiag_act, n)
                    for b in range(2, BT):
                        rows = slice(b * NQ, (b + 1) * NQ)
                        last = nc.vector.tensor_copy(pdiag[rows, :, b, :], ps[rows, 5, :].rearrange("p (j n) -> p j n", j=GT))
                    last.then_inc(pdiag_dve, 1)
                    if kv:
                        add_output(kv - 1)
                    for j in range(GT):
                        dve.wait_ge(o_hi, (g * KV + kv) * GT + j + 1)
                        dst = o_l[:, :, j * P:(j + 1) * P].rearrange("p h (b n) -> p b h n", b=BT)
                        hi = f32(o_h[:, :, j * P:(j + 1) * P]).rearrange("p h (b n) -> p b h n", b=BT)
                        nc.vector.tensor_tensor(dst, ps[:, 2 + j % 2, :].rearrange("p (b h n) -> p b h n", b=BT, h=SG), hi,
                                                ALU.subtract).then_inc(o_split, 1)
                add_output(KV - 1)

        @block.tensor
        def _(pe):
            x2, o2 = (x_h, x_l), (o_h, o_l)
            with pe.Fori(0, NG) as g:

                def copied(n):
                    on_act, on_dve = copies(n + 1)
                    if copies(n) == (on_act, on_dve - 1):
                        pe.wait_ge(proj_dve, g * copies(NPROJ)[1] + on_dve)
                    else:
                        pe.wait_ge(proj_act, g * copies(NPROJ)[0] + on_act)

                def bank_free(n):
                    if n >= 2:
                        copied(n - 2)

                def project(kv):
                    for j in range(SG + 1):
                        n = proj_index(kv, j)
                        bank_free(n)
                        w, col = (W["q"], (kv * SG + j) * SD) if j < SG else (W["k"], kv * SD)
                        for m, (c, (a, b)) in enumerate((c, x) for c in range(DC) for x in THREE):
                            last = nc.tensor.matmul(ps[:, n % 2, :], w[a][:, c, col:col + SD], x2[b][:, c, :],
                                                    start=m == 0, stop=m == 3 * DC - 1)
                        last.then_inc(proj_mm, 1)

                def score(kv):
                    copied(proj_index(kv, SG - 1))
                    copied(proj_index(kv, SG))
                    for b in range(GB):
                        cols = slice(b * NQ, (b + 1) * NQ)
                        last = nc.tensor.matmul(ps[:, 4, cols], q[:, b].rearrange("p h n -> p (h n)"), k[:, cols], start=True, stop=True)
                    last.then_inc(s_mm, 1)

                def project_output(kv):
                    pe.wait_ge(o_split, (g * KV + kv) * GT + GT + O_CREDIT)
                    for j in range(GT):
                        if j % 2 == 0:
                            pe.wait_ge(y_added, (g * KV + kv) * 2 + j // 2 + 1)
                        for m, (h, (a, b)) in enumerate((h, x) for h in range(SG) for x in THREE):
                            last = nc.tensor.matmul(ps[:, 6 + j // 2, j % 2 * D:(j % 2 + 1) * D], o2[a][:, h, j * P:(j + 1) * P],
                                                    W["o"][b][:, kv * SG + h, :], start=m == 0, stop=m == 3 * SG - 1)
                        if j % 2:
                            last.then_inc(y_mm, 1)

                pe.wait_ge(x_split, g + 1)
                for j in range(GT):
                    bank_free(j)
                    for m, (c, (a, b)) in enumerate((c, x) for c in range(DC) for x in THREE):
                        last = nc.tensor.matmul(ps[:, j % 2, :], x2[a][:, c, j * P:(j + 1) * P], W["v"][b][:, c, :],
                                                start=m == 0, stop=m == 3 * DC - 1)
                    last.then_inc(proj_mm, 1)
                project(0)
                score(0)
                for kv in range(KV):
                    if kv + 1 < KV:
                        project(kv + 1)
                    pe.wait_ge(probs_ready, g * KV + kv + 1)
                    for j in range(GT):
                        last = nc.tensor.transpose(ps[:, 5, j * P:(j + 1) * P],
                                                   probs[:, j * BT:(j + 1) * BT, :].rearrange("p b k -> p (b k)"), ident[:, :])
                    last.then_inc(p_turned, 1)
                    if kv:
                        project_output(kv - 1)
                    pe.wait_ge(pdiag_act, g * KV + kv + 1)
                    pe.wait_ge(pdiag_dve, g * KV + kv + 1)
                    for j in range(GT):
                        pe.wait_ge(o_split, (g * KV + kv) * GT + j + 1)
                        nc.tensor.matmul(ps[:, 2 + j % 2, :], v[:, j, kv * SD:(kv + 1) * SD], pdiag[:, j].rearrange("p b n -> p (b n)"),
                                         start=True, stop=True).then_inc(o_mm, 1)
                    if kv + 1 < KV:
                        score(kv + 1)
                project_output(KV - 1)


def phase_experts(nc, t, X, ident, mv, rstd, ps):
    with ExitStack() as outer:
        sb = lambda n, s, d=F32: outer.enter_context(nc.sbuf_tensor(n, s, d))
        x_h, x_l = sb("xe_h", [P, DC, T], F32R), sb("xe_l", [P, DC, T], F32R)
        cwT = sb("cwT", [CWR, T], F32R)
        phase_route(nc, t, X, ident, mv, rstd, ps, x_h, x_l, cwT)
        phase_mix(nc, t, X, ps, x_h, x_l, cwT)


def phase_route(nc, t, X, ident, mv, rstd, ps, x_h, x_l, cwT):
    TOP = 4
    ctx = ExitStack()
    with ctx:
        sb = lambda n, s, d=F32: ctx.enter_context(nc.sbuf_tensor(n, s, d))
        sem = lambda n: ctx.enter_context(nc.semaphore(n))
        gate = sb("gate", [P, DC, NE])
        stats = sb("stats_r", [P, 2, 6])
        std = sb("std_r", [P, NT])
        xn = sb("xn_r", [P, 2, D])
        x32 = sb("x32", [P, 2, DC, P])
        logits = sb("logits", [P, NT, NE])
        key = sb("key", [P, NT, NE])
        top = sb("top", [P, NT, 8])
        above, equal = sb("above", [P, NT, NE]), sb("equal", [P, NT, NE])
        scan = [sb("scan0", [P, NT, NE]), sb("scan1", [P, NT, NE])]
        count = sb("count", [P, NT])
        left = sb("left", [P, NT])
        first, chosen = sb("first", [P, NT, NE]), sb("chosen", [P, NT, NE])
        shifted, expd, soft, weight = (sb(n, [P, NT, NE]) for n in ("shift_r", "expd", "soft", "weight"))
        small = sb("small", [P, NT, NC])
        norm, inv = sb("norm_r", [P, NT]), sb("inv_r", [P, NT])
        cw = sb("cw", [P, NT, CWR], F32R)
        g_loaded, dve_step, var_ready, std_ready = sem("g_loaded"), sem("dve_step"), sem("var_ready"), sem("std_ready")
        xn_ready, xn_turned, x_hi, x_split = sem("xn_ready"), sem("xn_turned"), sem("x_hi"), sem("x_split")
        l_mm, l_ready = sem("l_mm"), sem("l_ready")
        shift_ready, exp_ready, cw_ready, cw_turned, cw_copied = (sem(n) for n in (
            "shift_ready", "exp_ready", "cw_ready", "cw_turned", "cw_copied"))
        block = ctx.enter_context(nc.Block())

        @block.sync
        def _(sp):
            sp.dma_start(gate[:, :, :], t["gateT"].rearrange("(c p) e -> p c e", p=P)).then_inc(g_loaded, 16)

        @block.scalar
        def _(act):
            act.wait_ge(var_ready, 1)
            act.activation(std[:, :], rstd[:, :], ACT.Sqrt).then_inc(std_ready, 1)
            with act.Fori(0, NT // 2) as it:
                for u in range(2):
                    act.wait_ge(xn_turned, it * 2 + u + 1)
                    turned = ps[:, u, 0:D].rearrange("p (c n) -> p c n", c=DC)
                    act.activation(x32[:, u], turned, ACT.Copy)
                    act.activation(x_h[:, :, bass.ds((it * 2 + u) * P, P)], turned, ACT.Copy).then_inc(x_hi, 1)
            act.wait_ge(shift_ready, 1)
            act.activation(expd[:, :, :], shifted[:, :, :], ACT.Exp).then_inc(exp_ready, 1)
            for g in range(NG):
                act.wait_ge(cw_turned, g + 1)
                act.activation(cwT[:, g * GW:(g + 1) * GW], ps[0:CWR, 4 + g, :], ACT.Copy).then_inc(cw_copied, 1)

        @block.vector
        def _(dve):
            steps = Steps(dve, dve_step)
            token_stats(nc, steps, X, stats, mv)
            nc.vector.tensor_scalar(rstd[:, :], mv[:, :, 1], EPS, None, ALU.add).then_inc(var_ready, 1)
            dve.wait_ge(std_ready, 1)
            steps.then(nc.vector.reciprocal(rstd[:, :], std[:, :]))
            tile = lambda a, at: a[:, bass.ds(at, 1), :].rearrange("p n d -> p (n d)")
            with dve.Fori(0, NT // 2) as it:
                for u in range(2):
                    at = it * 2 + u
                    nc.vector.tensor_scalar(xn[:, u, :], tile(X, at), mv[:, bass.ds(at, 1), 0], rstd[:, bass.ds(at, 1)],
                                            ALU.subtract, ALU.mult).then_inc(xn_ready, 1)
                for u in range(2):
                    at = it * 2 + u
                    dve.wait_ge(x_hi, at + 1)
                    cols = bass.ds(at * P, P)
                    nc.vector.tensor_tensor(x_l[:, :, cols], ps[:, u, 0:D].rearrange("p (c n) -> p c n", c=DC), f32(x_h[:, :, cols]),
                                            ALU.subtract).then_inc(x_split, 1)
                    dve.wait_ge(l_mm, at + 1)
                    nc.vector.tensor_copy(tile(logits, at), ps[:, 2 + u, 0:NE]).then_inc(l_ready, 1)
            dve.wait_ge(l_ready, NT)
            v = nc.vector
            all_ = lambda a: a[:, :, :]
            over = lambda a: a.unsqueeze(2).broadcast_to([P, NT, NE])
            steps.then(v.tensor_scalar(all_(key), all_(logits), SATURATED, None, ALU.min))
            for n in range(NT):
                last = v.max(top[:, n, :], key[:, n, :])
            steps.then(last)
            fourth = over(top[:, :, TOP - 1])
            steps.then(v.tensor_tensor(all_(above), all_(key), fourth, ALU.is_gt))
            steps.then(v.tensor_tensor(all_(equal), all_(key), fourth, ALU.is_equal))
            steps.then(v.tensor_reduce(count[:, :], all_(above), AX, ALU.add))
            steps.then(v.tensor_scalar(left[:, :], count[:, :], -1.0, float(TOP), ALU.mult, ALU.add))
            src, s = equal, 1
            while s < NE:
                dst = scan[0] if src is not scan[0] else scan[1]
                steps.then(v.tensor_copy(dst[:, :, 0:s], src[:, :, 0:s]))
                steps.then(v.tensor_tensor(dst[:, :, s:NE], src[:, :, s:NE], src[:, :, 0:NE - s], ALU.add))
                src, s = dst, 2 * s
            steps.then(v.tensor_tensor(all_(first), all_(src), over(left[:, :]), ALU.is_le))
            steps.then(v.tensor_tensor(all_(first), all_(first), all_(equal), ALU.mult))
            steps.then(v.tensor_tensor(all_(chosen), all_(first), all_(above), ALU.add))
            steps.then(v.tensor_reduce(norm[:, :], all_(logits), AX, ALU.max))
            v.tensor_tensor(all_(shifted), all_(logits), over(norm[:, :]), ALU.subtract).then_inc(shift_ready, 1)
            dve.wait_ge(exp_ready, 1)
            steps.then(v.tensor_reduce(norm[:, :], all_(expd), AX, ALU.add))
            steps.then(v.reciprocal(inv[:, :], norm[:, :]))
            steps.then(v.tensor_tensor(all_(soft), all_(expd), over(inv[:, :]), ALU.mult))
            steps.then(v.tensor_tensor(all_(soft), all_(soft), all_(chosen), ALU.mult))
            steps.then(v.tensor_reduce(norm[:, :], all_(soft), AX, ALU.add))
            steps.then(v.reciprocal(inv[:, :], norm[:, :]))
            steps.then(v.tensor_tensor(all_(weight), all_(soft), over(inv[:, :]), ALU.mult))
            pairs = all_(weight).rearrange("p n (c two) -> p n c two", two=2)
            steps.then(v.tensor_reduce(all_(small), pairs, AX, ALU.add))
            steps.then(v.tensor_scalar(all_(small), all_(small), SMALL_SCALE, None, ALU.mult))
            at = 0
            for part, w in ((weight, NE), (small, NC)):
                steps.then(v.tensor_copy(cw[:, :, at:at + w], all_(part)))
                steps.then(v.tensor_tensor(cw[:, :, at + w:at + 2 * w], all_(part), f32(cw[:, :, at:at + w]), ALU.subtract))
                at += 2 * w
            v.engine_nop().then_inc(cw_ready, 1)

        @block.tensor
        def _(pe):
            pe.wait_ge(g_loaded, 16)
            with pe.Fori(0, NT // 2) as it:
                for u in range(2):
                    pe.wait_ge(xn_ready, it * 2 + u + 1)
                    for c in range(DC):
                        last = nc.tensor.transpose(ps[:, u, c * P:(c + 1) * P], xn[:, u, c * P:(c + 1) * P], ident[:, :])
                    last.then_inc(xn_turned, 1)
                for u in range(2):
                    pe.wait_ge(x_hi, it * 2 + u + 1)
                    for c in range(DC):
                        last = nc.tensor.matmul(ps[:, 2 + u, 0:NE], x32[:, u, c, :], gate[:, c, :], start=c == 0, stop=c == DC - 1)
                    last.then_inc(l_mm, 1)
            pe.wait_ge(cw_ready, 1)
            for g in range(NG):
                for j in range(GT):
                    last = nc.tensor.transpose(ps[0:CWR, 4 + g, j * P:(j + 1) * P], f32(cw[:, g * GT + j, :]), ident[:, :])
                last.then_inc(cw_turned, 1)


def phase_mix(nc, t, X, ps, x_h, x_l, cwT):
    ctx = ExitStack()
    with ctx:
        sb = lambda n, s, d=F32: ctx.enter_context(nc.sbuf_tensor(n, s, d))
        sem = lambda n: ctx.enter_context(nc.semaphore(n))
        SHAPES = {"g": [P, DC, BW], "u": [P, DC, BW], "d": [P, SB, D], "s": [CWR, 1, BW]}
        raw = {n: sb(f"raw_{n}", s) for n, s in SHAPES.items()}
        hi = {n: sb(f"hi_{n}", [s[0], 2, *s[1:]], F32R) for n, s in SHAPES.items()}
        lo = {n: sb(f"lo_{n}", [s[0], 2, *s[1:]], F32R) for n, s in SHAPES.items() if n != "s"}
        ones = sb("ones", [P, 1])
        silu = sb("silu", [P, 2, GW])
        gated = sb("gated", [P, 2, GW])
        a = sb("act_raw", [P, 2, SB, GW])
        a_h, a_l = sb("act_h", [P, 2, SB, GW], F32R), sb("act_l", [P, 2, SB, GW], F32R)
        ones_ready, w_loaded, w_hi, w_split = sem("ones_ready"), sem("w_loaded"), sem("w_hi"), sem("w_split")
        g_mm, u_mm, silu_ready, gated_ready, a_ready, a_hi, a_split = (sem(n) for n in (
            "g_mm", "u_mm", "silu_ready", "gated_ready", "a_ready", "a_hi", "a_split"))
        y_mm, y_added = sem("y_mm"), sem("y_added")
        block = ctx.enter_context(nc.Block())
        A_READY_CREDIT = 2
        A_SPLIT_CREDIT = 2 * SB
        Y_MM_CREDIT = 2 * 2
        Y_ADDED_CREDIT = 2
        UNITS = NG

        def source(name, at):
            if name in ("g", "u"):
                return t["eW" + name][:, bass.ds(at * BW, BW)].rearrange("(c p) n -> p c n", p=P)
            if name == "d":
                return t["eWd"][bass.ds(at * BW, BW), :].rearrange("(s p) d -> p s d", p=P)
            return t["sel"][:, bass.ds(at * BW, BW)].rearrange("r (a n) -> r a n", a=1)

        @block.sync
        def _(sp):
            for n in SHAPES:
                sp.dma_start(raw[n][:, :, :], source(n, 0)).then_inc(w_loaded, 16)
            with sp.Fori(0, NBLK - 1) as k:
                sp.wait_ge(w_split, k + 1)
                for n in SHAPES:
                    sp.dma_start(raw[n][:, :, :], source(n, k + 1)).then_inc(w_loaded, 16)

        @block.gpsimd
        def _(pool):
            nc.gpsimd.memset(ones[:, :], 1.0).then_inc(ones_ready, 1)
            pool.wait_ge(ones_ready, 1)
            pool.sem_inc(a_ready, A_READY_CREDIT)
            pool.sem_inc(a_split, A_SPLIT_CREDIT)
            pool.sem_inc(y_mm, Y_MM_CREDIT)
            pool.sem_inc(y_added, Y_ADDED_CREDIT)

            def split_weights(k, slot):
                pool.wait_ge(w_loaded, (k + 1) * 16 * len(SHAPES))
                for n in SHAPES:
                    r = raw[n][:, :, :]
                    one = ones[0:r.shape[0], :].unsqueeze(2).broadcast_to(list(r.shape))
                    nc.gpsimd.tensor_tensor(hi[n][:, slot], r, one, ALU.mult).then_inc(w_hi, 1)
                pool.wait_ge(w_hi, (k + 1) * len(SHAPES))
                for n in lo:
                    last = nc.gpsimd.tensor_tensor(lo[n][:, slot], raw[n][:, :, :], f32(hi[n][:, slot]), ALU.subtract)
                last.then_inc(w_split, 1)

            def split_activations(k, ks):
                with pool.Fori(0, UNITS // 2) as gg:
                    for gu in range(2):
                        for s in range(SB):
                            pool.wait_ge(a_hi, (k * UNITS + gg * 2 + gu) * SB + s + 1)
                            nc.gpsimd.tensor_tensor(a_l[:, gu, s, :], a[:, gu, s, :], f32(a_h[:, gu, s, :]), ALU.subtract).then_inc(a_split, 1)

            split_weights(0, 0)
            with pool.Fori(0, NBLK // 2 - 1) as kk:
                for ks in range(2):
                    k = kk * 2 + ks
                    pool.wait_ge(y_mm, k * UNITS * 2 + Y_MM_CREDIT)
                    split_weights(k + 1, 1 - ks)
                    split_activations(k, ks)
            k = NBLK - 2
            pool.wait_ge(y_mm, k * UNITS * 2 + Y_MM_CREDIT)
            split_weights(k + 1, 1)
            split_activations(k, 0)
            split_activations(k + 1, 1)

        @block.scalar
        def _(act):
            with act.Fori(0, NBLK * UNITS // 2) as pair:
                for gu in range(2):
                    unit = pair * 2 + gu
                    for s in range(SB):
                        act.wait_ge(g_mm, unit * SB + s + 1)
                        act.activation(silu[:, s % 2, :], ps[:, s % 2, :], ACT.Silu).then_inc(silu_ready, 1)
                        act.wait_ge(a_ready, unit * SB + s + 1 + A_READY_CREDIT)
                        act.wait_ge(y_mm, unit * 2 + 2)
                        act.activation(a_h[:, gu, s, :], a[:, gu, s, :], ACT.Copy).then_inc(a_hi, 1)

        @block.vector
        def _(dve):
            with dve.Fori(0, NBLK // 2 * 2) as k:
                with dve.Fori(0, UNITS // 2) as gg:
                    for gu in range(2):
                        unit = k * UNITS + gg * 2 + gu
                        for s in range(SB):
                            n = unit * SB + s + 1
                            dve.wait_ge(silu_ready, n)
                            dve.wait_ge(u_mm, n)
                            nc.vector.tensor_tensor(gated[:, s % 2, :], silu[:, s % 2, :], ps[:, 2 + s % 2, :], ALU.mult).then_inc(gated_ready, 1)
                            dve.wait_ge(gated_ready, n)
                            dve.wait_ge(a_split, n)
                            nc.vector.tensor_tensor(a[:, gu, s, :], gated[:, s % 2, :], ps[:, 4 + s % 2, :], ALU.mult).then_inc(a_ready, 1)
                    for gu in range(2):
                        unit = k * UNITS + gg * 2 + gu
                        for half in range(2):
                            dve.wait_ge(y_mm, unit * 2 + half + 1 + Y_MM_CREDIT)
                            x = X[:, bass.ds((gg * 2 + gu) * GT + 2 * half, 2), :].rearrange("p n d -> p (n d)")
                            nc.vector.tensor_tensor(x, x, ps[:, 6 + half, :], ALU.add).then_inc(y_added, 1)

        @block.tensor
        def _(pe):
            x2 = (x_h, x_l)
            w2 = {n: (hi[n], lo[n]) for n in lo}
            with pe.Fori(0, NBLK // 2) as kk:
                for ks in range(2):
                    k = kk * 2 + ks
                    with pe.Fori(0, UNITS // 2) as gg:
                        pe.wait_ge(w_split, k + 1)
                        for gu in range(2):
                            cols = bass.ds((gg * 2 + gu) * GW, GW)
                            for s in range(SB):
                                n = (k * UNITS + gg * 2 + gu) * SB + s + 1
                                units = slice(s * P, (s + 1) * P)
                                pe.wait_ge(a_ready, n)
                                for name, bank, done in (("g", s % 2, g_mm), ("u", 2 + s % 2, None)):
                                    for m, (c, (i, j)) in enumerate((c, x) for c in range(DC) for x in THREE):
                                        last = nc.tensor.matmul(ps[:, bank, :], w2[name][i][:, ks, c, units], x2[j][:, c, cols],
                                                                start=m == 0, stop=m == 3 * DC - 1)
                                    if done is not None:
                                        last.then_inc(done, 1)
                                nc.tensor.matmul(ps[:, 4 + s % 2, :], hi["s"][:, ks, 0, units], cwT[:, cols], start=True, stop=True) \
                                    .then_inc(u_mm, 1)
                        for gu in range(2):
                            unit = k * UNITS + gg * 2 + gu
                            pe.wait_ge(a_split, unit * SB + SB + A_SPLIT_CREDIT)
                            for j in range(GT):
                                if j % 2 == 0:
                                    pe.wait_ge(y_added, unit * 2 + j // 2 + 1)
                                for m, (s, (x, y)) in enumerate((s, x) for s in range(SB) for x in THREE):
                                    last = nc.tensor.matmul(ps[:, 6 + j // 2, j % 2 * D:(j % 2 + 1) * D],
                                                            (a_h, a_l)[x][:, gu, s, j * P:(j + 1) * P], w2["d"][y][:, ks, s, :],
                                                            start=m == 0, stop=m == 3 * SB - 1)
                                if j % 2:
                                    last.then_inc(y_mm, 1)


def kernel(**inputs):
    import numpy as np
    import concourse.bacc as bacc
    from concourse.bass_utils import run_bass_kernel_spmd
    a = {k: np.asarray(v) for k, v in inputs.items()}
    wkvT = a["L0_xattn_wkv"].T
    up = lambda w: w.transpose(1, 0, 2).reshape(D, -1)
    arrays = {
        "x": a["x"].reshape(T, D),
        "ctxT": a["ctx_2048"].transpose(0, 2, 1),
        "clast": a["ctx_2048"][:, NK - 1, :].T,
        "xwq": a["L0_xattn_wq"], "xwp": a["L0_xattn_wp"], "wkvT": wkvT, "wvT": wkvT[:, D:],
        "xbq": a["L0_xattn_bq"], "xbk": a["L0_xattn_bkv"][:D].reshape(DC, P).T, "xbv": a["L0_xattn_bkv"][D:],
        "xbp": a["L0_xattn_bp"],
        "sWq": a["L0_attn_Wq"], "sWk": a["L0_attn_Wk"], "sWv": a["L0_attn_Wv"], "sWo": a["L0_attn_Wo"],
        "sbq": a["L0_attn_bq"].reshape(SH, SD).T, "sbk": a["L0_attn_bk"].reshape(KV, SD).T, "sbv": a["L0_attn_bv"],
        "sbo": a["L0_attn_bo"],
        "gateT": a["L0_ffn_gate_w"].T,
        "eWg": np.concatenate([up(a["L0_ffn_Wg"]), up(a["L0_ffn_cWg"])], axis=1),
        "eWu": np.concatenate([up(a["L0_ffn_Wu"]), up(a["L0_ffn_cWu"])], axis=1),
        "eWd": np.concatenate([a["L0_ffn_Wd"].reshape(-1, D), a["L0_ffn_cWd"].reshape(-1, D)]),
    }
    arrays = {f"in_{k}": np.ascontiguousarray(v) for k, v in arrays.items()}
    sel = np.zeros((CWR, INTER), np.float32)
    sel[:2 * NE, :NE * EI] = np.tile(np.repeat(np.eye(NE), EI, axis=1), (2, 1))
    sel[2 * NE:, NE * EI:] = np.tile(np.repeat(np.eye(NC), CI, axis=1), (2, 1))
    arrays["in_sel"] = sel
    nc = bacc.Bacc("TRN2", target_bir_lowering=False, num_devices=1)
    t = {k[3:]: nc.dram_tensor(k, v.shape, mybir.dt.from_np(v.dtype), kind="ExternalInput").ap() for k, v in arrays.items()}
    out = nc.dram_tensor("out", (T, D), F32, kind="ExternalOutput").ap()
    program(nc, t, out)
    got = run_bass_kernel_spmd(nc, [arrays], core_ids=[0])
    return got.results[0]["out"].reshape(NB, NQ, D)
```

```python
import concourse.bass as bass
from concourse import mybir
from contextlib import ExitStack

F32 = mybir.dt.float32
F32R = mybir.dt.float32r
ALU = mybir.AluOpType
ACT = mybir.ActivationFunctionType
AX = mybir.AxisListType.X

P = 128
D = 256
DC = D // P
NB, NQ, NK = 64, 32, 257
T = NB * NQ
NT = T // P
BT = P // NQ
XH, XD = 16, 16
RB = XH // 4
RW = D // RB
KP = NK + 1
SH, SD, KV = 16, 128, 4
SG = SH // KV
GT = 4
GW = GT * P
NG = NT // GT
NE, EI = 32, 96
NC, CI = 16, 128
INTER = NE * EI + NC * CI
SB = 4
BW = SB * P
NBLK = INTER // BW
CWR = 2 * NE + 2 * NC
EPS = 1e-5
ROUND = 12582912.0
QMAX = 127.0
SMALL_SCALE = 0.05
SATURATED = 16.6355


def f32(ap):
    return ap.bitcast(F32)


class Steps:

    def __init__(self, eng, sem):
        self.eng, self.sem, self.base, self.n = eng, sem, 0, 0

    def begin(self, i, per_round, before=0):
        self.base, self.n, self.per_round = i * per_round + before, 0, per_round

    def end(self):
        assert self.n == self.per_round, (self.n, self.per_round)

    def then(self, ins):
        self.n += 1
        ins.then_inc(self.sem, 1)
        self.eng.wait_ge(self.sem, self.base + self.n)


def program(nc, t, out):
    vlast_dram = nc.dram_tensor("vlast_scratch", (NB, RB, D), F32, kind="Internal").ap()
    ctx = ExitStack()
    with ctx:
        X = ctx.enter_context(nc.sbuf_tensor("resid", [P, NT, D], F32))
        otok = ctx.enter_context(nc.sbuf_tensor("otok", [P, NT, D], F32))
        wpT_h = ctx.enter_context(nc.sbuf_tensor("wpT_h", [P, DC, D], F32R))
        wpT_l = ctx.enter_context(nc.sbuf_tensor("wpT_l", [P, DC, D], F32R))
        ident = ctx.enter_context(nc.sbuf_tensor("ident", [P, P], F32))
        mv = ctx.enter_context(nc.sbuf_tensor("mv", [P, NT, 2], F32))
        rstd = ctx.enter_context(nc.sbuf_tensor("rstd", [P, NT], F32))
        ps = ctx.enter_context(nc.psum_tensor("ps", [P, 8, 512], F32))
        with ExitStack() as cross:
            qT = [cross.enter_context(nc.sbuf_tensor(f"qT_{x}", [P, DC, T], F32R)) for x in ("hi", "lo")]
            first = CrossFirst(nc, t, cross)
            phase_queries(nc, t, X, wpT_h, wpT_l, ident, mv, rstd, ps, qT, vlast_dram, first)
            phase_cross(nc, t, X, otok, ps, qT, ident, vlast_dram, first)
        phase_self(nc, t, X, otok, wpT_h, wpT_l, ident, mv, rstd, ps)
        phase_experts(nc, t, X, ident, mv, rstd, ps)
        phase_store(nc, X, out)


def phase_store(nc, X, out):
    with nc.semaphore("stored") as stored, nc.Block() as block:
        @block.sync
        def _(sp):
            sp.dma_start(out.rearrange("(n p) d -> p n d", p=P), X[:, :, :]).then_inc(stored, 16)
            sp.wait_ge(stored, 16)


def row_scales(nc, steps, src, amax, s, rs):
    steps.then(nc.vector.tensor_reduce(amax, src, AX, ALU.max, apply_absolute_value=True))
    steps.then(nc.vector.tensor_scalar(s, amax, 1.0 / QMAX, 1e-8, ALU.mult, ALU.max))
    return nc.vector.reciprocal(rs, s)


def clip_shifted(nc, dst, src):
    return nc.vector.tensor_scalar(dst, src, ROUND + QMAX, ROUND - QMAX, ALU.min, ALU.max)


def group_stats(nc, steps, X, stats, mv, g):
    for j in range(GT):
        last = nc.vector.bn_stats(stats[:, j, :], X[:, g * GT + j, :])
    steps.then(last)
    for j in range(GT):
        last = nc.vector.bn_aggr(mv[:, g * GT + j, :], stats[:, j, :])
    steps.then(last)


def normalise(nc, X, mv, rstd, xn, g):
    for j in range(GT):
        n = g * GT + j
        last = nc.vector.tensor_scalar(xn[:, j, :], X[:, n, :], mv[:, n, 0:1], rstd[:, n:n + 1], ALU.subtract, ALU.mult)
    return last


def turn_group(nc, ps, bank, src, ident):
    for c in range(DC):
        for j in range(GT):
            last = nc.tensor.transpose(ps[:, bank + c, j * P:(j + 1) * P], src[:, j, c * P:(c + 1) * P], ident[:, :])
    return last


def project_ints(nc, ps, bank, intsT, w2):
    for j in range(GT):
        for n, (c, w) in enumerate((c, w) for c in range(DC) for w in w2):
            last = nc.tensor.matmul(ps[:, bank + j // 2, j % 2 * D:(j % 2 + 1) * D], intsT[:, c, j * P:(j + 1) * P], w[:, c, :],
                                    start=n == 0, stop=n == 2 * DC - 1)
    return last


class CrossFirst:

    def __init__(self, nc, t, ctx):
        sb = lambda n, s, d=F32: ctx.enter_context(nc.sbuf_tensor(n, s, d))
        sem = lambda n: ctx.enter_context(nc.semaphore(n))
        self.nc, self.t = nc, t
        self.wraw = sb("wkv_raw", [P, DC, 2 * D])
        self.wkv_h = sb("wkv_h", [P, DC, 2 * D], F32R)
        self.wkv_l = sb("wkv_l", [P, DC, 2 * D], F32R)
        self.craw = sb("craw", [P, BT, DC, NK])
        self.mask = sb("mask", [P, 8, NQ])
        self.ones = sb("ones_cross", [P, 1])
        self.w_loaded, self.w_hi, self.w_split = sem("wkv_loaded"), sem("wkv_hi"), sem("wkv_split")
        self.ctx_loaded = [sem(f"ctx_loaded{b}") for b in range(BT)]
        self.mask_step, self.ones_ready = sem("mask_step"), sem("ones_ready")

    def load(self, sp):
        sp.dma_start(self.wraw[:, :, :], self.t["wkvT"].rearrange("(c p) o -> p c o", p=P)).then_inc(self.w_loaded, 16)
        for b in range(BT):
            sp.dma_start(self.craw[:, b], self.t["ctxT"][b].rearrange("(c p) k -> p c k", p=P)).then_inc(self.ctx_loaded[b], 16)

    def prepare(self, pool):
        nc, mask, hi = self.nc, self.mask[:, :, :], self.wkv_h[:, :, :]
        nc.gpsimd.memset(self.ones[:, :], 1.0).then_inc(self.ones_ready, 1)
        nc.gpsimd.memset(mask, 1.0).then_inc(self.mask_step, 1)
        pool.wait_ge(self.mask_step, 1)
        nc.gpsimd.affine_select(out=mask, in_=mask, compare_op=ALU.is_ge, fill=0.0, base=0,
                                pattern=[[-XD, 8], [0, NQ]], channel_multiplier=1).then_inc(self.mask_step, 1)
        pool.wait_ge(self.mask_step, 2)
        nc.gpsimd.affine_select(out=mask, in_=mask, compare_op=ALU.is_ge, fill=0.0, base=XD - 1,
                                pattern=[[XD, 8], [0, NQ]], channel_multiplier=-1).then_inc(self.mask_step, 1)
        pool.wait_ge(self.ones_ready, 1)
        pool.wait_ge(self.w_loaded, 16)
        nc.gpsimd.tensor_tensor(hi, self.wraw[:, :, :], self.ones[:, :].unsqueeze(2).broadcast_to([P, DC, 2 * D]),
                                ALU.mult).then_inc(self.w_hi, 1)
        pool.wait_ge(self.w_hi, 1)
        nc.gpsimd.tensor_tensor(self.wkv_l[:, :, :], self.wraw[:, :, :], f32(hi), ALU.subtract).then_inc(self.w_split, 1)


def phase_queries(nc, t, X, wpT_h, wpT_l, ident, mv, rstd, ps, qT, vlast_dram, first):
    ctx = ExitStack()
    with ctx:
        sb = lambda n, s, d=F32: ctx.enter_context(nc.sbuf_tensor(n, s, d))
        sem = lambda n: ctx.enter_context(nc.semaphore(n))
        wraw = sb("wraw", [P, 2, DC, D])
        wamax = sb("wamax", [P, 2, DC])
        wscale = sb("wscale", [P, 2, DC])
        wrs = sb("wrs", [P, 2, DC])
        wtmp = sb("wtmp", [P, 2, DC, D])
        wtmp2 = sb("wtmp2", [P, 2, DC, D])
        wints = sb("wints", [P, 2, DC, D])
        wdeq = sb("wdeq", [P, 2, DC, D])
        wqT_h = sb("wqT_h", [P, DC, D], F32R)
        wqT_l = sb("wqT_l", [P, DC, D], F32R)
        bq_b = sb("bq_b", [P, D])
        bv_b = sb("bv_b", [P, D])
        clast = sb("clast", [P, DC, NB])
        wv32 = sb("wv32", [P, DC, D])
        vlast = sb("vlast", [NB, RB, D])
        shift = sb("shift", [P, 2])
        stats = sb("stats", [P, GT, 6])
        std = sb("std", [P, NT])
        xn = sb("xn", [P, GT, D])
        amax = sb("amax", [P, NT])
        sx = sb("sx", [P, NT])
        rs = sb("rs", [P, NT])
        rounded = sb("rounded", [P, GT, D])
        ints = sb("ints", [P, GT, D])
        intsT = sb("intsT", [P, DC, GW], F32R)
        q = sb("q", [P, GT, D])
        x_loaded = [sem(f"x_loaded{g}") for g in range(NG)]
        shift_ready = sem("shift_ready")
        w_loaded = [sem("wq_loaded"), sem("wp_loaded")]
        v_loaded, b_loaded = sem("v_loaded"), sem("b_loaded")
        ident_zero, ident_ready = sem("ident_zero"), sem("ident_ready")
        dve_step = sem("dve_step")
        w_deq, w_turned, w_hi, w_split = sem("w_deq"), sem("w_turned"), sem("w_hi"), sem("w_split")
        var_ready, std_ready = sem("var_ready"), sem("std_ready")
        xn_ready, scales_ready, rounded_ready = sem("xn_ready"), sem("scales_ready"), sem("rounded_ready")
        ints_ready, ints_turned, ints_copied = sem("ints_ready"), sem("ints_turned"), sem("ints_copied")
        q_mm, q_ready, q_turned, q_copied, q_split = (sem(n) for n in (
            "q_mm", "q_ready", "q_turned", "q_copied", "q_split"))
        vlast_mm, vlast_ready, vlast_stored = sem("vlast_mm"), sem("vlast_ready"), sem("vlast_stored")
        block = ctx.enter_context(nc.Block())

        @block.sync
        def _(sp):
            sp.dma_start(wraw[:, 0], t["xwq"].rearrange("(c p) i -> p c i", p=P)).then_inc(w_loaded[0], 16)
            for g in range(NG):
                sp.dma_start(X[:, g * GT:(g + 1) * GT, :],
                             t["x"][g * GW:(g + 1) * GW, :].rearrange("(n p) d -> p n d", p=P)).then_inc(x_loaded[g], 16)
                if g == 0:
                    sp.dma_start(wraw[:, 1], t["xwp"].rearrange("(c p) i -> p c i", p=P)).then_inc(w_loaded[1], 16)
            first.load(sp)
            sp.wait_ge(vlast_ready, 1)
            sp.dma_start(vlast_dram, vlast[:, :, :]).then_inc(vlast_stored, 16)
            sp.wait_ge(vlast_stored, 16)

        @block.gpsimd
        def _(pool):
            nc.gpsimd.memset(ident[:, :], 0.0).then_inc(ident_zero, 1)
            nc.gpsimd.memset(shift[:, 0:1], ROUND)
            nc.gpsimd.memset(shift[:, 1:2], -ROUND).then_inc(shift_ready, 1)
            pool.wait_ge(ident_zero, 1)
            nc.gpsimd.affine_select(out=ident[:, :], in_=ident[:, :], compare_op=ALU.not_equal, fill=1.0, base=0,
                                    pattern=[[-1, P]], channel_multiplier=1).then_inc(ident_ready, 1)
            first.prepare(pool)

        @block.scalar
        def _(act):
            act.dma_start(bq_b[:, :], t["xbq"].partition_broadcast(P)).then_inc(b_loaded, 16)
            act.dma_start(bv_b[:, :], t["xbv"].partition_broadcast(P)).then_inc(b_loaded, 16)
            act.dma_start(clast[:, :, :], t["clast"].rearrange("(c p) b -> p c b", p=P)).then_inc(v_loaded, 16)
            act.dma_start(wv32[:, :, :], t["wvT"].rearrange("(c p) o -> p c o", p=P)).then_inc(v_loaded, 16)
            def weight_hi(w):
                act.wait_ge(w_turned, w + 1)
                act.activation((wqT_h, wpT_h)[w][:, :, :], ps[:, 6, :].rearrange("p (c o) -> p c o", c=DC), ACT.Copy).then_inc(w_hi, 1)

            def deviations(g):
                tiles = slice(g * GT, (g + 1) * GT)
                act.wait_ge(var_ready, g + 1)
                act.activation(std[:, tiles], rstd[:, tiles], ACT.Sqrt).then_inc(std_ready, 1)

            def queries_hi(g):
                act.wait_ge(q_turned, g + 1)
                act.activation(qT[0][:, :, g * GW:(g + 1) * GW], ps[:, 4:6, :], ACT.Copy, scale=float(XD) ** -0.5).then_inc(q_copied, 1)

            def round_ints(g):
                act.wait_ge(scales_ready, g + 1)
                for j in range(GT):
                    n = g * GT + j
                    last = act.activation(rounded[:, j, :], xn[:, j, :], ACT.Identity, bias=shift[:, 0:1], scale=rs[:, n:n + 1])
                last.then_inc(rounded_ready, 1)

            act.wait_ge(shift_ready, 1)
            deviations(0)
            weight_hi(0)
            round_ints(0)
            deviations(1)
            for g in range(NG):
                act.wait_ge(ints_turned, g + 1)
                act.activation(intsT[:, :, :], ps[:, 0:2, :], ACT.Identity, bias=shift[:, 1:2]).then_inc(ints_copied, 1)
                if g + 1 < NG:
                    round_ints(g + 1)
                if g + 2 < NG:
                    deviations(g + 2)
                queries_hi(g)
                if g == 1:
                    weight_hi(1)

        @block.vector
        def _(dve):
            steps = Steps(dve, dve_step)
            def weight(w):
                amax, scale, rscale = wamax[:, w, :], wscale[:, w, :], wrs[:, w, :]
                rows = lambda a: a.unsqueeze(2).broadcast_to([P, DC, D])
                dve.wait_ge(w_loaded[w], 16)
                steps.then(nc.vector.tensor_reduce(amax, wraw[:, w], AX, ALU.max, apply_absolute_value=True))
                steps.then(nc.vector.tensor_scalar(scale, amax, 1.0 / QMAX, 1e-8, ALU.mult, ALU.max))
                steps.then(nc.vector.reciprocal(rscale, scale))
                steps.then(nc.vector.tensor_tensor(wtmp[:, w], wraw[:, w], rows(rscale), ALU.mult))
                steps.then(nc.vector.tensor_scalar(wtmp2[:, w], wtmp[:, w], ROUND, ROUND, ALU.add, ALU.subtract))
                steps.then(nc.vector.tensor_scalar(wints[:, w], wtmp2[:, w], QMAX, -QMAX, ALU.min, ALU.max))
                nc.vector.tensor_tensor(wdeq[:, w], wints[:, w], rows(scale), ALU.mult).then_inc(w_deq, 1)

            def weight_lo(w):
                dve.wait_ge(w_hi, w + 1)
                lo, hi = ((wqT_l, wqT_h), (wpT_l, wpT_h))[w]
                nc.vector.tensor_tensor(lo[:, :, :], ps[:, 6, :].rearrange("p (c o) -> p c o", c=DC), f32(hi[:, :, :]),
                                        ALU.subtract).then_inc(w_split, 1)

            def last_values():
                dve.wait_ge(vlast_mm, 1)
                steps.then(nc.vector.memset(vlast[:, :, :], 0.0))
                for b in range(RB):
                    cols = slice(b * RW, (b + 1) * RW)
                    last = nc.vector.tensor_tensor(vlast[:, b, cols], ps[0:NB, 7, cols], bv_b[0:NB, cols], ALU.add)
                last.then_inc(vlast_ready, 1)

            def statistics(g):
                dve.wait_ge(x_loaded[g], 16)
                group_stats(nc, steps, X, stats, mv, g)
                tiles = slice(g * GT, (g + 1) * GT)
                nc.vector.tensor_scalar(rstd[:, tiles], mv[:, tiles, 1], EPS, None, ALU.add).then_inc(var_ready, 1)

            def scales(g):
                tiles = slice(g * GT, (g + 1) * GT)
                dve.wait_ge(std_ready, g + 1)
                steps.then(nc.vector.reciprocal(rstd[:, tiles], std[:, tiles]))
                steps.then(normalise(nc, X, mv, rstd, xn, g))
                row_scales(nc, steps, xn[:, :, :], amax[:, tiles], sx[:, tiles], rs[:, tiles]).then_inc(scales_ready, 1)

            def clip(g):
                dve.wait_ge(rounded_ready, g + 1)
                clip_shifted(nc, ints[:, :, :], rounded[:, :, :]).then_inc(ints_ready, 1)

            weight(0)
            statistics(0)
            scales(0)
            weight_lo(0)
            statistics(1)
            clip(0)
            dve.wait_ge(b_loaded, 32)
            for g in range(NG):
                if g + 1 < NG:
                    scales(g + 1)
                dve.wait_ge(q_mm, g + 1)
                for j in range(GT):
                    last = nc.vector.scalar_tensor_tensor(out=q[:, j, :], in0=ps[:, 2 + j // 2, j % 2 * D:(j % 2 + 1) * D],
                                                          scalar=sx[:, g * GT + j:g * GT + j + 1], in1=bq_b[:, :], op0=ALU.mult, op1=ALU.add)
                last.then_inc(q_ready, 1)
                if g + 2 < NG:
                    statistics(g + 2)
                dve.wait_ge(q_copied, g + 1)
                cols = slice(g * GW, (g + 1) * GW)
                nc.vector.scalar_tensor_tensor(out=qT[1][:, :, cols], in0=ps[:, 4:6, :], scalar=float(XD) ** -0.5,
                                               in1=f32(qT[0][:, :, cols]), op0=ALU.mult, op1=ALU.subtract).then_inc(q_split, 1)
                if g + 1 < NG:
                    clip(g + 1)
                if g == 0:
                    weight(1)
                if g == 1:
                    last_values()
                if g == 2:
                    weight_lo(1)

        @block.tensor
        def _(pe):
            pe.wait_ge(ident_ready, 1)

            def turn_weight(w):
                pe.wait_ge(w_deq, w + 1)
                for c in range(DC):
                    for o in range(DC):
                        last = nc.tensor.transpose(ps[:, 6, c * D + o * P:c * D + (o + 1) * P], wdeq[:, w, o, c * P:(c + 1) * P], ident[:, :])
                last.then_inc(w_turned, 1)

            def turn_ints(g):
                pe.wait_ge(ints_ready, g + 1)
                turn_group(nc, ps, 0, ints, ident).then_inc(ints_turned, 1)

            turn_weight(0)
            pe.wait_ge(v_loaded, 32)
            for c in range(DC):
                last = nc.tensor.matmul(ps[0:NB, 7, 0:D], clast[:, c, :], wv32[:, c, :], start=c == 0, stop=c == DC - 1)
            last.then_inc(vlast_mm, 1)
            turn_ints(0)
            pe.wait_ge(w_split, 1)
            for g in range(NG):
                pe.wait_ge(ints_copied, g + 1)
                project_ints(nc, ps, 2, intsT, (wqT_h, wqT_l)).then_inc(q_mm, 1)
                pe.wait_ge(q_ready, g + 1)
                if g:
                    pe.wait_ge(q_split, g)
                turn_group(nc, ps, 4, q, ident).then_inc(q_turned, 1)
                if g + 1 < NG:
                    turn_ints(g + 1)
                if g == 0:
                    turn_weight(1)


THREE = ((0, 0), (0, 1), (1, 0))


def phase_cross(nc, t, X, otok, ps, qT, ident, vlast_dram, first):
    LASTP = slice(D, D + P)
    ctx = ExitStack()
    with ctx:
        sb = lambda n, s, d=F32: ctx.enter_context(nc.sbuf_tensor(n, s, d))
        sem = lambda n: ctx.enter_context(nc.semaphore(n))
        wkv_h, wkv_l, craw, mask, ctx_loaded = first.wkv_h, first.wkv_l, first.craw, first.mask, first.ctx_loaded
        bk = sb("bk", [P, DC])
        bv_b = sb("bv_bc", [P, D])
        bp_b = sb("bp_b", [P, D])
        ch = sb("ch", [P, 2, DC, KP], F32R)
        cl = sb("cl", [P, 2, DC, KP], F32R)
        kh = sb("kh", [P, 2, DC, KP], F32R)
        kl = sb("kl", [P, 2, DC, KP], F32R)
        qh = sb("qh", [P, 2, DC, 8, NQ], F32R)
        ql = sb("ql", [P, 2, DC, 8, NQ], F32R)
        v = sb("v", [P, 2, 2, D])
        vl = sb("vl", [RB, BT, D])
        probs = sb("probs", [P, RB, KP])
        nmax = sb("nmax", [P, 2, RB])
        rsum = sb("rsum", [P, 2, RB])
        rinv = sb("rinv", [P, 2, RB])
        pT = sb("pT", [P, 2, 512])
        pT_last = sb("pT_last", [RB, P])
        bp_loaded, bp_added = sem("bp_loaded"), sem("bp_added")
        b_loaded = sem("b_loaded")
        vl_loaded = [sem(f"vl_loaded{b}") for b in range(BT)]
        pad_ready = sem("pad_ready")
        ctx_hi, ctx_split = sem("ctx_hi"), sem("ctx_split")
        k_mm, k_hi, k_split, q_masked = sem("k_mm"), sem("k_hi"), sem("k_split"), sem("q_masked")
        s_mm, nmax_ready, exp_done = sem("s_mm"), sem("nmax_ready"), sem("exp_done")
        v_mm, v_ready = sem("v_mm"), sem("v_ready")
        p_turned, pT_dve, pT_act = sem("p_turned"), sem("pT_dve"), sem("pT_act")
        rinv_ready, o_mm, o_ready = sem("rinv_ready"), sem("o_mm"), sem("o_ready")
        block = ctx.enter_context(nc.Block())

        O_CREDIT = 1

        def rounds(eng, one):
            with eng.Fori(0, NT - 1) as it:
                for b in range(BT):
                    one(it, b, 2)
            for b in range(BT):
                one(NT - 1, b, min(2, BT - 1 - b))

        @block.sync
        def _(sp):
            sp.dma_start(bk[:, :], t["xbk"]).then_inc(b_loaded, 16)
            sp.dma_start(bv_b[:, :], t["xbv"].partition_broadcast(P)).then_inc(b_loaded, 16)
            sp.dma_start(bp_b[:, :], t["xbp"].partition_broadcast(P)).then_inc(bp_loaded, 16)
            for b in range(BT):
                sp.dma_start(vl[:, b, :], vlast_dram[b]).then_inc(vl_loaded[b], 16)
            with sp.Fori(0, NT - 1) as it:
                for b in range(BT):
                    sp.wait_ge(ctx_split, it * BT + b + 1)
                    sp.dma_start(craw[:, b], t["ctxT"][bass.ds(it * BT + BT + b, 1)].rearrange("a (c p) k -> p (a c) k", p=P)) \
                        .then_inc(ctx_loaded[b], 16)
                    sp.wait_ge(o_mm, it * BT + b + 1)
                    sp.dma_start(vl[:, b, :], vlast_dram[bass.ds(it * BT + BT + b, 1)].rearrange("a r d -> r (a d)")).then_inc(vl_loaded[b], 16)

        @block.gpsimd
        def _(pool):
            for s in (ch, cl):
                nc.gpsimd.memset(f32(s[:, :, :, NK:KP]), 0.0).then_inc(pad_ready, 1)
            pool.sem_inc(o_ready, O_CREDIT)

            def prepare(n, slot):
                u = slot % 2
                pool.wait_ge(ctx_hi, n + 1)
                nc.gpsimd.tensor_tensor(cl[:, u, :, 0:NK], craw[:, slot], f32(ch[:, u, :, 0:NK]), ALU.subtract).then_inc(ctx_split, 1)
                for dst, src in ((qh, qT[0]), (ql, qT[1])):
                    for c in range(DC):
                        last = nc.gpsimd.tensor_tensor(dst[:, u, c], f32(src[:, c, bass.ds(n * NQ, NQ)]).unsqueeze(1).broadcast_to([P, 8, NQ]),
                                                       mask[:, :, :], ALU.mult)
                last.then_inc(q_masked, 1)

            def one(it, b, more):
                if more == 2:
                    pool.wait_ge(s_mm, (it * BT + b + 1) * RB)
                    prepare(it * BT + b + 2, (b + 2) % BT)

            prepare(0, 0)
            prepare(1, 1)
            rounds(pool, one)
            pool.wait_ge(bp_loaded, 16)
            for g in range(NG):
                x = X[:, g * GT:(g + 1) * GT, :]
                nc.gpsimd.tensor_tensor(x, x, bp_b[:, :].unsqueeze(1).broadcast_to([P, GT, D]), ALU.add).then_inc(bp_added, 1)

        @block.scalar
        def _(act):
            act.wait_ge(b_loaded, 32)

            def context_hi(n, slot, loads):
                act.wait_ge(ctx_loaded[slot], loads * 16)
                act.activation(ch[:, slot % 2, :, 0:NK], craw[:, slot], ACT.Copy).then_inc(ctx_hi, 1)

            def keys_hi(n, u):
                for c in range(DC):
                    act.wait_ge(k_mm, n * DC + c + 1)
                    act.activation(kh[:, u, c, :], ps[:, 4 + c, 0:KP], ACT.Identity, bias=bk[:, c:c + 1]).then_inc(k_hi, 1)

            def exps(n, u):
                for r in range(RB):
                    act.wait_ge(nmax_ready, n * 2 + r // 2 + 1)
                    act.activation(probs[:, r, 0:NK], ps[:, r, 0:NK], ACT.Exp, bias=nmax[:, u, r:r + 1],
                                   accum_out=rsum[:, u, r:r + 1]).then_inc(exp_done, 1)

            def one(it, b, more):
                n = it * BT + b
                if more >= 2:
                    act.wait_ge(v_mm, n + 1)
                    context_hi(n + 2, (b + 2) % BT, it + 1 + (b + 2) // BT)
                if more >= 1:
                    keys_hi(n + 1, (b + 1) % 2)
                act.wait_ge(p_turned, n * 3 + 2)
                act.activation(pT[:, 1, :], ps[:, 5, :], ACT.Copy).then_inc(pT_act, 1)
                act.wait_ge(p_turned, n * 3 + 3)
                act.activation(pT_last[:, :], ps[0:RB, 7, LASTP], ACT.Copy).then_inc(pT_act, 1)
                if more >= 1:
                    exps(n + 1, (b + 1) % 2)

            context_hi(0, 0, 1)
            context_hi(1, 1, 1)
            keys_hi(0, 0)
            exps(0, 0)
            rounds(act, one)

        @block.vector
        def _(dve):
            dve.wait_ge(b_loaded, 32)

            def keys_lo(n, u):
                for c in range(DC):
                    dve.wait_ge(k_hi, n * DC + c + 1)
                    nc.vector.scalar_tensor_tensor(out=kl[:, u, c, :], in0=ps[:, 4 + c, 0:KP], scalar=bk[:, c:c + 1],
                                                   in1=f32(kh[:, u, c, :]), op0=ALU.add, op1=ALU.subtract).then_inc(k_split, 1)

            def values(n, u):
                dve.wait_ge(v_mm, n + 1)
                nc.vector.tensor_tensor(v[:, u], ps[:, 6, :].rearrange("p (k d) -> p k d", k=2),
                                        bv_b[:, :].unsqueeze(1).broadcast_to([P, 2, D]), ALU.add).then_inc(v_ready, 1)

            def maxima(n, u):
                for half in range(2):
                    dve.wait_ge(s_mm, n * RB + 2 * half + 2)
                    nc.vector.tensor_reduce(nmax[:, u, 2 * half:2 * half + 2], ps[:, 2 * half:2 * half + 2, 0:NK], AX, ALU.max,
                                            negate=True).then_inc(nmax_ready, 1)

            def one(it, b, more):
                n, u = it * BT + b, b % 2
                if more >= 1:
                    keys_lo(n + 1, 1 - u)
                    values(n + 1, 1 - u)
                dve.wait_ge(exp_done, (n + 1) * RB)
                nc.vector.reciprocal(rinv[:, u, :], rsum[:, u, :]).then_inc(rinv_ready, 1)
                dve.wait_ge(p_turned, n * 3 + 1)
                nc.vector.tensor_copy(pT[:, 0, :], ps[:, 4, :]).then_inc(pT_dve, 1)
                if more >= 1:
                    maxima(n + 1, 1 - u)
                dve.wait_ge(rinv_ready, n + 1)
                dve.wait_ge(o_mm, n + 1)
                for h in range(4):
                    rows = slice(h * NQ, (h + 1) * NQ)
                    dst = otok[b * NQ:(b + 1) * NQ, bass.ds(it, 1), :].rearrange("p n (r h d) -> p (n r) h d", r=RB, h=4)[:, :, h, :]
                    src = ps[rows, 7, 0:D].rearrange("p (r h d) -> p r h d", r=RB, h=4)[:, :, h, :]
                    last = nc.vector.tensor_tensor(dst, src, rinv[rows, u, :].unsqueeze(2).broadcast_to([NQ, RB, XD]), ALU.mult)
                last.then_inc(o_ready, 1)

            keys_lo(0, 0)
            values(0, 0)
            maxima(0, 0)
            rounds(dve, one)

        @block.tensor
        def _(pe):
            pe.wait_ge(first.w_split, 1)
            pe.wait_ge(pad_ready, 2)
            w2, c2, k2, q2 = (wkv_h, wkv_l), (ch, cl), (kh, kl), (qh, ql)

            def keys(n, u):
                pe.wait_ge(ctx_split, n + 1)
                for o in range(DC):
                    for m, (c, (i, j)) in enumerate((c, x) for c in range(DC) for x in THREE):
                        last = nc.tensor.matmul(ps[:, 4 + o, 0:KP], w2[i][:, c, o * P:(o + 1) * P], c2[j][:, u, c, :],
                                                start=m == 0, stop=m == 3 * DC - 1)
                    last.then_inc(k_mm, 1)

            def values(n, u):
                for kb in range(2):
                    for m, (c, (i, j)) in enumerate((c, x) for c in range(DC) for x in THREE):
                        last = nc.tensor.matmul(ps[:, 6, kb * D:(kb + 1) * D], c2[i][:, u, c, kb * P:(kb + 1) * P],
                                                w2[j][:, c, D:2 * D], start=m == 0, stop=m == 3 * DC - 1)
                last.then_inc(v_mm, 1)

            def scores(n, u):
                pe.wait_ge(k_split, (n + 1) * DC)
                pe.wait_ge(q_masked, n + 1)
                for r in range(RB):
                    rows = slice(r % 2 * 4, r % 2 * 4 + 4)
                    for m, (i, j) in enumerate(THREE):
                        last = nc.tensor.matmul(ps[:, r, 0:KP], q2[i][:, u, r // 2, rows, :].rearrange("p h n -> p (h n)"),
                                                k2[j][:, u, r // 2, :], start=m == 0, stop=m == 2)
                    last.then_inc(s_mm, 1)

            def one(it, b, more):
                n, u = it * BT + b, b % 2
                if more >= 1:
                    keys(n + 1, 1 - u)
                    pe.wait_ge(v_ready, n + 1)
                    values(n + 1, 1 - u)
                pe.wait_ge(exp_done, (n + 1) * RB)
                for kb in range(2):
                    if more >= 1:
                        pe.wait_ge(k_split, (n + 1) * DC + kb + 1)
                    for r in range(RB):
                        last = nc.tensor.transpose(ps[:, 4 + kb, r * P:(r + 1) * P], probs[:, r, kb * P:(kb + 1) * P], ident[:, :])
                    last.then_inc(p_turned, 1)
                pe.wait_ge(o_ready, n + O_CREDIT)
                nc.tensor.transpose(ps[0:RB, 7, LASTP], probs[:, :, NK - 1], ident[:, :]).then_inc(p_turned, 1)
                if more >= 1:
                    scores(n + 1, 1 - u)
                else:
                    pe.wait_ge(v_ready, n + 1)
                pe.wait_ge(vl_loaded[b], it * 16 + 16)
                pe.wait_ge(pT_act, 2 * n + 2)
                nc.tensor.matmul(ps[:, 7, 0:D], pT_last[:, :], vl[:, b, :], start=True, stop=False)
                pe.wait_ge(pT_dve, n + 1)
                for r in range(RB):
                    cols = slice(r * RW, (r + 1) * RW)
                    for kb in range(2):
                        last = nc.tensor.matmul(ps[:, 7, cols], pT[:, kb, r * P:(r + 1) * P], v[:, u, kb, cols],
                                                start=False, stop=r == RB - 1 and kb == 1)
                last.then_inc(o_mm, 1)

            keys(0, 0)
            values(0, 0)
            scores(0, 0)
            rounds(pe, one)


def phase_project(nc, t, X, otok, wpT_h, wpT_l, ident, mv, rstd, ps, xT, W):
    CH = 2048
    ctx = ExitStack()
    with ctx:
        sb = lambda n, s, d=F32: ctx.enter_context(nc.sbuf_tensor(n, s, d))
        sem = lambda n: ctx.enter_context(nc.semaphore(n))
        wraw = sb("self_wraw", [P, 2, CH])
        bo_b = sb("bo_b", [P, D])
        shift = sb("shift_p", [P, 2])
        stats = sb("stats_p", [P, GT, 6])
        std = sb("std_p", [P, NT])
        amax = sb("amax_p", [P, NT])
        so = sb("so_p", [P, NT])
        rs = sb("rs_p", [P, NT])
        rounded = sb("rounded_p", [P, GT, D])
        ints = sb("ints_p", [P, GT, D])
        intsT = sb("intsT_p", [P, DC, GW], F32R)
        xn = sb("xn_p", [P, GT, D])
        b_loaded, shift_ready = sem("b_loaded"), sem("shift_ready")
        w_loaded = [sem("w_loaded0"), sem("w_loaded1")]
        w_hi, w_split = sem("w_hi"), sem("w_split")
        dve_step = sem("dve_step")
        scales_ready, rounded_ready = sem("scales_ready"), sem("rounded_ready")
        ints_ready, ints_turned, ints_copied, y_mm = sem("ints_ready"), sem("ints_turned"), sem("ints_copied"), sem("y_mm")
        y_added, bias_added = sem("y_added"), sem("bias_added")
        var_ready, std_ready = sem("var_ready"), sem("std_ready")
        xn_ready, xn_turned, xn_copied = sem("xn_ready"), sem("xn_turned"), sem("xn_copied")
        block = ctx.enter_context(nc.Block())

        chunks = []
        for c in range(DC):
            chunks.append((t["sWq"][c * P:(c + 1) * P, :], [w[:, c, :] for w in W["q"]], SH * SD))
        for name in ("k", "v"):
            for c in range(DC):
                chunks.append((t["sW" + name][c * P:(c + 1) * P, :], [w[:, c, :] for w in W[name]], KV * SD))
        for c in range(2):
            h = SH // 2
            chunks.append((t["sWo"][c * h * SD:(c + 1) * h * SD, :].rearrange("(h p) o -> p h o", p=P),
                           [w[:, c * h:(c + 1) * h, :].rearrange("p h o -> p (h o)") for w in W["o"]], h * D))
        PER_GROUP = len(chunks) // NG

        @block.sync
        def _(sp):
            for n, (src, _, w) in enumerate(chunks):
                if n >= 2:
                    sp.wait_ge(w_split, n - 1)
                dst = wraw[:, n % 2, 0:w]
                if len(src.shape) == 3:
                    dst = dst.rearrange("p (h o) -> p h o", o=D)
                sp.dma_start(dst, src).then_inc(w_loaded[n % 2], 16)
                if n == 1:
                    sp.dma_start(bo_b[:, :], t["sbo"].partition_broadcast(P)).then_inc(b_loaded, 16)

        @block.gpsimd
        def _(pool):
            nc.gpsimd.memset(shift[:, 0:1], ROUND)
            nc.gpsimd.memset(shift[:, 1:2], -ROUND).then_inc(shift_ready, 1)
            for n, (_, (hi, lo), w) in enumerate(chunks):
                pool.wait_ge(w_hi, n + 1)
                nc.gpsimd.tensor_tensor(lo, wraw[:, n % 2, 0:w], f32(hi), ALU.subtract).then_inc(w_split, 1)
            pool.wait_ge(b_loaded, 16)
            for g in range(NG):
                x = X[:, g * GT:(g + 1) * GT, :]
                pool.wait_ge(xn_ready, g + 1)
                nc.gpsimd.tensor_tensor(x, x, bo_b[:, :].unsqueeze(1).broadcast_to([P, GT, D]), ALU.add).then_inc(bias_added, 1)

        @block.scalar
        def _(act):
            def round_ints(g):
                act.wait_ge(scales_ready, g + 1)
                for j in range(GT):
                    n = g * GT + j
                    last = act.activation(rounded[:, j, :], otok[:, n, :], ACT.Identity, bias=shift[:, 0:1], scale=rs[:, n:n + 1])
                last.then_inc(rounded_ready, 1)

            def weights_hi(n):
                _, (hi, _), w = chunks[n]
                act.wait_ge(w_loaded[n % 2], 16 * (n // 2 + 1))
                act.activation(hi, wraw[:, n % 2, 0:w], ACT.Copy).then_inc(w_hi, 1)

            act.wait_ge(shift_ready, 1)
            round_ints(0)
            for g in range(NG):
                act.wait_ge(ints_turned, g + 1)
                act.activation(intsT[:, :, :], ps[:, 0:2, :], ACT.Identity, bias=shift[:, 1:2]).then_inc(ints_copied, 1)
                if g + 1 < NG:
                    round_ints(g + 1)
                tiles = slice(g * GT, (g + 1) * GT)
                act.wait_ge(var_ready, g + 1)
                act.activation(std[:, tiles], rstd[:, tiles], ACT.Sqrt).then_inc(std_ready, 1)
                for n in range(g * PER_GROUP, (g + 1) * PER_GROUP):
                    weights_hi(n)
                act.wait_ge(xn_turned, g + 1)
                bank = 4 + g % 2 * 2
                act.activation(xT[:, :, g * GW:(g + 1) * GW], ps[:, bank:bank + 2, :], ACT.Copy).then_inc(xn_copied, 1)

        @block.vector
        def _(dve):
            steps = Steps(dve, dve_step)

            def scales(g):
                tiles = slice(g * GT, (g + 1) * GT)
                row_scales(nc, steps, otok[:, tiles, :], amax[:, tiles], so[:, tiles], rs[:, tiles]).then_inc(scales_ready, 1)

            def clip(g):
                dve.wait_ge(rounded_ready, g + 1)
                clip_shifted(nc, ints[:, :, :], rounded[:, :, :]).then_inc(ints_ready, 1)

            scales(0)
            clip(0)
            for g in range(NG):
                tiles = slice(g * GT, (g + 1) * GT)
                if g + 1 < NG:
                    scales(g + 1)
                dve.wait_ge(y_mm, g + 1)
                for j in range(GT):
                    n = g * GT + j
                    last = nc.vector.scalar_tensor_tensor(out=X[:, n, :], in0=ps[:, 2 + j // 2, j % 2 * D:(j % 2 + 1) * D],
                                                          scalar=so[:, n:n + 1], in1=X[:, n, :], op0=ALU.mult, op1=ALU.add)
                last.then_inc(y_added, 1)
                dve.wait_ge(y_added, g + 1)
                group_stats(nc, steps, X, stats, mv, g)
                nc.vector.tensor_scalar(rstd[:, tiles], mv[:, tiles, 1], EPS, None, ALU.add).then_inc(var_ready, 1)
                if g + 1 < NG:
                    clip(g + 1)
                dve.wait_ge(std_ready, g + 1)
                steps.then(nc.vector.reciprocal(rstd[:, tiles], std[:, tiles]))
                if g:
                    dve.wait_ge(xn_turned, g)
                normalise(nc, X, mv, rstd, xn, g).then_inc(xn_ready, 1)

        @block.tensor
        def _(pe):
            def turn_ints(g):
                pe.wait_ge(ints_ready, g + 1)
                turn_group(nc, ps, 0, ints, ident).then_inc(ints_turned, 1)

            turn_ints(0)
            for g in range(NG):
                pe.wait_ge(ints_copied, g + 1)
                if g:
                    pe.wait_ge(y_added, g)
                project_ints(nc, ps, 2, intsT, (wpT_h, wpT_l)).then_inc(y_mm, 1)
                if g + 1 < NG:
                    turn_ints(g + 1)
                pe.wait_ge(xn_ready, g + 1)
                if g >= 2:
                    pe.wait_ge(xn_copied, g - 1)
                turn_group(nc, ps, 4 + g % 2 * 2, xn, ident).then_inc(xn_turned, 1)


def phase_self(nc, t, X, otok, wpT_h, wpT_l, ident, mv, rstd, ps):
    with ExitStack() as outer:
        sb = lambda n, s, d=F32: outer.enter_context(nc.sbuf_tensor(n, s, d))
        W = {n: [sb(f"sW{n}_{x}", s, F32R) for x in ("hi", "lo")] for n, s in (
            ("q", [P, DC, SH * SD]), ("k", [P, DC, KV * SD]), ("v", [P, DC, KV * SD]), ("o", [P, SH, D]))}
        xT = sb("xT_self", [P, DC, T])
        phase_project(nc, t, X, otok, wpT_h, wpT_l, ident, mv, rstd, ps, xT, W)
        phase_attend(nc, t, X, ident, ps, xT, W)


def phase_attend(nc, t, X, ident, ps, xT, W):
    GB = GW // NQ
    NPROJ = GT + KV * (SG + 1)
    O_BANK = (4, 2, 3, 5)
    ctx = ExitStack()
    with ctx:
        sb = lambda n, s, d=F32: ctx.enter_context(nc.sbuf_tensor(n, s, d))
        sem = lambda n: ctx.enter_context(nc.semaphore(n))
        x_h, x_l = sb("x_h", [P, DC, GW], F32R), sb("x_l", [P, DC, GW], F32R)
        q = sb("q_self", [P, GB, SG, NQ])
        k = sb("k_self", [P, GW])
        o_h, o_l = sb("o_h", [P, SG, GW], F32R), sb("o_l", [P, SG, GW], F32R)
        v = sb("v_self", [P, GT, KV * SD])
        bq, bk = sb("sbq", [P, SH]), sb("sbk", [P, KV])
        bv_b = sb("sbv_b", [P, KV * SD])
        ones = sb("ones_self", [P, 1])
        smax = sb("smax", [P, GB])
        shifted = sb("shifted", [P, GB, NQ])
        probs = sb("probs_self", [P, GB, NQ])
        psum_, pinv = sb("prob_sum", [P, GB]), sb("prob_inv", [P, GB])
        pdiag = sb("pdiag", [P, GT, BT, P])
        b_loaded, ones_ready = sem("b_loaded"), sem("ones_ready")
        x_hi, x_split = sem("x_hi"), sem("x_split")
        proj_mm, proj_act, proj_dve = sem("proj_mm"), sem("proj_act"), sem("proj_dve")
        s_mm, s_max, s_shifted, s_exp, s_sum, s_inv, probs_ready = (sem(n) for n in (
            "s_mm", "s_max", "s_shifted", "s_exp", "s_sum", "s_inv", "probs_ready"))
        p_turned, pdiag_zero, pdiag_act, pdiag_dve = sem("p_turned"), sem("pdiag_zero"), sem("pdiag_act"), sem("pdiag_dve")
        o_mm, o_hi, o_split = sem("o_mm"), sem("o_hi"), sem("o_split")
        y_mm, y_added = sem("y_mm"), sem("y_added")
        block = ctx.enter_context(nc.Block())
        Y_CREDIT = 2

        def proj_index(kv, j):
            return kv * (SG + 1) + j + (GT if kv else 0)

        def value_index(j):
            return SG + 1 + j

        ON_ACT = [proj_index(kv, j) for kv in range(KV) for j in range(0, SG + 1, 2)]

        def copies(n):
            on_act = sum(m < n for m in ON_ACT)
            return on_act, n - on_act

        def by_batch(a):
            return a.rearrange("p (b n) -> p b n", b=GB)

        def groups(eng, one):
            one(0, None, True, False)
            with eng.Fori(0, NG - 2) as i:
                one(i + 1, i, False, False)
            one(NG - 1, NG - 2, False, True)

        def following(g, kv):
            return (g, kv + 1) if kv + 1 < KV else (g + 1, 0)

        @block.sync
        def _(sp):
            sp.dma_start(bq[:, :], t["sbq"]).then_inc(b_loaded, 16)
            sp.dma_start(bk[:, :], t["sbk"]).then_inc(b_loaded, 16)
            sp.dma_start(bv_b[:, :], t["sbv"].partition_broadcast(P)).then_inc(b_loaded, 16)

        @block.gpsimd
        def _(pool):
            pool.sem_inc(y_added, Y_CREDIT)
            nc.gpsimd.memset(ones[:, :], 1.0).then_inc(ones_ready, 1)
            nc.gpsimd.memset(pdiag[:, :, :, :], 0.0).then_inc(pdiag_zero, 1)
            pool.wait_ge(ones_ready, 1)
            for g in range(1, NG):
                cols = slice(g * GW, (g + 1) * GW)
                pool.wait_ge(proj_mm, g * NPROJ)
                nc.gpsimd.tensor_tensor(x_h[:, :, :], xT[:, :, cols], ones[:, :].unsqueeze(2).broadcast_to([P, DC, GW]),
                                        ALU.mult).then_inc(x_hi, 1)
                pool.wait_ge(x_hi, g + 1)
                nc.gpsimd.tensor_tensor(x_l[:, :, :], xT[:, :, cols], f32(x_h[:, :, :]), ALU.subtract).then_inc(x_split, 1)

        @block.scalar
        def _(act):
            def project_copy(g, kv, j):
                if j % 2 == 0:
                    n = proj_index(kv, j)
                    act.wait_ge(proj_mm, g * NPROJ + n + 1)
                    dst, bias = (q[:, :, j, :], bq[:, kv * SG + j:kv * SG + j + 1]) if j < SG else (by_batch(k[:, :]), bk[:, kv:kv + 1])
                    act.activation(dst, by_batch(ps[:, n % 2, :]), ACT.Identity, bias=bias).then_inc(proj_act, 1)

            def one(g, before, first, last_group):
                for kv in range(KV):
                    act.wait_ge(s_shifted, g * KV + kv + 1)
                    act.activation(probs[:, :, :], shifted[:, :, :], ACT.Exp, scale=float(SD) ** -0.5).then_inc(s_exp, 1)
                    if not (last_group and kv == KV - 1):
                        for j in range(SG + 1):
                            project_copy(*following(g, kv), j)
                    act.wait_ge(p_turned, g * KV + kv + 1)
                    for b in range(2):
                        rows = slice(b * NQ, (b + 1) * NQ)
                        last = act.activation(pdiag[rows, :, b, :], ps[rows, 5, :].rearrange("p (j n) -> p j n", j=GT), ACT.Copy)
                    last.then_inc(pdiag_act, 1)
                    for j in range(GT):
                        act.wait_ge(o_mm, (g * KV + kv) * GT + j + 1)
                        dst = o_h[:, :, j * P:(j + 1) * P].rearrange("p h (b n) -> p b h n", b=BT)
                        act.activation(dst, ps[:, O_BANK[j], :].rearrange("p (b h n) -> p b h n", b=BT, h=SG), ACT.Copy).then_inc(o_hi, 1)

            act.activation(x_h[:, :, :], xT[:, :, 0:GW], ACT.Copy).then_inc(x_hi, 1)
            act.wait_ge(b_loaded, 48)
            act.wait_ge(pdiag_zero, 1)
            for j in range(SG + 1):
                project_copy(0, 0, j)
            groups(act, one)

        @block.vector
        def _(dve):
            def project_copy(g, kv, j):
                if j % 2:
                    n = proj_index(kv, j)
                    dve.wait_ge(proj_mm, g * NPROJ + n + 1)
                    nc.vector.tensor_scalar(q[:, :, j, :], by_batch(ps[:, n % 2, :]), bq[:, kv * SG + j:kv * SG + j + 1], None,
                                            ALU.add).then_inc(proj_dve, 1)

            def values_copy(g):
                for j in range(GT):
                    dve.wait_ge(proj_mm, g * NPROJ + value_index(j) + 1)
                    nc.vector.tensor_tensor(v[:, j, :], ps[:, value_index(j) % 2, :], bv_b[:, :], ALU.add).then_inc(proj_dve, 1)

            def add_output(g, kv):
                for half in range(2):
                    dve.wait_ge(y_mm, (g * KV + kv) * 2 + half + 1)
                    x = X[:, bass.ds(g * GT + 2 * half, 2), :].rearrange("p n d -> p (n d)")
                    nc.vector.tensor_tensor(x, x, ps[:, 6 + half, :], ALU.add).then_inc(y_added, 1)

            def one(g, before, first, last_group):
                for kv in range(KV):
                    n = g * KV + kv + 1
                    more = not (last_group and kv == KV - 1)
                    scores = ps[:, 4, :].rearrange("p (b k) -> p b k", b=GB)
                    dve.wait_ge(s_mm, n)
                    nc.vector.tensor_reduce(smax[:, :], scores, AX, ALU.max).then_inc(s_max, 1)
                    dve.wait_ge(s_max, n)
                    nc.vector.tensor_tensor(shifted[:, :, :], scores, smax[:, :].unsqueeze(2).broadcast_to([P, GB, NQ]),
                                            ALU.subtract).then_inc(s_shifted, 1)
                    if more:
                        for j in range(2):
                            project_copy(*following(g, kv), j)
                    dve.wait_ge(s_exp, n)
                    nc.vector.tensor_reduce(psum_[:, :], probs[:, :, :], AX, ALU.add).then_inc(s_sum, 1)
                    dve.wait_ge(s_sum, n)
                    nc.vector.reciprocal(pinv[:, :], psum_[:, :]).then_inc(s_inv, 1)
                    dve.wait_ge(s_inv, n)
                    nc.vector.tensor_tensor(probs[:, :, :], probs[:, :, :], pinv[:, :].unsqueeze(2).broadcast_to([P, GB, NQ]),
                                            ALU.mult).then_inc(probs_ready, 1)
                    if more:
                        for j in range(2, SG + 1):
                            project_copy(*following(g, kv), j)
                    dve.wait_ge(p_turned, n)
                    dve.wait_ge(pdiag_act, n)
                    for b in range(2, BT):
                        rows = slice(b * NQ, (b + 1) * NQ)
                        last = nc.vector.tensor_copy(pdiag[rows, :, b, :], ps[rows, 5, :].rearrange("p (j n) -> p j n", j=GT))
                    last.then_inc(pdiag_dve, 1)
                    if kv:
                        add_output(g, kv - 1)
                    elif not first:
                        add_output(before, KV - 1)
                    for j in range(GT):
                        dve.wait_ge(o_hi, (g * KV + kv) * GT + j + 1)
                        dst = o_l[:, :, j * P:(j + 1) * P].rearrange("p h (b n) -> p b h n", b=BT)
                        hi = f32(o_h[:, :, j * P:(j + 1) * P]).rearrange("p h (b n) -> p b h n", b=BT)
                        nc.vector.tensor_tensor(dst, ps[:, O_BANK[j], :].rearrange("p (b h n) -> p b h n", b=BT, h=SG), hi,
                                                ALU.subtract).then_inc(o_split, 1)
                    if kv == KV - 1 and not last_group:
                        values_copy(g + 1)

            dve.wait_ge(x_hi, 1)
            nc.vector.tensor_tensor(x_l[:, :, :], xT[:, :, 0:GW], f32(x_h[:, :, :]), ALU.subtract).then_inc(x_split, 1)
            dve.wait_ge(b_loaded, 48)
            dve.wait_ge(pdiag_zero, 1)
            for j in range(SG + 1):
                project_copy(0, 0, j)
            values_copy(0)
            groups(dve, one)
            add_output(NG - 1, KV - 1)

        @block.tensor
        def _(pe):
            x2, o2 = (x_h, x_l), (o_h, o_l)

            def copied(g, n):
                on_act, on_dve = copies(n + 1)
                if n in ON_ACT:
                    pe.wait_ge(proj_act, g * copies(NPROJ)[0] + on_act)
                else:
                    pe.wait_ge(proj_dve, g * copies(NPROJ)[1] + on_dve)

            def bank_free(g, n):
                if n >= 2:
                    copied(g, n - 2)

            def project(g, kv):
                if kv == 0:
                    pe.wait_ge(x_split, g + 1)
                for j in range(SG + 1):
                    n = proj_index(kv, j)
                    bank_free(g, n)
                    w, col = (W["q"], (kv * SG + j) * SD) if j < SG else (W["k"], kv * SD)
                    for m, (c, (a, b)) in enumerate((c, x) for c in range(DC) for x in THREE):
                        last = nc.tensor.matmul(ps[:, n % 2, :], w[a][:, c, col:col + SD], x2[b][:, c, :],
                                                start=m == 0, stop=m == 3 * DC - 1)
                    last.then_inc(proj_mm, 1)

            def values(g):
                for j in range(GT):
                    n = value_index(j)
                    bank_free(g, n)
                    for m, (c, (a, b)) in enumerate((c, x) for c in range(DC) for x in THREE):
                        last = nc.tensor.matmul(ps[:, n % 2, :], x2[a][:, c, j * P:(j + 1) * P], W["v"][b][:, c, :],
                                                start=m == 0, stop=m == 3 * DC - 1)
                    last.then_inc(proj_mm, 1)

            def score(g, kv):
                copied(g, proj_index(kv, SG - 1))
                copied(g, proj_index(kv, SG))
                for b in range(GB):
                    cols = slice(b * NQ, (b + 1) * NQ)
                    last = nc.tensor.matmul(ps[:, 4, cols], q[:, b].rearrange("p h n -> p (h n)"), k[:, cols], start=True, stop=True)
                last.then_inc(s_mm, 1)

            def project_output(g, kv):
                for j in range(GT):
                    if j % 2 == 0:
                        pe.wait_ge(y_added, (g * KV + kv) * 2 + j // 2 + 1)
                    for m, (h, (a, b)) in enumerate((h, x) for h in range(SG) for x in THREE):
                        last = nc.tensor.matmul(ps[:, 6 + j // 2, j % 2 * D:(j % 2 + 1) * D], o2[a][:, h, j * P:(j + 1) * P],
                                                W["o"][b][:, kv * SG + h, :], start=m == 0, stop=m == 3 * SG - 1)
                    if j % 2:
                        last.then_inc(y_mm, 1)

            def one(g, before, first, last_group):
                for kv in range(KV):
                    n = g * KV + kv
                    more = not (last_group and kv == KV - 1)
                    start = first and kv == 0
                    if more:
                        project(*following(g, kv))
                    if not start:
                        pe.wait_ge(o_split, n * GT)
                    pe.wait_ge(probs_ready, n + 1)
                    for j in range(GT):
                        last = nc.tensor.transpose(ps[:, 5, j * P:(j + 1) * P],
                                                   probs[:, j * BT:(j + 1) * BT, :].rearrange("p b k -> p (b k)"), ident[:, :])
                    last.then_inc(p_turned, 1)
                    if kv:
                        project_output(g, kv - 1)
                    elif not first:
                        project_output(before, KV - 1)
                    pe.wait_ge(pdiag_act, n + 1)
                    pe.wait_ge(pdiag_dve, n + 1)
                    for j in range(GT):
                        nc.tensor.matmul(ps[:, O_BANK[j], :], v[:, j, kv * SD:(kv + 1) * SD], pdiag[:, j].rearrange("p b n -> p (b n)"),
                                         start=True, stop=True).then_inc(o_mm, 1)
                    if more:
                        if kv == KV - 1:
                            values(g + 1)
                        pe.wait_ge(o_split, n * GT + 1)
                        score(*following(g, kv))

            project(0, 0)
            values(0)
            score(0, 0)
            groups(pe, one)
            pe.wait_ge(o_split, NG * KV * GT)
            project_output(NG - 1, KV - 1)


class ExpertWeights:
    SHAPES = {"g": [P, DC, BW], "u": [P, DC, BW], "d": [P, SB, D], "s": [CWR, 1, BW]}

    def __init__(self, nc, t, ctx):
        sb = lambda n, s, d=F32: ctx.enter_context(nc.sbuf_tensor(n, s, d))
        self.nc, self.t = nc, t
        self.raw = {n: sb(f"raw_{n}", s) for n, s in self.SHAPES.items()}
        self.hi = {n: sb(f"hi_{n}", [s[0], 2, *s[1:]], F32R) for n, s in self.SHAPES.items()}
        self.lo = {n: sb(f"lo_{n}", [s[0], 2, *s[1:]], F32R) for n, s in self.SHAPES.items() if n != "s"}
        self.ones = sb("ones", [P, 1])
        self.loaded, self.hi_done, self.split_done, self.ones_ready = (ctx.enter_context(nc.semaphore(n)) for n in (
            "ew_loaded", "ew_hi", "ew_split", "ew_ones"))

    def load(self, sp, k):
        units = bass.ds(k * BW, BW)
        for n in ("g", "u"):
            sp.dma_start(self.raw[n][:, :, :], self.t["eW" + n][:, units].rearrange("(c p) n -> p c n", p=P)).then_inc(self.loaded, 16)
        sp.dma_start(self.raw["d"][:, :, :], self.t["eWd"][units, :].rearrange("(s p) d -> p s d", p=P)).then_inc(self.loaded, 16)
        sp.dma_start(self.raw["s"][:, :, :], self.t["sel"][:, units].rearrange("r (a n) -> r a n", a=1)).then_inc(self.loaded, 16)

    def split(self, pool, k, slot):
        pool.wait_ge(self.loaded, (k + 1) * 16 * len(self.SHAPES))
        for n in self.SHAPES:
            r = self.raw[n][:, :, :]
            one = self.ones[0:r.shape[0], :].unsqueeze(2).broadcast_to(list(r.shape))
            self.nc.gpsimd.tensor_tensor(self.hi[n][:, slot], r, one, ALU.mult).then_inc(self.hi_done, 1)
        pool.wait_ge(self.hi_done, (k + 1) * len(self.SHAPES))
        for n in self.lo:
            last = self.nc.gpsimd.tensor_tensor(self.lo[n][:, slot], self.raw[n][:, :, :], f32(self.hi[n][:, slot]), ALU.subtract)
        last.then_inc(self.split_done, 1)


def phase_experts(nc, t, X, ident, mv, rstd, ps):
    with ExitStack() as outer:
        sb = lambda n, s, d=F32: outer.enter_context(nc.sbuf_tensor(n, s, d))
        x_h, x_l = sb("xe_h", [P, DC, T], F32R), sb("xe_l", [P, DC, T], F32R)
        cwT = sb("cwT", [CWR, T], F32R)
        weights = ExpertWeights(nc, t, outer)
        phase_route(nc, t, X, ident, mv, rstd, ps, x_h, x_l, cwT, weights)
        phase_mix(nc, X, ps, x_h, x_l, cwT, weights)


def phase_route(nc, t, X, ident, mv, rstd, ps, x_h, x_l, cwT, weights):
    TOP = 4
    ctx = ExitStack()
    with ctx:
        sb = lambda n, s, d=F32: ctx.enter_context(nc.sbuf_tensor(n, s, d))
        sem = lambda n: ctx.enter_context(nc.semaphore(n))
        gate = sb("gate", [P, DC, NE])
        stats = sb("stats_r", [P, GT, 6])
        std = sb("std_r", [P, NT])
        xn = sb("xn_r", [P, 2, GT, D])
        x32 = sb("x32", [P, 2, DC, GW])
        logits = sb("logits", [P, NT, NE])
        key = sb("key", [P, NT, NE])
        top = sb("top", [P, NT, 8])
        above, equal = sb("above", [P, NT, NE]), sb("equal", [P, NT, NE])
        scan = [sb("scan0", [P, NT, NE]), sb("scan1", [P, NT, NE])]
        count = sb("count", [P, NT])
        left = sb("left", [P, NT])
        first, chosen = sb("first", [P, NT, NE]), sb("chosen", [P, NT, NE])
        shifted, expd, soft, weight = (sb(n, [P, NT, NE]) for n in ("shift_r", "expd", "soft", "weight"))
        small = sb("small", [P, NT, NC])
        norm, inv = sb("norm_r", [P, NT]), sb("inv_r", [P, NT])
        cw = sb("cw", [P, NT, CWR], F32R)
        g_loaded, dve_step, var_ready, std_ready = sem("g_loaded"), sem("dve_step"), sem("var_ready"), sem("std_ready")
        xn_ready, xn_turned, x_hi, x_split = sem("xn_ready"), sem("xn_turned"), sem("x_hi"), sem("x_split")
        x_copied, l_mm, l_ready = sem("x_copied"), sem("l_mm"), sem("l_ready")
        shift_ready, exp_ready, cw_ready, cw_turned, cw_copied = (sem(n) for n in (
            "shift_ready", "exp_ready", "cw_ready", "cw_turned", "cw_copied"))
        block = ctx.enter_context(nc.Block())

        @block.sync
        def _(sp):
            sp.dma_start(gate[:, :, :], t["gateT"].rearrange("(c p) e -> p c e", p=P)).then_inc(g_loaded, 16)
            weights.load(sp, 0)

        @block.gpsimd
        def _(pool):
            nc.gpsimd.memset(weights.ones[:, :], 1.0).then_inc(weights.ones_ready, 1)
            pool.wait_ge(weights.ones_ready, 1)
            weights.split(pool, 0, 0)

        @block.scalar
        def _(act):
            def deviations(g):
                tiles = slice(g * GT, (g + 1) * GT)
                act.wait_ge(var_ready, g + 1)
                act.activation(std[:, tiles], rstd[:, tiles], ACT.Sqrt).then_inc(std_ready, 1)

            deviations(0)
            for g in range(NG):
                bank = g % 2 * 2
                if g + 1 < NG:
                    deviations(g + 1)
                act.wait_ge(xn_turned, g + 1)
                act.activation(x_h[:, :, g * GW:(g + 1) * GW], ps[:, bank:bank + 2, :], ACT.Copy).then_inc(x_hi, 1)
                if g >= 2:
                    act.wait_ge(l_mm, g - 1)
                act.activation(x32[:, g % 2], ps[:, bank:bank + 2, :], ACT.Copy).then_inc(x_copied, 1)
            act.wait_ge(shift_ready, 1)
            act.activation(expd[:, :, :], shifted[:, :, :], ACT.Exp).then_inc(exp_ready, 1)
            for g in range(NG):
                act.wait_ge(cw_turned, g + 1)
                act.activation(cwT[:, g * GW:(g + 1) * GW], ps[0:CWR, 4 + g, :], ACT.Copy).then_inc(cw_copied, 1)

        @block.vector
        def _(dve):
            steps = Steps(dve, dve_step)

            def statistics(g):
                group_stats(nc, steps, X, stats, mv, g)
                tiles = slice(g * GT, (g + 1) * GT)
                nc.vector.tensor_scalar(rstd[:, tiles], mv[:, tiles, 1], EPS, None, ALU.add).then_inc(var_ready, 1)

            def split(g):
                dve.wait_ge(x_copied, g + 1)
                cols, bank = slice(g * GW, (g + 1) * GW), g % 2 * 2
                nc.vector.tensor_tensor(x_l[:, :, cols], ps[:, bank:bank + 2, :], f32(x_h[:, :, cols]), ALU.subtract).then_inc(x_split, 1)
                dve.wait_ge(l_mm, g + 1)
                nc.vector.tensor_copy(logits[:, g * GT:(g + 1) * GT, :], ps[:, 4 + g, 0:GT * NE].rearrange("p (j e) -> p j e", j=GT)) \
                    .then_inc(l_ready, 1)

            statistics(0)
            for g in range(NG):
                tiles = slice(g * GT, (g + 1) * GT)
                if g + 1 < NG:
                    statistics(g + 1)
                dve.wait_ge(std_ready, g + 1)
                steps.then(nc.vector.reciprocal(rstd[:, tiles], std[:, tiles]))
                normalise(nc, X, mv, rstd, xn[:, g % 2], g).then_inc(xn_ready, 1)
                if g:
                    split(g - 1)
            split(NG - 1)
            dve.wait_ge(l_ready, NG)
            v = nc.vector
            all_ = lambda a: a[:, :, :]
            over = lambda a: a.unsqueeze(2).broadcast_to([P, NT, NE])
            steps.then(v.tensor_scalar(all_(key), all_(logits), SATURATED, None, ALU.min))
            for n in range(NT):
                last = v.max(top[:, n, :], key[:, n, :])
            steps.then(last)
            fourth = over(top[:, :, TOP - 1])
            steps.then(v.tensor_tensor(all_(above), all_(key), fourth, ALU.is_gt))
            steps.then(v.tensor_tensor(all_(equal), all_(key), fourth, ALU.is_equal))
            steps.then(v.tensor_reduce(count[:, :], all_(above), AX, ALU.add))
            steps.then(v.tensor_scalar(left[:, :], count[:, :], -1.0, float(TOP), ALU.mult, ALU.add))
            src, s = equal, 1
            while s < NE:
                dst = scan[0] if src is not scan[0] else scan[1]
                steps.then(v.tensor_copy(dst[:, :, 0:s], src[:, :, 0:s]))
                steps.then(v.tensor_tensor(dst[:, :, s:NE], src[:, :, s:NE], src[:, :, 0:NE - s], ALU.add))
                src, s = dst, 2 * s
            steps.then(v.tensor_tensor(all_(first), all_(src), over(left[:, :]), ALU.is_le))
            steps.then(v.tensor_tensor(all_(first), all_(first), all_(equal), ALU.mult))
            steps.then(v.tensor_tensor(all_(chosen), all_(first), all_(above), ALU.add))
            steps.then(v.tensor_reduce(norm[:, :], all_(logits), AX, ALU.max))
            v.tensor_tensor(all_(shifted), all_(logits), over(norm[:, :]), ALU.subtract).then_inc(shift_ready, 1)
            dve.wait_ge(exp_ready, 1)
            steps.then(v.tensor_reduce(norm[:, :], all_(expd), AX, ALU.add))
            steps.then(v.reciprocal(inv[:, :], norm[:, :]))
            steps.then(v.tensor_tensor(all_(soft), all_(expd), over(inv[:, :]), ALU.mult))
            steps.then(v.tensor_tensor(all_(soft), all_(soft), all_(chosen), ALU.mult))
            steps.then(v.tensor_reduce(norm[:, :], all_(soft), AX, ALU.add))
            steps.then(v.reciprocal(inv[:, :], norm[:, :]))
            steps.then(v.tensor_tensor(all_(weight), all_(soft), over(inv[:, :]), ALU.mult))
            pairs = all_(weight).rearrange("p n (c two) -> p n c two", two=2)
            steps.then(v.tensor_reduce(all_(small), pairs, AX, ALU.add))
            steps.then(v.tensor_scalar(all_(small), all_(small), SMALL_SCALE, None, ALU.mult))
            at = 0
            for part, w in ((weight, NE), (small, NC)):
                steps.then(v.tensor_copy(cw[:, :, at:at + w], all_(part)))
                steps.then(v.tensor_tensor(cw[:, :, at + w:at + 2 * w], all_(part), f32(cw[:, :, at:at + w]), ALU.subtract))
                at += 2 * w
            v.engine_nop().then_inc(cw_ready, 1)

        @block.tensor
        def _(pe):
            def turn(g):
                pe.wait_ge(xn_ready, g + 1)
                if g >= 2:
                    pe.wait_ge(x_split, g - 1)
                    pe.wait_ge(x_copied, g - 1)
                turn_group(nc, ps, g % 2 * 2, xn[:, g % 2], ident).then_inc(xn_turned, 1)

            turn(0)
            pe.wait_ge(g_loaded, 16)
            for g in range(NG):
                if g + 1 < NG:
                    turn(g + 1)
                pe.wait_ge(x_copied, g + 1)
                for j in range(GT):
                    for c in range(DC):
                        last = nc.tensor.matmul(ps[:, 4 + g, j * NE:(j + 1) * NE], x32[:, g % 2, c, j * P:(j + 1) * P], gate[:, c, :],
                                                start=c == 0, stop=c == DC - 1)
                last.then_inc(l_mm, 1)
            pe.wait_ge(cw_ready, 1)
            for g in range(NG):
                for j in range(GT):
                    last = nc.tensor.transpose(ps[0:CWR, 4 + g, j * P:(j + 1) * P], f32(cw[:, g * GT + j, :]), ident[:, :])
                last.then_inc(cw_turned, 1)


def phase_mix(nc, X, ps, x_h, x_l, cwT, weights):
    ctx = ExitStack()
    with ctx:
        sb = lambda n, s, d=F32: ctx.enter_context(nc.sbuf_tensor(n, s, d))
        sem = lambda n: ctx.enter_context(nc.semaphore(n))
        hi, lo = weights.hi, weights.lo
        silu = sb("silu", [P, 2, GW])
        gated = sb("gated", [P, 2, GW])
        a = sb("act_raw", [P, 2, SB, GW])
        a_h, a_l = sb("act_h", [P, 2, SB, GW], F32R), sb("act_l", [P, 2, SB, GW], F32R)
        g_mm, u_mm, silu_ready, gated_ready, a_ready, a_hi, a_split = (sem(n) for n in (
            "g_mm", "u_mm", "silu_ready", "gated_ready", "a_ready", "a_hi", "a_split"))
        y_mm, y_added = sem("y_mm"), sem("y_added")
        block = ctx.enter_context(nc.Block())
        A_READY_CREDIT = 2
        A_SPLIT_CREDIT = 2 * SB
        Y_MM_CREDIT = 2 * 2
        Y_ADDED_CREDIT = 2
        UNITS = NG

        @block.sync
        def _(sp):
            with sp.Fori(0, NBLK - 1) as k:
                sp.wait_ge(weights.split_done, k + 1)
                weights.load(sp, k + 1)

        @block.gpsimd
        def _(pool):
            pool.sem_inc(a_ready, A_READY_CREDIT)
            pool.sem_inc(a_split, A_SPLIT_CREDIT)
            pool.sem_inc(y_mm, Y_MM_CREDIT)
            pool.sem_inc(y_added, Y_ADDED_CREDIT)

            def split_activations(k, ks):
                with pool.Fori(0, UNITS // 2) as gg:
                    for gu in range(2):
                        for s in range(SB):
                            pool.wait_ge(a_hi, (k * UNITS + gg * 2 + gu) * SB + s + 1)
                            nc.gpsimd.tensor_tensor(a_l[:, gu, s, :], a[:, gu, s, :], f32(a_h[:, gu, s, :]), ALU.subtract).then_inc(a_split, 1)

            with pool.Fori(0, NBLK // 2 - 1) as kk:
                for ks in range(2):
                    k = kk * 2 + ks
                    pool.wait_ge(y_mm, k * UNITS * 2 + Y_MM_CREDIT)
                    weights.split(pool, k + 1, 1 - ks)
                    split_activations(k, ks)
            k = NBLK - 2
            pool.wait_ge(y_mm, k * UNITS * 2 + Y_MM_CREDIT)
            weights.split(pool, k + 1, 1)
            split_activations(k, 0)
            split_activations(k + 1, 1)

        @block.scalar
        def _(act):
            with act.Fori(0, NBLK * UNITS // 2) as pair:
                for gu in range(2):
                    unit = pair * 2 + gu
                    for s in range(SB):
                        act.wait_ge(g_mm, unit * SB + s + 1)
                        act.activation(silu[:, s % 2, :], ps[:, s % 2, :], ACT.Silu).then_inc(silu_ready, 1)
                        act.wait_ge(a_ready, unit * SB + s + 1 + A_READY_CREDIT)
                        act.wait_ge(y_mm, unit * 2 + 2)
                        act.activation(a_h[:, gu, s, :], a[:, gu, s, :], ACT.Copy).then_inc(a_hi, 1)

        @block.vector
        def _(dve):
            with dve.Fori(0, NBLK // 2 * 2) as k:
                with dve.Fori(0, UNITS // 2) as gg:
                    for gu in range(2):
                        unit = k * UNITS + gg * 2 + gu
                        for s in range(SB):
                            n = unit * SB + s + 1
                            dve.wait_ge(silu_ready, n)
                            dve.wait_ge(u_mm, n)
                            nc.vector.tensor_tensor(gated[:, s % 2, :], silu[:, s % 2, :], ps[:, 2 + s % 2, :], ALU.mult).then_inc(gated_ready, 1)
                            dve.wait_ge(gated_ready, n)
                            dve.wait_ge(a_split, n)
                            nc.vector.tensor_tensor(a[:, gu, s, :], gated[:, s % 2, :], ps[:, 4 + s % 2, :], ALU.mult).then_inc(a_ready, 1)
                    for gu in range(2):
                        unit = k * UNITS + gg * 2 + gu
                        for half in range(2):
                            dve.wait_ge(y_mm, unit * 2 + half + 1 + Y_MM_CREDIT)
                            x = X[:, bass.ds((gg * 2 + gu) * GT + 2 * half, 2), :].rearrange("p n d -> p (n d)")
                            nc.vector.tensor_tensor(x, x, ps[:, 6 + half, :], ALU.add).then_inc(y_added, 1)

        @block.tensor
        def _(pe):
            x2 = (x_h, x_l)
            w2 = {n: (hi[n], lo[n]) for n in lo}
            with pe.Fori(0, NBLK // 2) as kk:
                for ks in range(2):
                    k = kk * 2 + ks
                    with pe.Fori(0, UNITS // 2) as gg:
                        pe.wait_ge(weights.split_done, k + 1)
                        for gu in range(2):
                            cols = bass.ds((gg * 2 + gu) * GW, GW)
                            for s in range(SB):
                                n = (k * UNITS + gg * 2 + gu) * SB + s + 1
                                units = slice(s * P, (s + 1) * P)
                                pe.wait_ge(a_ready, n)
                                for name, bank, done in (("g", s % 2, g_mm), ("u", 2 + s % 2, None)):
                                    for m, (c, (i, j)) in enumerate((c, x) for c in range(DC) for x in THREE):
                                        last = nc.tensor.matmul(ps[:, bank, :], w2[name][i][:, ks, c, units], x2[j][:, c, cols],
                                                                start=m == 0, stop=m == 3 * DC - 1)
                                    if done is not None:
                                        last.then_inc(done, 1)
                                nc.tensor.matmul(ps[:, 4 + s % 2, :], hi["s"][:, ks, 0, units], cwT[:, cols], start=True, stop=True) \
                                    .then_inc(u_mm, 1)
                        for gu in range(2):
                            unit = k * UNITS + gg * 2 + gu
                            pe.wait_ge(a_split, unit * SB + SB + A_SPLIT_CREDIT)
                            for j in range(GT):
                                if j % 2 == 0:
                                    pe.wait_ge(y_added, unit * 2 + j // 2 + 1)
                                for m, (s, (x, y)) in enumerate((s, x) for s in range(SB) for x in THREE):
                                    last = nc.tensor.matmul(ps[:, 6 + j // 2, j % 2 * D:(j % 2 + 1) * D],
                                                            (a_h, a_l)[x][:, gu, s, j * P:(j + 1) * P], w2["d"][y][:, ks, s, :],
                                                            start=m == 0, stop=m == 3 * SB - 1)
                                if j % 2:
                                    last.then_inc(y_mm, 1)


def kernel(**inputs):
    import numpy as np
    import concourse.bacc as bacc
    from concourse.bass_utils import run_bass_kernel_spmd
    a = {k: np.asarray(v) for k, v in inputs.items()}
    wkvT = a["L0_xattn_wkv"].T
    up = lambda w: w.transpose(1, 0, 2).reshape(D, -1)
    arrays = {
        "x": a["x"].reshape(T, D),
        "ctxT": a["ctx_2048"].transpose(0, 2, 1),
        "clast": a["ctx_2048"][:, NK - 1, :].T,
        "xwq": a["L0_xattn_wq"], "xwp": a["L0_xattn_wp"], "wkvT": wkvT, "wvT": wkvT[:, D:],
        "xbq": a["L0_xattn_bq"], "xbk": a["L0_xattn_bkv"][:D].reshape(DC, P).T, "xbv": a["L0_xattn_bkv"][D:],
        "xbp": a["L0_xattn_bp"],
        "sWq": a["L0_attn_Wq"], "sWk": a["L0_attn_Wk"], "sWv": a["L0_attn_Wv"], "sWo": a["L0_attn_Wo"],
        "sbq": a["L0_attn_bq"].reshape(SH, SD).T, "sbk": a["L0_attn_bk"].reshape(KV, SD).T, "sbv": a["L0_attn_bv"],
        "sbo": a["L0_attn_bo"],
        "gateT": a["L0_ffn_gate_w"].T,
        "eWg": np.concatenate([up(a["L0_ffn_Wg"]), up(a["L0_ffn_cWg"])], axis=1),
        "eWu": np.concatenate([up(a["L0_ffn_Wu"]), up(a["L0_ffn_cWu"])], axis=1),
        "eWd": np.concatenate([a["L0_ffn_Wd"].reshape(-1, D), a["L0_ffn_cWd"].reshape(-1, D)]),
    }
    arrays = {f"in_{k}": np.ascontiguousarray(v) for k, v in arrays.items()}
    sel = np.zeros((CWR, INTER), np.float32)
    sel[:2 * NE, :NE * EI] = np.tile(np.repeat(np.eye(NE), EI, axis=1), (2, 1))
    sel[2 * NE:, NE * EI:] = np.tile(np.repeat(np.eye(NC), CI, axis=1), (2, 1))
    arrays["in_sel"] = sel
    nc = bacc.Bacc("TRN2", target_bir_lowering=False, num_devices=1)
    t = {k[3:]: nc.dram_tensor(k, v.shape, mybir.dt.from_np(v.dtype), kind="ExternalInput").ap() for k, v in arrays.items()}
    out = nc.dram_tensor("out", (T, D), F32, kind="ExternalOutput").ap()
    program(nc, t, out)
    got = run_bass_kernel_spmd(nc, [arrays], core_ids=[0])
    return got.results[0]["out"].reshape(NB, NQ, D)
```

```python
import concourse.bass as bass
from concourse import mybir
from contextlib import ExitStack

F32 = mybir.dt.float32
F32R = mybir.dt.float32r
ALU = mybir.AluOpType
ACT = mybir.ActivationFunctionType
AX = mybir.AxisListType.X

P = 128
D = 256
DC = D // P
NB, NQ, NK = 64, 32, 257
T = NB * NQ
NT = T // P
BT = P // NQ
XH, XD = 16, 16
RB = XH // 4
RW = D // RB
KP = NK + 1
SH, SD, KV = 16, 128, 4
SG = SH // KV
GT = 4
GW = GT * P
NG = NT // GT
NE, EI = 32, 96
NC, CI = 16, 128
INTER = NE * EI + NC * CI
SB = 4
BW = SB * P
NBLK = INTER // BW
EP, CP = P // NE, P // NC
LARGE_BLK = NE * EI // BW
EPS = 1e-5
ROUND = 12582912.0
QMAX = 127.0
SMALL_SCALE = 0.05
SATURATED = 16.6355


def f32(ap):
    return ap.bitcast(F32)


class Steps:

    def __init__(self, eng, sem):
        self.eng, self.sem, self.base, self.n = eng, sem, 0, 0

    def begin(self, i, per_round, before=0):
        self.base, self.n, self.per_round = i * per_round + before, 0, per_round

    def end(self):
        assert self.n == self.per_round, (self.n, self.per_round)

    def then(self, ins):
        self.n += 1
        ins.then_inc(self.sem, 1)
        self.eng.wait_ge(self.sem, self.base + self.n)


def program(nc, t, out):
    vlast_dram = nc.dram_tensor("vlast_scratch", (NB, D), F32, kind="Internal").ap()
    ctx = ExitStack()
    with ctx:
        X = ctx.enter_context(nc.sbuf_tensor("resid", [P, NT, D], F32))
        otok = ctx.enter_context(nc.sbuf_tensor("otok", [P, NT, D], F32))
        wpT_h = ctx.enter_context(nc.sbuf_tensor("wpT_h", [P, DC, D], F32R))
        wpT_l = ctx.enter_context(nc.sbuf_tensor("wpT_l", [P, DC, D], F32R))
        ident = ctx.enter_context(nc.sbuf_tensor("ident", [P, P], F32))
        mv = ctx.enter_context(nc.sbuf_tensor("mv", [P, NT, 2], F32))
        rstd = ctx.enter_context(nc.sbuf_tensor("rstd", [P, NT], F32))
        so = ctx.enter_context(nc.sbuf_tensor("so", [P, NT], F32))
        ps = ctx.enter_context(nc.psum_tensor("ps", [P, 8, 512], F32))
        with ExitStack() as attention:
            self_w = SelfWeights(nc, t, attention)
            with ExitStack() as cross:
                qT = [cross.enter_context(nc.sbuf_tensor(f"qT_{x}", [P, DC, T], F32R)) for x in ("hi", "lo")]
                first = CrossFirst(nc, t, cross)
                phase_queries(nc, t, X, wpT_h, wpT_l, ident, mv, rstd, ps, qT, vlast_dram, first, self_w)
                phase_cross(nc, t, X, otok, so, ps, qT, ident, vlast_dram, first)
            phase_self(nc, t, X, otok, so, wpT_h, wpT_l, ident, mv, rstd, ps, self_w)
        phase_experts(nc, t, X, ident, mv, rstd, ps, out)


def row_scales(nc, steps, src, amax, s, rs):
    steps.then(nc.vector.tensor_reduce(amax, src, AX, ALU.max, apply_absolute_value=True))
    steps.then(nc.vector.tensor_scalar(s, amax, 1.0 / QMAX, 1e-8, ALU.mult, ALU.max))
    return nc.vector.reciprocal(rs, s)


def clip_shifted(nc, dst, src):
    return nc.vector.tensor_scalar(dst, src, ROUND + QMAX, ROUND - QMAX, ALU.min, ALU.max)


def group_stats(nc, steps, X, stats, mv, g):
    for j in range(GT):
        last = nc.vector.bn_stats(stats[:, j, :], X[:, g * GT + j, :])
    steps.then(last)
    for j in range(GT):
        last = nc.vector.bn_aggr(mv[:, g * GT + j, :], stats[:, j, :])
    steps.then(last)


def normalise(nc, X, mv, rstd, xn, g):
    for j in range(GT):
        n = g * GT + j
        last = nc.vector.tensor_scalar(xn[:, j, :], X[:, n, :], mv[:, n, 0:1], rstd[:, n:n + 1], ALU.subtract, ALU.mult)
    return last


def turn_group(nc, ps, bank, src, ident):
    for c in range(DC):
        for j in range(GT):
            last = nc.tensor.transpose(ps[:, bank + c, j * P:(j + 1) * P], src[:, j, c * P:(c + 1) * P], ident[:, :])
    return last


def project_ints(nc, ps, bank, intsT, w2):
    for j in range(GT):
        for n, (c, w) in enumerate((c, w) for c in range(DC) for w in w2):
            last = nc.tensor.matmul(ps[:, bank + j // 2, j % 2 * D:(j % 2 + 1) * D], intsT[:, c, j * P:(j + 1) * P], w[:, c, :],
                                    start=n == 0, stop=n == 2 * DC - 1)
    return last


class CrossFirst:

    def __init__(self, nc, t, ctx):
        sb = lambda n, s, d=F32: ctx.enter_context(nc.sbuf_tensor(n, s, d))
        sem = lambda n: ctx.enter_context(nc.semaphore(n))
        self.nc, self.t = nc, t
        self.wraw = sb("wkv_raw", [P, DC, 2 * D])
        self.wkv_h = sb("wkv_h", [P, DC, 2 * D], F32R)
        self.wkv_l = sb("wkv_l", [P, DC, 2 * D], F32R)
        self.craw = sb("craw", [P, BT, DC, NK])
        self.bk = sb("bk", [P, DC])
        self.bv_b = sb("bv_bc", [P, D])
        self.bp_b = sb("bp_b", [P, D])
        self.mask = sb("mask", [P, 8, NQ])
        self.ones = sb("ones_cross", [P, 1])
        self.w_loaded, self.w_hi, self.w_split = sem("wkv_loaded"), sem("wkv_hi"), sem("wkv_split")
        self.ctx_loaded = [sem(f"ctx_loaded{b}") for b in range(BT)]
        self.b_loaded = sem("bias_loaded")
        self.mask_step, self.ones_ready = sem("mask_step"), sem("ones_ready")

    def load(self, sp):
        sp.dma_start(self.wraw[:, :, :], self.t["wkvT"].rearrange("(c p) o -> p c o", p=P)).then_inc(self.w_loaded, 16)
        sp.dma_start(self.bk[:, :], self.t["xbk"]).then_inc(self.b_loaded, 16)
        sp.dma_start(self.bv_b[:, :], self.t["xbv"].partition_broadcast(P)).then_inc(self.b_loaded, 16)
        sp.dma_start(self.bp_b[:, :], self.t["xbp"].partition_broadcast(P)).then_inc(self.b_loaded, 16)
        for b in range(BT):
            sp.dma_start(self.craw[:, b], self.t["ctxT"][b].rearrange("(c p) k -> p c k", p=P)).then_inc(self.ctx_loaded[b], 16)

    def prepare(self, pool):
        nc, mask, hi = self.nc, self.mask[:, :, :], self.wkv_h[:, :, :]
        nc.gpsimd.memset(self.ones[:, :], 1.0).then_inc(self.ones_ready, 1)
        nc.gpsimd.memset(mask, 1.0).then_inc(self.mask_step, 1)
        pool.wait_ge(self.mask_step, 1)
        nc.gpsimd.affine_select(out=mask, in_=mask, compare_op=ALU.is_ge, fill=0.0, base=0,
                                pattern=[[-XD, 8], [0, NQ]], channel_multiplier=1).then_inc(self.mask_step, 1)
        pool.wait_ge(self.mask_step, 2)
        nc.gpsimd.affine_select(out=mask, in_=mask, compare_op=ALU.is_ge, fill=0.0, base=XD - 1,
                                pattern=[[XD, 8], [0, NQ]], channel_multiplier=-1).then_inc(self.mask_step, 1)
        pool.wait_ge(self.ones_ready, 1)
        pool.wait_ge(self.w_loaded, 16)
        nc.gpsimd.tensor_tensor(hi, self.wraw[:, :, :], self.ones[:, :].unsqueeze(2).broadcast_to([P, DC, 2 * D]),
                                ALU.mult).then_inc(self.w_hi, 1)
        pool.wait_ge(self.w_hi, 1)
        nc.gpsimd.tensor_tensor(self.wkv_l[:, :, :], self.wraw[:, :, :], f32(hi), ALU.subtract).then_inc(self.w_split, 1)


class SelfWeights:
    COLS = (SH + 2 * KV) * SD
    CHUNK = COLS // 4

    def __init__(self, nc, t, ctx):
        self.nc, self.t = nc, t
        self.parts = [ctx.enter_context(nc.sbuf_tensor(f"sWqkv_{x}", [P, DC, self.COLS], F32R)) for x in ("hi", "lo")]
        self.loaded = [ctx.enter_context(nc.semaphore(f"sw_loaded{n}")) for n in range(2)]
        self.hi_done, self.split_done = (ctx.enter_context(nc.semaphore(n)) for n in ("sw_hi", "sw_split"))
        self.W = {"q": [w[:, :, 0:SH * SD] for w in self.parts], "k": [w[:, :, SH * SD:(SH + KV) * SD] for w in self.parts],
                  "v": [w[:, :, (SH + KV) * SD:] for w in self.parts]}

    def load(self, sp, raw):
        for n in range(4):
            if n >= 2:
                sp.wait_ge(self.split_done, n - 1)
            cols = slice(n * self.CHUNK, (n + 1) * self.CHUNK)
            sp.dma_start(raw[:, n % 2], self.t["sWqkv"][:, cols].rearrange("(c p) n -> p c n", p=P)).then_inc(self.loaded[n % 2], 16)

    def split(self, pool, raw, ones):
        for n in range(4):
            hi, lo = (w[:, :, n * self.CHUNK:(n + 1) * self.CHUNK] for w in self.parts)
            pool.wait_ge(self.loaded[n % 2], 16 * (n // 2 + 1))
            self.nc.gpsimd.tensor_tensor(hi, raw[:, n % 2], ones[:, :].unsqueeze(2).broadcast_to([P, DC, self.CHUNK]),
                                         ALU.mult).then_inc(self.hi_done, 1)
            pool.wait_ge(self.hi_done, n + 1)
            self.nc.gpsimd.tensor_tensor(lo, raw[:, n % 2], f32(hi), ALU.subtract).then_inc(self.split_done, 1)


def phase_queries(nc, t, X, wpT_h, wpT_l, ident, mv, rstd, ps, qT, vlast_dram, first, self_w):
    ctx = ExitStack()
    with ctx:
        sb = lambda n, s, d=F32: ctx.enter_context(nc.sbuf_tensor(n, s, d))
        sem = lambda n: ctx.enter_context(nc.semaphore(n))
        wraw = sb("wraw", [P, 2, DC, D])
        wamax = sb("wamax", [P, 2, DC])
        wscale = sb("wscale", [P, 2, DC])
        wrs = sb("wrs", [P, 2, DC])
        wtmp = sb("wtmp", [P, 2, DC, D])
        wtmp2 = sb("wtmp2", [P, 2, DC, D])
        wints = sb("wints", [P, 2, DC, D])
        wdeq = sb("wdeq", [P, 2, DC, D])
        sraw = sb("sraw", [P, 2, DC, self_w.CHUNK])
        wqT_h = sb("wqT_h", [P, DC, D], F32R)
        wqT_l = sb("wqT_l", [P, DC, D], F32R)
        bq_b = sb("bq_b", [P, D])
        bv_b = sb("bv_b", [P, D])
        clast = sb("clast", [P, DC, NB])
        wv32 = sb("wv32", [P, DC, D])
        vlast = sb("vlast", [NB, D])
        shift = sb("shift", [P, 2])
        stats = sb("stats", [P, GT, 6])
        std = sb("std", [P, NT])
        xn = sb("xn", [P, GT, D])
        amax = sb("amax", [P, NT])
        sx = sb("sx", [P, NT])
        rs = sb("rs", [P, NT])
        rounded = sb("rounded", [P, GT, D])
        ints = sb("ints", [P, GT, D])
        intsT = sb("intsT", [P, DC, GW], F32R)
        q = sb("q", [P, GT, D])
        x_loaded = [sem(f"x_loaded{g}") for g in range(NG)]
        shift_ready = sem("shift_ready")
        w_loaded = [sem("wq_loaded"), sem("wp_loaded")]
        v_loaded, b_loaded = sem("v_loaded"), sem("b_loaded")
        ident_zero, ident_ready = sem("ident_zero"), sem("ident_ready")
        dve_step = sem("dve_step")
        w_deq, w_turned, w_hi, w_split = sem("w_deq"), sem("w_turned"), sem("w_hi"), sem("w_split")
        var_ready, std_ready = sem("var_ready"), sem("std_ready")
        xn_ready, scales_ready, rounded_ready = sem("xn_ready"), sem("scales_ready"), sem("rounded_ready")
        ints_ready, ints_turned, ints_copied = sem("ints_ready"), sem("ints_turned"), sem("ints_copied")
        q_mm, q_ready, q_turned, q_copied, q_split = (sem(n) for n in (
            "q_mm", "q_ready", "q_turned", "q_copied", "q_split"))
        vlast_mm, vlast_ready, vlast_stored = sem("vlast_mm"), sem("vlast_ready"), sem("vlast_stored")
        block = ctx.enter_context(nc.Block())

        @block.sync
        def _(sp):
            sp.dma_start(wraw[:, 0], t["xwq"].rearrange("(c p) i -> p c i", p=P)).then_inc(w_loaded[0], 16)
            for g in range(NG):
                sp.dma_start(X[:, g * GT:(g + 1) * GT, :],
                             t["x"][g * GW:(g + 1) * GW, :].rearrange("(n p) d -> p n d", p=P)).then_inc(x_loaded[g], 16)
                if g == 0:
                    sp.dma_start(wraw[:, 1], t["xwp"].rearrange("(c p) i -> p c i", p=P)).then_inc(w_loaded[1], 16)
            first.load(sp)
            self_w.load(sp, sraw)
            sp.wait_ge(vlast_ready, 1)
            sp.dma_start(vlast_dram, vlast[:, :]).then_inc(vlast_stored, 16)
            sp.wait_ge(vlast_stored, 16)

        @block.gpsimd
        def _(pool):
            nc.gpsimd.memset(ident[:, :], 0.0).then_inc(ident_zero, 1)
            nc.gpsimd.memset(shift[:, 0:1], ROUND)
            nc.gpsimd.memset(shift[:, 1:2], -ROUND).then_inc(shift_ready, 1)
            pool.wait_ge(ident_zero, 1)
            nc.gpsimd.affine_select(out=ident[:, :], in_=ident[:, :], compare_op=ALU.not_equal, fill=1.0, base=0,
                                    pattern=[[-1, P]], channel_multiplier=1).then_inc(ident_ready, 1)
            first.prepare(pool)
            self_w.split(pool, sraw, first.ones)

        @block.scalar
        def _(act):
            nc.scalar.preload_act_table(ACT.Sqrt)
            act.dma_start(bq_b[:, :], t["xbq"].partition_broadcast(P)).then_inc(b_loaded, 16)
            act.dma_start(bv_b[:, :], t["xbv"].partition_broadcast(P)).then_inc(b_loaded, 16)
            act.dma_start(clast[:, :, :], t["clast"].rearrange("(c p) b -> p c b", p=P)).then_inc(v_loaded, 16)
            act.dma_start(wv32[:, :, :], t["wvT"].rearrange("(c p) o -> p c o", p=P)).then_inc(v_loaded, 16)
            def weight_hi(w):
                act.wait_ge(w_turned, w + 1)
                act.activation((wqT_h, wpT_h)[w][:, :, :], ps[:, 6, :].rearrange("p (c o) -> p c o", c=DC), ACT.Copy).then_inc(w_hi, 1)

            def deviations(g):
                tiles = slice(g * GT, (g + 1) * GT)
                act.wait_ge(var_ready, g + 1)
                act.activation(std[:, tiles], rstd[:, tiles], ACT.Sqrt).then_inc(std_ready, 1)

            def queries_hi(g):
                act.wait_ge(q_turned, g + 1)
                act.activation(qT[0][:, :, g * GW:(g + 1) * GW], ps[:, 4:6, :], ACT.Copy, scale=float(XD) ** -0.5).then_inc(q_copied, 1)

            def round_ints(g):
                act.wait_ge(scales_ready, g + 1)
                for j in range(GT):
                    n = g * GT + j
                    last = act.activation(rounded[:, j, :], xn[:, j, :], ACT.Identity, bias=shift[:, 0:1], scale=rs[:, n:n + 1])
                last.then_inc(rounded_ready, 1)

            def copy_ints(g):
                act.wait_ge(ints_turned, g + 1)
                act.activation(intsT[:, :, :], ps[:, 0:2, :], ACT.Identity, bias=shift[:, 1:2]).then_inc(ints_copied, 1)

            act.wait_ge(shift_ready, 1)
            weight_hi(0)
            deviations(0)
            round_ints(0)
            deviations(1)
            copy_ints(0)
            round_ints(1)
            deviations(2)
            for g in range(NG):
                if g + 1 < NG:
                    copy_ints(g + 1)
                queries_hi(g)
                if g + 2 < NG:
                    round_ints(g + 2)
                if g + 3 < NG:
                    deviations(g + 3)
                if g == 2:
                    weight_hi(1)

        @block.vector
        def _(dve):
            steps = Steps(dve, dve_step)
            def weight(w):
                amax, scale, rscale = wamax[:, w, :], wscale[:, w, :], wrs[:, w, :]
                rows = lambda a: a.unsqueeze(2).broadcast_to([P, DC, D])
                dve.wait_ge(w_loaded[w], 16)
                steps.then(nc.vector.tensor_reduce(amax, wraw[:, w], AX, ALU.max, apply_absolute_value=True))
                steps.then(nc.vector.tensor_scalar(scale, amax, 1.0 / QMAX, 1e-8, ALU.mult, ALU.max))
                steps.then(nc.vector.reciprocal(rscale, scale))
                steps.then(nc.vector.tensor_tensor(wtmp[:, w], wraw[:, w], rows(rscale), ALU.mult))
                steps.then(nc.vector.tensor_scalar(wtmp2[:, w], wtmp[:, w], ROUND, ROUND, ALU.add, ALU.subtract))
                steps.then(nc.vector.tensor_scalar(wints[:, w], wtmp2[:, w], QMAX, -QMAX, ALU.min, ALU.max))
                nc.vector.tensor_tensor(wdeq[:, w], wints[:, w], rows(scale), ALU.mult).then_inc(w_deq, 1)

            def weight_lo(w):
                dve.wait_ge(w_hi, w + 1)
                lo, hi = ((wqT_l, wqT_h), (wpT_l, wpT_h))[w]
                nc.vector.tensor_tensor(lo[:, :, :], ps[:, 6, :].rearrange("p (c o) -> p c o", c=DC), f32(hi[:, :, :]),
                                        ALU.subtract).then_inc(w_split, 1)

            def last_values():
                dve.wait_ge(vlast_mm, 1)
                nc.vector.tensor_tensor(vlast[:, :], ps[0:NB, 7, 0:D], bv_b[0:NB, :], ALU.add).then_inc(vlast_ready, 1)

            def statistics(g):
                dve.wait_ge(x_loaded[g], 16)
                group_stats(nc, steps, X, stats, mv, g)
                tiles = slice(g * GT, (g + 1) * GT)
                nc.vector.tensor_scalar(rstd[:, tiles], mv[:, tiles, 1], EPS, None, ALU.add).then_inc(var_ready, 1)

            def scales(g):
                tiles = slice(g * GT, (g + 1) * GT)
                dve.wait_ge(std_ready, g + 1)
                steps.then(nc.vector.reciprocal(rstd[:, tiles], std[:, tiles]))
                steps.then(normalise(nc, X, mv, rstd, xn, g))
                row_scales(nc, steps, xn[:, :, :], amax[:, tiles], sx[:, tiles], rs[:, tiles]).then_inc(scales_ready, 1)

            def clip(g):
                dve.wait_ge(rounded_ready, g + 1)
                if g:
                    dve.wait_ge(ints_turned, g)
                clip_shifted(nc, ints[:, :, :], rounded[:, :, :]).then_inc(ints_ready, 1)

            weight(0)
            statistics(0)
            scales(0)
            statistics(1)
            weight_lo(0)
            clip(0)
            scales(1)
            statistics(2)
            dve.wait_ge(b_loaded, 32)
            for g in range(NG):
                if g + 1 < NG:
                    clip(g + 1)
                dve.wait_ge(q_mm, g + 1)
                for j in range(GT):
                    last = nc.vector.scalar_tensor_tensor(out=q[:, j, :], in0=ps[:, 2 + j // 2, j % 2 * D:(j % 2 + 1) * D],
                                                          scalar=sx[:, g * GT + j:g * GT + j + 1], in1=bq_b[:, :], op0=ALU.mult, op1=ALU.add)
                last.then_inc(q_ready, 1)
                if g + 2 < NG:
                    scales(g + 2)
                if g == 2:
                    weight(1)
                dve.wait_ge(q_copied, g + 1)
                cols = slice(g * GW, (g + 1) * GW)
                nc.vector.scalar_tensor_tensor(out=qT[1][:, :, cols], in0=ps[:, 4:6, :], scalar=float(XD) ** -0.5,
                                               in1=f32(qT[0][:, :, cols]), op0=ALU.mult, op1=ALU.subtract).then_inc(q_split, 1)
                if g + 3 < NG:
                    statistics(g + 3)
                if g == 2:
                    last_values()
            weight_lo(1)

        @block.tensor
        def _(pe):
            pe.wait_ge(ident_ready, 1)

            def turn_weight(w):
                pe.wait_ge(w_deq, w + 1)
                for c in range(DC):
                    for o in range(DC):
                        last = nc.tensor.transpose(ps[:, 6, c * D + o * P:c * D + (o + 1) * P], wdeq[:, w, o, c * P:(c + 1) * P], ident[:, :])
                last.then_inc(w_turned, 1)

            def turn_ints(g):
                pe.wait_ge(ints_ready, g + 1)
                turn_group(nc, ps, 0, ints, ident).then_inc(ints_turned, 1)

            turn_weight(0)
            pe.wait_ge(v_loaded, 32)
            for c in range(DC):
                last = nc.tensor.matmul(ps[0:NB, 7, 0:D], clast[:, c, :], wv32[:, c, :], start=c == 0, stop=c == DC - 1)
            last.then_inc(vlast_mm, 1)
            turn_ints(0)
            pe.wait_ge(w_split, 1)

            def project(g):
                pe.wait_ge(ints_copied, g + 1)
                project_ints(nc, ps, 2, intsT, (wqT_h, wqT_l)).then_inc(q_mm, 1)

            project(0)
            turn_ints(1)
            for g in range(NG):
                pe.wait_ge(q_ready, g + 1)
                if g:
                    pe.wait_ge(q_split, g)
                turn_group(nc, ps, 4, q, ident).then_inc(q_turned, 1)
                if g + 1 < NG:
                    project(g + 1)
                if g + 2 < NG:
                    turn_ints(g + 2)
                if g == 2:
                    turn_weight(1)


THREE = ((0, 0), (0, 1), (1, 0))


def phase_cross(nc, t, X, otok, so, ps, qT, ident, vlast_dram, first):
    ctx = ExitStack()
    with ctx:
        sb = lambda n, s, d=F32: ctx.enter_context(nc.sbuf_tensor(n, s, d))
        sem = lambda n: ctx.enter_context(nc.semaphore(n))
        wkv_h, wkv_l, craw, mask, ctx_loaded = first.wkv_h, first.wkv_l, first.craw, first.mask, first.ctx_loaded
        bk, bv_b = first.bk, first.bv_b
        ch = sb("ch", [P, 2, DC, KP], F32R)
        cl = sb("cl", [P, 2, DC, KP], F32R)
        kh = sb("kh", [P, 2, DC, KP], F32R)
        kl = sb("kl", [P, 2, DC, KP], F32R)
        qh = sb("qh", [P, 2, DC, 8, NQ], F32R)
        ql = sb("ql", [P, 2, DC, 8, NQ], F32R)
        v = sb("v", [P, 2, 2, D])
        vl = sb("vl", [P, BT, D])
        last_part = sb("last_part", [P, 2, RB, RW])
        osum = sb("osum", [P, D])
        otile = sb("otile", [P, D])
        amax, scale, rs = sb("amax_o", [P, 1]), sb("scale_o", [P, 1]), sb("rs_o", [P, 1])
        rounded = sb("rounded_o", [P, D])
        probs = sb("probs", [P, RB, KP])
        nmax = sb("nmax", [P, 2, RB])
        rsum = sb("rsum", [P, 2, RB])
        rinv = sb("rinv", [P, 2, RB])
        pT = sb("pT", [P, 2, 512])
        bp_added = sem("bp_added")
        vl_loaded = [sem(f"vl_loaded{b}") for b in range(BT)]
        pad_ready = sem("pad_ready")
        ctx_hi, ctx_split = sem("ctx_hi"), sem("ctx_split")
        k_mm, k_hi, k_split, q_masked = sem("k_mm"), sem("k_hi"), sem("k_split"), sem("q_masked")
        s_mm, nmax_ready, exp_done = sem("s_mm"), sem("nmax_ready"), sem("exp_done")
        v_mm, v_ready = sem("v_mm"), sem("v_ready")
        p_turned, pT_dve, pT_act = sem("p_turned"), sem("pT_dve"), sem("pT_act")
        rinv_ready, o_mm, o_ready, last_ready = sem("rinv_ready"), sem("o_mm"), sem("o_ready"), sem("last_ready")
        o_stored, quant_step, quantised = sem("o_stored"), sem("quant_step"), sem("quantised")
        block = ctx.enter_context(nc.Block())

        O_CREDIT = 2

        def rounds(eng, one):
            with eng.Fori(0, NT - 1) as it:
                for b in range(BT):
                    one(it, b, 2)
            for b in range(BT):
                one(NT - 1, b, min(2, BT - 1 - b))

        @block.sync
        def _(sp):
            for b in range(BT):
                sp.dma_start(vl[:, b, :], vlast_dram[b].partition_broadcast(P)).then_inc(vl_loaded[b], 16)
            with sp.Fori(0, NT - 1) as it:
                for b in range(BT):
                    sp.wait_ge(ctx_split, it * BT + b + 1)
                    sp.dma_start(craw[:, b], t["ctxT"][bass.ds(it * BT + BT + b, 1)].rearrange("a (c p) k -> p (a c) k", p=P)) \
                        .then_inc(ctx_loaded[b], 16)
                    sp.wait_ge(last_ready, it * BT + b + 1)
                    sp.dma_start(vl[:, b, :], vlast_dram[bass.ds(it * BT + BT + b, 1)].rearrange("a d -> (a d)").partition_broadcast(P)) \
                        .then_inc(vl_loaded[b], 16)

        @block.gpsimd
        def _(pool):
            for s in (ch, cl):
                nc.gpsimd.memset(f32(s[:, :, :, NK:KP]), 0.0).then_inc(pad_ready, 1)
            pool.sem_inc(o_ready, O_CREDIT)

            def prepare(n, slot):
                u = slot % 2
                pool.wait_ge(ctx_hi, n + 1)
                nc.gpsimd.tensor_tensor(cl[:, u, :, 0:NK], craw[:, slot], f32(ch[:, u, :, 0:NK]), ALU.subtract).then_inc(ctx_split, 1)
                for dst, src in ((qh, qT[0]), (ql, qT[1])):
                    for c in range(DC):
                        last = nc.gpsimd.tensor_tensor(dst[:, u, c], f32(src[:, c, bass.ds(n * NQ, NQ)]).unsqueeze(1).broadcast_to([P, 8, NQ]),
                                                       mask[:, :, :], ALU.mult)
                last.then_inc(q_masked, 1)

            def last_key(n, it, b):
                pool.wait_ge(vl_loaded[b], it * 16 + 16)
                pool.wait_ge(exp_done, (n + 1) * RB)
                pool.wait_ge(o_ready, n - 1 + O_CREDIT)
                nc.gpsimd.tensor_tensor(last_part[:, b % 2], vl[:, b, :].rearrange("p (r d) -> p r d", r=RB),
                                        probs[:, :, NK - 1:NK].broadcast_to([P, RB, RW]), ALU.mult).then_inc(last_ready, 1)

            def one(it, b, more):
                last_key(it * BT + b, it, b)
                if b == 0:
                    x = X[:, bass.ds(it, 1), :].rearrange("p n d -> p (n d)")
                    nc.gpsimd.tensor_tensor(x, x, first.bp_b[:, :], ALU.add).then_inc(bp_added, 1)
                if more == 2:
                    pool.wait_ge(s_mm, (it * BT + b + 1) * RB)
                    prepare(it * BT + b + 2, (b + 2) % BT)

            prepare(0, 0)
            prepare(1, 1)
            pool.wait_ge(first.b_loaded, 48)
            rounds(pool, one)

        @block.scalar
        def _(act):
            act.wait_ge(first.b_loaded, 48)

            def context_hi(n, slot, loads):
                act.wait_ge(ctx_loaded[slot], loads * 16)
                act.activation(ch[:, slot % 2, :, 0:NK], craw[:, slot], ACT.Copy).then_inc(ctx_hi, 1)

            def keys_hi(n, u):
                for c in range(DC):
                    act.wait_ge(k_mm, n * DC + c + 1)
                    act.activation(kh[:, u, c, :], ps[:, 4 + c, 0:KP], ACT.Identity, bias=bk[:, c:c + 1]).then_inc(k_hi, 1)

            def exps(n, u):
                for r in range(RB):
                    act.wait_ge(nmax_ready, n * 2 + r // 2 + 1)
                    act.activation(probs[:, r, 0:NK], ps[:, r, 0:NK], ACT.Exp, bias=nmax[:, u, r:r + 1],
                                   accum_out=rsum[:, u, r:r + 1]).then_inc(exp_done, 1)

            def one(it, b, more):
                n = it * BT + b
                if more >= 2:
                    act.wait_ge(v_mm, n + 1)
                    context_hi(n + 2, (b + 2) % BT, it + 1 + (b + 2) // BT)
                if more >= 1:
                    keys_hi(n + 1, (b + 1) % 2)
                act.wait_ge(p_turned, n * 2 + 2)
                act.activation(pT[:, 1, :], ps[:, 5, :], ACT.Copy).then_inc(pT_act, 1)
                if more >= 1:
                    act.wait_ge(last_ready, n + 1)
                    exps(n + 1, (b + 1) % 2)

            context_hi(0, 0, 1)
            context_hi(1, 1, 1)
            keys_hi(0, 0)
            exps(0, 0)
            rounds(act, one)

        @block.vector
        def _(dve):
            dve.wait_ge(first.b_loaded, 48)

            def keys_lo(n, u):
                for c in range(DC):
                    dve.wait_ge(k_hi, n * DC + c + 1)
                    nc.vector.scalar_tensor_tensor(out=kl[:, u, c, :], in0=ps[:, 4 + c, 0:KP], scalar=bk[:, c:c + 1],
                                                   in1=f32(kh[:, u, c, :]), op0=ALU.add, op1=ALU.subtract).then_inc(k_split, 1)

            def values(n, u):
                dve.wait_ge(v_mm, n + 1)
                nc.vector.tensor_tensor(v[:, u], ps[:, 6, :].rearrange("p (k d) -> p k d", k=2),
                                        bv_b[:, :].unsqueeze(1).broadcast_to([P, 2, D]), ALU.add).then_inc(v_ready, 1)

            def maxima(n, u):
                for half in range(2):
                    dve.wait_ge(s_mm, n * RB + 2 * half + 2)
                    nc.vector.tensor_reduce(nmax[:, u, 2 * half:2 * half + 2], ps[:, 2 * half:2 * half + 2, 0:NK], AX, ALU.max,
                                            negate=True).then_inc(nmax_ready, 1)

            def quantise(tile, step):
                if step:
                    dve.wait_ge(quant_step, tile * 5 + step)
                else:
                    dve.wait_ge(o_stored, tile * BT + BT)
                if step == 0:
                    ins = nc.vector.tensor_reduce(amax[:, :], otile[:, :], AX, ALU.max, apply_absolute_value=True)
                elif step == 1:
                    ins = nc.vector.tensor_scalar(so[:, bass.ds(tile, 1)], amax[:, :], 1.0 / QMAX, 1e-8, ALU.mult, ALU.max)
                elif step == 2:
                    ins = nc.vector.tensor_scalar(scale[:, :], amax[:, :], 1.0 / QMAX, 1e-8, ALU.mult, ALU.max)
                elif step == 3:
                    ins = nc.vector.reciprocal(rs[:, :], scale[:, :])
                else:
                    ins = nc.vector.tensor_scalar(rounded[:, :], otile[:, :], rs[:, :], ROUND, ALU.mult, ALU.add)
                ins.then_inc(quant_step, 1)
                if step == 4:
                    dve.wait_ge(quant_step, tile * 5 + 5)
                    clip_shifted(nc, otok[:, bass.ds(tile, 1), :].rearrange("p n d -> p (n d)"), rounded[:, :]).then_inc(quantised, 1)

            def one(it, b, more, before):
                n, u = it * BT + b, b % 2
                quant = b == 0 and before is not None
                if more >= 1:
                    keys_lo(n + 1, 1 - u)
                    values(n + 1, 1 - u)
                if quant:
                    quantise(before, 0)
                dve.wait_ge(exp_done, (n + 1) * RB)
                nc.vector.reciprocal(rinv[:, u, :], rsum[:, u, :]).then_inc(rinv_ready, 1)
                if quant:
                    quantise(before, 1)
                dve.wait_ge(p_turned, n * 2 + 1)
                nc.vector.tensor_copy(pT[:, 0, :], ps[:, 4, :]).then_inc(pT_dve, 1)
                if quant:
                    quantise(before, 2)
                if more >= 1:
                    maxima(n + 1, 1 - u)
                if quant:
                    quantise(before, 3)
                    quantise(before, 4)
                dve.wait_ge(o_mm, n + 1)
                dve.wait_ge(last_ready, n + 1)
                nc.vector.tensor_tensor(osum[:, :], ps[:, 7, 0:D], last_part[:, u].rearrange("p r d -> p (r d)"), ALU.add).then_inc(o_ready, 1)
                dve.wait_ge(rinv_ready, n + 1)
                dve.wait_ge(o_ready, n + 1 + O_CREDIT)
                for h in range(4):
                    rows = slice(h * NQ, (h + 1) * NQ)
                    dst = otile[b * NQ:(b + 1) * NQ, :].rearrange("p (r h d) -> p r h d", r=RB, h=4)[:, :, h, :]
                    src = osum[rows, :].rearrange("p (r h d) -> p r h d", r=RB, h=4)[:, :, h, :]
                    last = nc.vector.tensor_tensor(dst, src, rinv[rows, u, :].unsqueeze(2).broadcast_to([NQ, RB, XD]), ALU.mult)
                last.then_inc(o_stored, 1)

            keys_lo(0, 0)
            values(0, 0)
            maxima(0, 0)
            for b in range(BT):
                one(0, b, 2, None)
            with dve.Fori(0, NT - 2) as before:
                for b in range(BT):
                    one(before + 1, b, 2, before)
            for b in range(BT):
                one(NT - 1, b, min(2, BT - 1 - b), NT - 2)
            for step in range(5):
                quantise(NT - 1, step)

        @block.tensor
        def _(pe):
            pe.wait_ge(first.w_split, 1)
            pe.wait_ge(pad_ready, 2)
            w2, c2, k2, q2 = (wkv_h, wkv_l), (ch, cl), (kh, kl), (qh, ql)

            def keys(n, u):
                pe.wait_ge(ctx_split, n + 1)
                for o in range(DC):
                    for m, (c, (i, j)) in enumerate((c, x) for c in range(DC) for x in THREE):
                        last = nc.tensor.matmul(ps[:, 4 + o, 0:KP], w2[i][:, c, o * P:(o + 1) * P], c2[j][:, u, c, :],
                                                start=m == 0, stop=m == 3 * DC - 1)
                    last.then_inc(k_mm, 1)

            def values(n, u):
                for kb in range(2):
                    for m, (c, (i, j)) in enumerate((c, x) for c in range(DC) for x in THREE):
                        last = nc.tensor.matmul(ps[:, 6, kb * D:(kb + 1) * D], c2[i][:, u, c, kb * P:(kb + 1) * P],
                                                w2[j][:, c, D:2 * D], start=m == 0, stop=m == 3 * DC - 1)
                last.then_inc(v_mm, 1)

            def scores(n, u):
                pe.wait_ge(k_split, (n + 1) * DC)
                pe.wait_ge(q_masked, n + 1)
                for r in range(RB):
                    rows = slice(r % 2 * 4, r % 2 * 4 + 4)
                    for m, (i, j) in enumerate(THREE):
                        last = nc.tensor.matmul(ps[:, r, 0:KP], q2[i][:, u, r // 2, rows, :].rearrange("p h n -> p (h n)"),
                                                k2[j][:, u, r // 2, :], start=m == 0, stop=m == 2)
                    last.then_inc(s_mm, 1)

            def one(it, b, more):
                n, u = it * BT + b, b % 2
                if more >= 1:
                    keys(n + 1, 1 - u)
                    pe.wait_ge(v_ready, n + 1)
                    values(n + 1, 1 - u)
                pe.wait_ge(exp_done, (n + 1) * RB)
                for kb in range(2):
                    if more >= 1:
                        pe.wait_ge(k_split, (n + 1) * DC + kb + 1)
                    for r in range(RB):
                        last = nc.tensor.transpose(ps[:, 4 + kb, r * P:(r + 1) * P], probs[:, r, kb * P:(kb + 1) * P], ident[:, :])
                    last.then_inc(p_turned, 1)
                if more >= 1:
                    scores(n + 1, 1 - u)
                else:
                    pe.wait_ge(v_ready, n + 1)
                pe.wait_ge(o_ready, n + O_CREDIT)
                pe.wait_ge(pT_act, n + 1)
                pe.wait_ge(pT_dve, n + 1)
                for r in range(RB):
                    cols = slice(r * RW, (r + 1) * RW)
                    for kb in range(2):
                        last = nc.tensor.matmul(ps[:, 7, cols], pT[:, kb, r * P:(r + 1) * P], v[:, u, kb, cols],
                                                start=kb == 0, stop=kb == 1)
                last.then_inc(o_mm, 1)

            keys(0, 0)
            values(0, 0)
            scores(0, 0)
            rounds(pe, one)


def phase_project(nc, t, X, otok, so, wpT_h, wpT_l, ident, mv, rstd, ps, xT, W, x_h, x_l):
    HH = SH // 2
    ctx = ExitStack()
    with ctx:
        sb = lambda n, s, d=F32: ctx.enter_context(nc.sbuf_tensor(n, s, d))
        sem = lambda n: ctx.enter_context(nc.semaphore(n))
        wraw = sb("self_wraw", [P, 2, HH, D])
        bo_b = sb("bo_b", [P, D])
        shift = sb("shift_p", [P, 1])
        stats = sb("stats_p", [P, GT, 6])
        std = sb("std_p", [P, NT])
        intsT = sb("intsT_p", [P, DC, GW], F32R)
        xn = sb("xn_p", [P, GT, D])
        b_loaded, shift_ready = sem("b_loaded"), sem("shift_ready")
        w_loaded = [sem("w_loaded0"), sem("w_loaded1")]
        w_hi, w_split = sem("w_hi"), sem("w_split")
        dve_step = sem("dve_step")
        ints_turned, ints_copied, y_mm = sem("ints_turned"), sem("ints_copied"), sem("y_mm")
        y_added, bias_added = sem("y_added"), sem("bias_added")
        var_ready, std_ready = sem("var_ready"), sem("std_ready")
        x_hi, x_split = sem("x_hi"), sem("x_split")
        xn_ready, xn_turned, xn_copied = sem("xn_ready"), sem("xn_turned"), sem("xn_copied")
        block = ctx.enter_context(nc.Block())

        def half(w, n):
            return w[:, n * HH:(n + 1) * HH, :]

        @block.sync
        def _(sp):
            for n in range(2):
                sp.dma_start(wraw[:, n], t["sWo"][n * HH * SD:(n + 1) * HH * SD, :].rearrange("(h p) o -> p h o", p=P)).then_inc(w_loaded[n], 16)
            sp.dma_start(bo_b[:, :], t["sbo"].partition_broadcast(P)).then_inc(b_loaded, 16)

        @block.gpsimd
        def _(pool):
            nc.gpsimd.memset(shift[:, :], -ROUND).then_inc(shift_ready, 1)
            pool.wait_ge(b_loaded, 16)
            for n in range(2):
                hi, lo = (half(w, n) for w in W["o"])
                pool.wait_ge(w_hi, n + 1)
                nc.gpsimd.tensor_tensor(lo, wraw[:, n], f32(hi), ALU.subtract).then_inc(w_split, 1)
            for g in range(NG):
                x = X[:, g * GT:(g + 1) * GT, :]
                pool.wait_ge(xn_ready, g + 1)
                nc.gpsimd.tensor_tensor(x, x, bo_b[:, :].unsqueeze(1).broadcast_to([P, GT, D]), ALU.add).then_inc(bias_added, 1)
                if g == 1:
                    pool.wait_ge(x_hi, 1)
                    nc.gpsimd.tensor_tensor(x_l[:, :, :], xT[:, :, 0:GW], f32(x_h[:, :, :]), ALU.subtract).then_inc(x_split, 1)

        @block.scalar
        def _(act):
            def copy_ints(g):
                act.wait_ge(ints_turned, g + 1)
                act.activation(intsT[:, :, :], ps[:, 0:2, :], ACT.Identity, bias=shift[:, :]).then_inc(ints_copied, 1)

            def weights_hi(n):
                act.wait_ge(w_loaded[n], 16)
                act.activation(half(W["o"][0], n), wraw[:, n], ACT.Copy).then_inc(w_hi, 1)

            nc.scalar.preload_act_table(ACT.Sqrt)
            act.wait_ge(shift_ready, 1)
            copy_ints(0)
            weights_hi(0)
            for g in range(NG):
                tiles = slice(g * GT, (g + 1) * GT)
                if g + 1 < NG:
                    copy_ints(g + 1)
                act.wait_ge(var_ready, g + 1)
                act.activation(std[:, tiles], rstd[:, tiles], ACT.Sqrt).then_inc(std_ready, 1)
                if g == 0:
                    weights_hi(1)
                act.wait_ge(xn_turned, g + 1)
                bank = 4 + g % 2 * 2
                act.activation(xT[:, :, g * GW:(g + 1) * GW], ps[:, bank:bank + 2, :], ACT.Copy).then_inc(xn_copied, 1)
                if g == 1:
                    act.activation(x_h[:, :, :], xT[:, :, 0:GW], ACT.Copy).then_inc(x_hi, 1)

        @block.vector
        def _(dve):
            steps = Steps(dve, dve_step)

            for g in range(NG):
                tiles = slice(g * GT, (g + 1) * GT)
                dve.wait_ge(y_mm, g + 1)
                for j in range(GT):
                    n = g * GT + j
                    last = nc.vector.scalar_tensor_tensor(out=X[:, n, :], in0=ps[:, 2 + j // 2, j % 2 * D:(j % 2 + 1) * D],
                                                          scalar=so[:, n:n + 1], in1=X[:, n, :], op0=ALU.mult, op1=ALU.add)
                last.then_inc(y_added, 1)
                dve.wait_ge(y_added, g + 1)
                group_stats(nc, steps, X, stats, mv, g)
                nc.vector.tensor_scalar(rstd[:, tiles], mv[:, tiles, 1], EPS, None, ALU.add).then_inc(var_ready, 1)
                dve.wait_ge(std_ready, g + 1)
                steps.then(nc.vector.reciprocal(rstd[:, tiles], std[:, tiles]))
                if g:
                    dve.wait_ge(xn_turned, g)
                normalise(nc, X, mv, rstd, xn, g).then_inc(xn_ready, 1)

        @block.tensor
        def _(pe):
            def turn_ints(g):
                turn_group(nc, ps, 0, otok[:, g * GT:(g + 1) * GT, :], ident).then_inc(ints_turned, 1)

            def project(g):
                pe.wait_ge(ints_copied, g + 1)
                if g:
                    pe.wait_ge(y_added, g)
                project_ints(nc, ps, 2, intsT, (wpT_h, wpT_l)).then_inc(y_mm, 1)

            turn_ints(0)
            project(0)
            turn_ints(1)
            for g in range(NG):
                if g + 1 < NG:
                    project(g + 1)
                pe.wait_ge(xn_ready, g + 1)
                if g >= 2:
                    pe.wait_ge(xn_copied, g - 1)
                turn_group(nc, ps, 4 + g % 2 * 2, xn, ident).then_inc(xn_turned, 1)
                if g + 2 < NG:
                    turn_ints(g + 2)


def phase_self(nc, t, X, otok, so, wpT_h, wpT_l, ident, mv, rstd, ps, self_w):
    with ExitStack() as outer:
        sb = lambda n, s, d=F32: outer.enter_context(nc.sbuf_tensor(n, s, d))
        W = dict(self_w.W, o=[sb(f"sWo_{x}", [P, SH, D], F32R) for x in ("hi", "lo")])
        xT = sb("xT_self", [P, DC, T])
        x_h, x_l = sb("x_h", [P, DC, GW], F32R), sb("x_l", [P, DC, GW], F32R)
        phase_project(nc, t, X, otok, so, wpT_h, wpT_l, ident, mv, rstd, ps, xT, W, x_h, x_l)
        phase_attend(nc, t, X, ident, mv, ps, xT, W, x_h, x_l)


def phase_attend(nc, t, X, ident, mv, ps, xT, W, x_h, x_l):
    GB = GW // NQ
    NPROJ = GT + KV * (SG + 1)
    O_BANK = (4, 2, 3, 5)
    ctx = ExitStack()
    with ctx:
        sb = lambda n, s, d=F32: ctx.enter_context(nc.sbuf_tensor(n, s, d))
        sem = lambda n: ctx.enter_context(nc.semaphore(n))
        q = sb("q_self", [P, GB, SG, NQ])
        k = sb("k_self", [P, GW])
        o_h, o_l = sb("o_h", [P, SG, GW], F32R), sb("o_l", [P, SG, GW], F32R)
        v = sb("v_self", [P, GT, KV * SD])
        bq, bk = sb("sbq", [P, SH]), sb("sbk", [P, KV])
        bv_b = sb("sbv_b", [P, KV * SD])
        ones = sb("ones_self", [P, 1])
        smax = sb("smax", [P, GB])
        stats = sb("stats_s", [P, GT, 6])
        shifted = sb("shifted", [P, GB, NQ])
        probs = sb("probs_self", [P, GB, NQ])
        psum_, pinv = sb("prob_sum", [P, GB]), sb("prob_inv", [P, GB])
        pdiag = sb("pdiag", [P, GT, BT, P])
        b_loaded, ones_ready = sem("b_loaded"), sem("ones_ready")
        x_hi, x_split = sem("x_hi"), sem("x_split")
        proj_mm, proj_act, proj_dve = sem("proj_mm"), sem("proj_act"), sem("proj_dve")
        s_mm, s_max, s_shifted, s_exp, s_sum, s_inv, probs_ready = (sem(n) for n in (
            "s_mm", "s_max", "s_shifted", "s_exp", "s_sum", "s_inv", "probs_ready"))
        p_turned, pdiag_zero, pdiag_act, pdiag_dve = sem("p_turned"), sem("pdiag_zero"), sem("pdiag_act"), sem("pdiag_dve")
        o_mm, o_hi, o_split = sem("o_mm"), sem("o_hi"), sem("o_split")
        y_mm, y_added, dve_step = sem("y_mm"), sem("y_added"), sem("dve_step")
        block = ctx.enter_context(nc.Block())
        Y_CREDIT = 2

        def proj_index(kv, j):
            return kv * (SG + 1) + j + (GT if kv else 0)

        def value_index(j):
            return SG + 1 + j

        ON_ACT = [proj_index(kv, j) for kv in range(KV) for j in range(0, SG + 1, 2)]

        def copies(n):
            on_act = sum(m < n for m in ON_ACT)
            return on_act, n - on_act

        def by_batch(a):
            return a.rearrange("p (b n) -> p b n", b=GB)

        def groups(eng, one):
            one(0, None, True, False)
            with eng.Fori(0, NG - 2) as i:
                one(i + 1, i, False, False)
            one(NG - 1, NG - 2, False, True)

        def following(g, kv):
            return (g, kv + 1) if kv + 1 < KV else (g + 1, 0)

        @block.sync
        def _(sp):
            sp.dma_start(bq[:, :], t["sbq"]).then_inc(b_loaded, 16)
            sp.dma_start(bk[:, :], t["sbk"]).then_inc(b_loaded, 16)
            sp.dma_start(bv_b[:, :], t["sbv"].partition_broadcast(P)).then_inc(b_loaded, 16)

        @block.gpsimd
        def _(pool):
            pool.sem_inc(y_added, Y_CREDIT)
            nc.gpsimd.memset(ones[:, :], 1.0).then_inc(ones_ready, 1)
            nc.gpsimd.memset(pdiag[:, :, :, :], 0.0).then_inc(pdiag_zero, 1)
            pool.wait_ge(ones_ready, 1)
            for g in range(1, NG):
                cols = slice(g * GW, (g + 1) * GW)
                pool.wait_ge(proj_mm, g * NPROJ)
                nc.gpsimd.tensor_tensor(x_h[:, :, :], xT[:, :, cols], ones[:, :].unsqueeze(2).broadcast_to([P, DC, GW]),
                                        ALU.mult).then_inc(x_hi, 1)
                pool.wait_ge(x_hi, g)
                nc.gpsimd.tensor_tensor(x_l[:, :, :], xT[:, :, cols], f32(x_h[:, :, :]), ALU.subtract).then_inc(x_split, 1)

        @block.scalar
        def _(act):
            def project_copy(g, kv, j):
                if j % 2 == 0:
                    n = proj_index(kv, j)
                    act.wait_ge(proj_mm, g * NPROJ + n + 1)
                    dst, bias = (q[:, :, j, :], bq[:, kv * SG + j:kv * SG + j + 1]) if j < SG else (by_batch(k[:, :]), bk[:, kv:kv + 1])
                    act.activation(dst, by_batch(ps[:, n % 2, :]), ACT.Identity, bias=bias).then_inc(proj_act, 1)

            def one(g, before, first, last_group):
                for kv in range(KV):
                    act.wait_ge(s_shifted, g * KV + kv + 1)
                    act.activation(probs[:, :, :], shifted[:, :, :], ACT.Exp, scale=float(SD) ** -0.5).then_inc(s_exp, 1)
                    if not (last_group and kv == KV - 1):
                        for j in range(SG + 1):
                            project_copy(*following(g, kv), j)
                    act.wait_ge(p_turned, g * KV + kv + 1)
                    for b in range(2):
                        rows = slice(b * NQ, (b + 1) * NQ)
                        last = act.activation(pdiag[rows, :, b, :], ps[rows, 5, :].rearrange("p (j n) -> p j n", j=GT), ACT.Copy)
                    last.then_inc(pdiag_act, 1)
                    for j in range(GT):
                        act.wait_ge(o_mm, (g * KV + kv) * GT + j + 1)
                        dst = o_h[:, :, j * P:(j + 1) * P].rearrange("p h (b n) -> p b h n", b=BT)
                        act.activation(dst, ps[:, O_BANK[j], :].rearrange("p (b h n) -> p b h n", b=BT, h=SG), ACT.Copy).then_inc(o_hi, 1)

            act.wait_ge(b_loaded, 48)
            act.wait_ge(pdiag_zero, 1)
            for j in range(SG + 1):
                project_copy(0, 0, j)
            groups(act, one)

        @block.vector
        def _(dve):
            def project_copy(g, kv, j):
                if j % 2:
                    n = proj_index(kv, j)
                    dve.wait_ge(proj_mm, g * NPROJ + n + 1)
                    nc.vector.tensor_scalar(q[:, :, j, :], by_batch(ps[:, n % 2, :]), bq[:, kv * SG + j:kv * SG + j + 1], None,
                                            ALU.add).then_inc(proj_dve, 1)

            def values_copy(g):
                for j in range(GT):
                    dve.wait_ge(proj_mm, g * NPROJ + value_index(j) + 1)
                    nc.vector.tensor_tensor(v[:, j, :], ps[:, value_index(j) % 2, :], bv_b[:, :], ALU.add).then_inc(proj_dve, 1)

            def add_output(g, kv):
                for half in range(2):
                    dve.wait_ge(y_mm, (g * KV + kv) * 2 + half + 1)
                    x = X[:, bass.ds(g * GT + 2 * half, 2), :].rearrange("p n d -> p (n d)")
                    nc.vector.tensor_tensor(x, x, ps[:, 6 + half, :], ALU.add).then_inc(y_added, 1)

            def one(g, before, first, last_group):
                for kv in range(KV):
                    n = g * KV + kv + 1
                    more = not (last_group and kv == KV - 1)
                    scores = ps[:, 4, :].rearrange("p (b k) -> p b k", b=GB)
                    dve.wait_ge(s_mm, n)
                    nc.vector.tensor_reduce(smax[:, :], scores, AX, ALU.max).then_inc(s_max, 1)
                    dve.wait_ge(s_max, n)
                    nc.vector.tensor_tensor(shifted[:, :, :], scores, smax[:, :].unsqueeze(2).broadcast_to([P, GB, NQ]),
                                            ALU.subtract).then_inc(s_shifted, 1)
                    if more:
                        for j in range(2):
                            project_copy(*following(g, kv), j)
                    dve.wait_ge(s_exp, n)
                    nc.vector.tensor_reduce(psum_[:, :], probs[:, :, :], AX, ALU.add).then_inc(s_sum, 1)
                    dve.wait_ge(s_sum, n)
                    nc.vector.reciprocal(pinv[:, :], psum_[:, :]).then_inc(s_inv, 1)
                    dve.wait_ge(s_inv, n)
                    nc.vector.tensor_tensor(probs[:, :, :], probs[:, :, :], pinv[:, :].unsqueeze(2).broadcast_to([P, GB, NQ]),
                                            ALU.mult).then_inc(probs_ready, 1)
                    if more:
                        for j in range(2, SG + 1):
                            project_copy(*following(g, kv), j)
                    dve.wait_ge(p_turned, n)
                    dve.wait_ge(pdiag_act, n)
                    for b in range(2, BT):
                        rows = slice(b * NQ, (b + 1) * NQ)
                        last = nc.vector.tensor_copy(pdiag[rows, :, b, :], ps[rows, 5, :].rearrange("p (j n) -> p j n", j=GT))
                    last.then_inc(pdiag_dve, 1)
                    if kv:
                        add_output(g, kv - 1)
                    elif not first:
                        add_output(before, KV - 1)
                    if last_group and kv:
                        dve.wait_ge(y_added, (NG - 1) * KV * 2 + Y_CREDIT)
                        group_stats(nc, steps, X, stats, mv, kv - 1)
                    for j in range(GT):
                        dve.wait_ge(o_hi, (g * KV + kv) * GT + j + 1)
                        dst = o_l[:, :, j * P:(j + 1) * P].rearrange("p h (b n) -> p b h n", b=BT)
                        hi = f32(o_h[:, :, j * P:(j + 1) * P]).rearrange("p h (b n) -> p b h n", b=BT)
                        nc.vector.tensor_tensor(dst, ps[:, O_BANK[j], :].rearrange("p (b h n) -> p b h n", b=BT, h=SG), hi,
                                                ALU.subtract).then_inc(o_split, 1)
                    if kv == KV - 1 and not last_group:
                        values_copy(g + 1)

            steps = Steps(dve, dve_step)
            dve.wait_ge(b_loaded, 48)
            dve.wait_ge(pdiag_zero, 1)
            for j in range(SG + 1):
                project_copy(0, 0, j)
            values_copy(0)
            groups(dve, one)
            add_output(NG - 1, KV - 1)

        @block.tensor
        def _(pe):
            x2, o2 = (x_h, x_l), (o_h, o_l)

            def copied(g, n):
                on_act, on_dve = copies(n + 1)
                if n in ON_ACT:
                    pe.wait_ge(proj_act, g * copies(NPROJ)[0] + on_act)
                else:
                    pe.wait_ge(proj_dve, g * copies(NPROJ)[1] + on_dve)

            def bank_free(g, n):
                if n >= 2:
                    copied(g, n - 2)

            def project(g, kv):
                if kv == 0 and not (isinstance(g, int) and g == 0):
                    pe.wait_ge(x_split, g)
                for j in range(SG + 1):
                    n = proj_index(kv, j)
                    bank_free(g, n)
                    w, col = (W["q"], (kv * SG + j) * SD) if j < SG else (W["k"], kv * SD)
                    for m, (c, (a, b)) in enumerate((c, x) for c in range(DC) for x in THREE):
                        last = nc.tensor.matmul(ps[:, n % 2, :], w[a][:, c, col:col + SD], x2[b][:, c, :],
                                                start=m == 0, stop=m == 3 * DC - 1)
                    last.then_inc(proj_mm, 1)

            def values(g):
                for j in range(GT):
                    n = value_index(j)
                    bank_free(g, n)
                    for m, (c, (a, b)) in enumerate((c, x) for c in range(DC) for x in THREE):
                        last = nc.tensor.matmul(ps[:, n % 2, :], x2[a][:, c, j * P:(j + 1) * P], W["v"][b][:, c, :],
                                                start=m == 0, stop=m == 3 * DC - 1)
                    last.then_inc(proj_mm, 1)

            def score(g, kv):
                copied(g, proj_index(kv, SG - 1))
                copied(g, proj_index(kv, SG))
                for b in range(GB):
                    cols = slice(b * NQ, min(b * NQ + P, GW))
                    last = nc.tensor.matmul(ps[:, 4, cols], q[:, b].rearrange("p h n -> p (h n)"), k[:, cols], start=True, stop=True)
                last.then_inc(s_mm, 1)

            def project_output(g, kv):
                for j in range(GT):
                    if j % 2 == 0:
                        pe.wait_ge(y_added, (g * KV + kv) * 2 + j // 2 + 1)
                    for m, (h, (a, b)) in enumerate((h, x) for h in range(SG) for x in THREE):
                        last = nc.tensor.matmul(ps[:, 6 + j // 2, j % 2 * D:(j % 2 + 1) * D], o2[a][:, h, j * P:(j + 1) * P],
                                                W["o"][b][:, kv * SG + h, :], start=m == 0, stop=m == 3 * SG - 1)
                    if j % 2:
                        last.then_inc(y_mm, 1)

            def one(g, before, first, last_group):
                for kv in range(KV):
                    n = g * KV + kv
                    more = not (last_group and kv == KV - 1)
                    start = first and kv == 0
                    if more:
                        project(*following(g, kv))
                    if not start:
                        pe.wait_ge(o_split, n * GT)
                    if not more:
                        project_output(g, kv - 1)
                    pe.wait_ge(probs_ready, n + 1)
                    for j in range(GT):
                        last = nc.tensor.transpose(ps[:, 5, j * P:(j + 1) * P],
                                                   probs[:, j * BT:(j + 1) * BT, :].rearrange("p b k -> p (b k)"), ident[:, :])
                    last.then_inc(p_turned, 1)
                    if kv and more:
                        project_output(g, kv - 1)
                    elif kv == 0 and not first:
                        project_output(before, KV - 1)
                    pe.wait_ge(pdiag_act, n + 1)
                    pe.wait_ge(pdiag_dve, n + 1)
                    for j in range(GT):
                        nc.tensor.matmul(ps[:, O_BANK[j], :], v[:, j, kv * SD:(kv + 1) * SD], pdiag[:, j].rearrange("p b n -> p (b n)"),
                                         start=True, stop=True).then_inc(o_mm, 1)
                    if more:
                        if kv == KV - 1:
                            values(g + 1)
                        pe.wait_ge(o_split, n * GT + 1)
                        score(*following(g, kv))

            project(0, 0)
            values(0)
            score(0, 0)
            groups(pe, one)
            pe.wait_ge(o_split, NG * KV * GT)
            project_output(NG - 1, KV - 1)


class ExpertWeights:
    SHAPES = {"g": [P, DC, BW], "u": [P, DC, BW], "d": [P, SB, D]}

    def __init__(self, nc, t, ctx):
        sb = lambda n, s, d=F32: ctx.enter_context(nc.sbuf_tensor(n, s, d))
        self.nc, self.t = nc, t
        self.raw = {n: sb(f"raw_{n}", s) for n, s in self.SHAPES.items()}
        self.hi = {n: sb(f"hi_{n}", [s[0], 2, *s[1:]], F32R) for n, s in self.SHAPES.items()}
        self.lo = {n: sb(f"lo_{n}", [s[0], 2, *s[1:]], F32R) for n, s in self.SHAPES.items()}
        self.ones = sb("ones", [P, 1])
        self.loaded, self.hi_done, self.split_done, self.ones_ready = (ctx.enter_context(nc.semaphore(n)) for n in (
            "ew_loaded", "ew_hi", "ew_split", "ew_ones"))

    def load(self, sp, k):
        units = bass.ds(k * BW, BW)
        for n in ("g", "u"):
            sp.dma_start(self.raw[n][:, :, :], self.t["eW" + n][:, units].rearrange("(c p) n -> p c n", p=P)).then_inc(self.loaded, 16)
        sp.dma_start(self.raw["d"][:, :, :], self.t["eWd"][units, :].rearrange("(s p) d -> p s d", p=P)).then_inc(self.loaded, 16)

    def split(self, pool, k, slot):
        pool.wait_ge(self.loaded, (k + 1) * 16 * len(self.SHAPES))
        for n in self.SHAPES:
            r = self.raw[n][:, :, :]
            one = self.ones[:, :].unsqueeze(2).broadcast_to(list(r.shape))
            self.nc.gpsimd.tensor_tensor(self.hi[n][:, slot], r, one, ALU.mult).then_inc(self.hi_done, 1)
        pool.wait_ge(self.hi_done, (k + 1) * len(self.SHAPES))
        for n in self.lo:
            last = self.nc.gpsimd.tensor_tensor(self.lo[n][:, slot], self.raw[n][:, :, :], f32(self.hi[n][:, slot]), ALU.subtract)
        last.then_inc(self.split_done, 1)


def phase_experts(nc, t, X, ident, mv, rstd, ps, out):
    with ExitStack() as outer:
        sb = lambda n, s, d=F32: outer.enter_context(nc.sbuf_tensor(n, s, d))
        x_h, x_l = sb("xe_h", [P, DC, T], F32R), sb("xe_l", [P, DC, T], F32R)
        cw = sb("cw", [P, 2, T])
        weights = ExpertWeights(nc, t, outer)
        phase_route(nc, t, X, ident, mv, rstd, ps, x_h, x_l, cw, weights)
        phase_mix(nc, X, ps, x_h, x_l, cw, weights, out)


def phase_route(nc, t, X, ident, mv, rstd, ps, x_h, x_l, cw, weights):
    TOP = 4
    ctx = ExitStack()
    with ctx:
        sb = lambda n, s, d=F32: ctx.enter_context(nc.sbuf_tensor(n, s, d))
        sem = lambda n: ctx.enter_context(nc.semaphore(n))
        gate = sb("gate", [P, DC, NE])
        stats = sb("stats_r", [P, GT, 6])
        std = sb("std_r", [P, NT])
        xn = sb("xn_r", [P, 2, GT, D])
        x32 = sb("x32", [P, 2, DC, GW])
        logits = sb("logits", [P, NT, NE])
        key = sb("key", [P, NT, NE])
        top = sb("top", [P, NT, 8])
        PAD = NE // 2
        above = sb("above", [P, NT, NE])
        equal, *scan = (sb(n, [P, NT, PAD + NE]) for n in ("equal", "scan0", "scan1"))
        count = sb("count", [P, NT])
        left = sb("left", [P, NT])
        first, chosen = sb("first", [P, NT, NE]), sb("chosen", [P, NT, NE])
        shifted, expd, soft, weight = (sb(n, [P, NT, NE]) for n in ("shift_r", "expd", "soft", "weight"))
        small = sb("small", [P, NT, NC])
        norm, inv = sb("norm_r", [P, NT]), sb("inv_r", [P, NT])
        by_unit = sb("by_unit", [P, NT, NE, EP])
        small_by_unit = sb("small_by_unit", [P, NT, NC, CP])
        g_loaded, dve_step, var_ready, std_ready = sem("g_loaded"), sem("dve_step"), sem("var_ready"), sem("std_ready")
        xn_ready, xn_turned, x_hi, x_split = sem("xn_ready"), sem("xn_turned"), sem("x_hi"), sem("x_split")
        x_copied, l_mm, l_ready, pads_ready = sem("x_copied"), sem("l_mm"), sem("l_ready"), sem("pads_ready")
        shift_ready, exp_ready, weight_ready, by_unit_ready, cw_turned, cw_act, cw_dve = (sem(n) for n in (
            "shift_ready", "exp_ready", "weight_ready", "by_unit_ready", "cw_turned", "cw_act", "cw_dve"))
        small_ready = sem("small_ready")
        block = ctx.enter_context(nc.Block())

        @block.sync
        def _(sp):
            sp.dma_start(gate[:, :, :], t["gateT"].rearrange("(c p) e -> p c e", p=P)).then_inc(g_loaded, 16)
            weights.load(sp, 0)

        @block.gpsimd
        def _(pool):
            nc.gpsimd.memset(weights.ones[:, :], 1.0).then_inc(weights.ones_ready, 1)
            for a in (equal, *scan):
                nc.gpsimd.memset(a[:, :, 0:PAD], 0.0).then_inc(pads_ready, 1)
            pool.wait_ge(weights.ones_ready, 1)
            weights.split(pool, 0, 0)

        @block.scalar
        def _(act):
            for n, tiles in enumerate((slice(0, NT - GT), slice(NT - GT, NT))):
                act.wait_ge(var_ready, n + 1)
                act.activation(std[:, tiles], rstd[:, tiles], ACT.Sqrt).then_inc(std_ready, 1)
            for g in range(NG):
                bank = g % 2 * 2
                act.wait_ge(xn_turned, g + 1)
                act.activation(x_h[:, :, g * GW:(g + 1) * GW], ps[:, bank:bank + 2, :], ACT.Copy).then_inc(x_hi, 1)
                if g >= 2:
                    act.wait_ge(l_mm, g - 1)
                act.activation(x32[:, g % 2], ps[:, bank:bank + 2, :], ACT.Copy).then_inc(x_copied, 1)
            act.wait_ge(shift_ready, 1)
            act.activation(expd[:, :, :], shifted[:, :, :], ACT.Exp).then_inc(exp_ready, 1)
            act.wait_ge(weight_ready, 1)
            for g in range(NG):
                tiles = slice(g * GT, (g + 1) * GT)
                act.activation(by_unit[:, tiles].rearrange("p n e u -> p (n e) u"),
                               weight[:, tiles, :].rearrange("p n e -> p (n e)").unsqueeze(2).broadcast_to([P, GT * NE, EP]),
                               ACT.Copy).then_inc(by_unit_ready, 1)
            for g in range(NG):
                act.wait_ge(cw_turned, g + 1)
                act.activation(cw[:, 0, g * GW:(g + 1) * GW], ps[:, g, :], ACT.Copy).then_inc(cw_act, 1)

        @block.vector
        def _(dve):
            steps = Steps(dve, dve_step)

            def split(g):
                dve.wait_ge(x_copied, g + 1)
                cols, bank = slice(g * GW, (g + 1) * GW), g % 2 * 2
                nc.vector.tensor_tensor(x_l[:, :, cols], ps[:, bank:bank + 2, :], f32(x_h[:, :, cols]), ALU.subtract).then_inc(x_split, 1)

            def take_logits(g):
                dve.wait_ge(l_mm, g + 1)
                nc.vector.tensor_copy(logits[:, g * GT:(g + 1) * GT, :], ps[:, 4 + g, 0:GT * NE].rearrange("p (j e) -> p j e", j=GT)) \
                    .then_inc(l_ready, 1)

            early, late = slice(0, NT - GT), slice(NT - GT, NT)
            nc.vector.tensor_scalar(rstd[:, early], mv[:, early, 1], EPS, None, ALU.add).then_inc(var_ready, 1)
            group_stats(nc, steps, X, stats, mv, NG - 1)
            nc.vector.tensor_scalar(rstd[:, late], mv[:, late, 1], EPS, None, ALU.add).then_inc(var_ready, 1)
            for n, tiles in enumerate((early, late)):
                dve.wait_ge(std_ready, n + 1)
                steps.then(nc.vector.reciprocal(rstd[:, tiles], std[:, tiles]))
            for g in range(NG):
                normalise(nc, X, mv, rstd, xn[:, g % 2], g).then_inc(xn_ready, 1)
                if g:
                    split(g - 1)
            split(NG - 1)
            for g in range(NG):
                take_logits(g)
            dve.wait_ge(l_ready, NG)
            v = nc.vector
            all_ = lambda a: a[:, :, :]
            over = lambda a: a.unsqueeze(2).broadcast_to([P, NT, NE])
            steps.then(v.tensor_reduce(norm[:, :], all_(logits), AX, ALU.max))
            v.tensor_tensor(all_(shifted), all_(logits), over(norm[:, :]), ALU.subtract).then_inc(shift_ready, 1)
            steps.then(v.tensor_scalar(all_(key), all_(logits), SATURATED, None, ALU.min))
            for n in range(NT):
                last = v.max(top[:, n, :], key[:, n, :])
            steps.then(last)
            fourth = over(top[:, :, TOP - 1])
            row = lambda a, s=0: a[:, :, PAD - s:PAD + NE - s]
            dve.wait_ge(pads_ready, 3)
            steps.then(v.tensor_tensor(all_(above), all_(key), fourth, ALU.is_gt))
            steps.then(v.tensor_tensor(row(equal), all_(key), fourth, ALU.is_equal))
            steps.then(v.tensor_reduce(count[:, :], all_(above), AX, ALU.add))
            steps.then(v.tensor_scalar(left[:, :], count[:, :], -1.0, float(TOP), ALU.mult, ALU.add))
            src, s = equal, 1
            while s < NE:
                dst = scan[0] if src is not scan[0] else scan[1]
                steps.then(v.tensor_tensor(row(dst), row(src), row(src, s), ALU.add))
                src, s = dst, 2 * s
            steps.then(v.tensor_tensor(all_(first), row(src), over(left[:, :]), ALU.is_le))
            steps.then(v.tensor_tensor(all_(first), all_(first), row(equal), ALU.mult))
            steps.then(v.tensor_tensor(all_(chosen), all_(first), all_(above), ALU.add))
            dve.wait_ge(exp_ready, 1)
            steps.then(v.tensor_reduce(norm[:, :], all_(expd), AX, ALU.add))
            steps.then(v.reciprocal(inv[:, :], norm[:, :]))
            steps.then(v.tensor_tensor(all_(soft), all_(expd), over(inv[:, :]), ALU.mult))
            steps.then(v.tensor_tensor(all_(soft), all_(soft), all_(chosen), ALU.mult))
            steps.then(v.tensor_reduce(norm[:, :], all_(soft), AX, ALU.add))
            steps.then(v.reciprocal(inv[:, :], norm[:, :]))
            v.tensor_tensor(all_(weight), all_(soft), over(inv[:, :]), ALU.mult).then_inc(weight_ready, 1)
            dve.wait_ge(weight_ready, 1)
            pairs = all_(weight).rearrange("p n (c two) -> p n c two", two=2)
            steps.then(v.tensor_reduce(all_(small), pairs, AX, ALU.add))
            for g in range(NG):
                tiles = slice(g * GT, (g + 1) * GT)
                v.tensor_scalar(small_by_unit[:, tiles].rearrange("p n c u -> p (n c) u"),
                                small[:, tiles, :].rearrange("p n c -> p (n c)").unsqueeze(2).broadcast_to([P, GT * NC, CP]),
                                SMALL_SCALE, None, ALU.mult).then_inc(small_ready, 1)
            for g in range(NG):
                dve.wait_ge(cw_turned, NG + g + 1)
                v.tensor_copy(cw[:, 1, g * GW:(g + 1) * GW], ps[:, 4 + g, :]).then_inc(cw_dve, 1)

        @block.tensor
        def _(pe):
            def turn(g):
                pe.wait_ge(xn_ready, g + 1)
                if g >= 2:
                    pe.wait_ge(x_split, g - 1)
                    pe.wait_ge(x_copied, g - 1)
                turn_group(nc, ps, g % 2 * 2, xn[:, g % 2], ident).then_inc(xn_turned, 1)

            turn(0)
            pe.wait_ge(g_loaded, 16)
            for g in range(NG):
                if g + 1 < NG:
                    turn(g + 1)
                pe.wait_ge(x_copied, g + 1)
                for j in range(GT):
                    for c in range(DC):
                        last = nc.tensor.matmul(ps[:, 4 + g, j * NE:(j + 1) * NE], x32[:, g % 2, c, j * P:(j + 1) * P], gate[:, c, :],
                                                start=c == 0, stop=c == DC - 1)
                last.then_inc(l_mm, 1)
            for bank, ready, src in ((0, by_unit_ready, by_unit), (4, small_ready, small_by_unit)):
                for g in range(NG):
                    pe.wait_ge(ready, g + 1)
                    for j in range(GT):
                        last = nc.tensor.transpose(ps[:, bank + g, j * P:(j + 1) * P],
                                                   src[:, g * GT + j].rearrange("p e u -> p (e u)"), ident[:, :])
                    last.then_inc(cw_turned, 1)


def phase_mix(nc, X, ps, x_h, x_l, cw, weights, out):
    ctx = ExitStack()
    with ctx:
        sb = lambda n, s, d=F32: ctx.enter_context(nc.sbuf_tensor(n, s, d))
        sem = lambda n: ctx.enter_context(nc.semaphore(n))
        hi, lo = weights.hi, weights.lo
        silu = sb("silu", [P, 2, GW])
        gated = sb("gated", [P, 2, GW])
        a = sb("act_raw", [P, 2, SB, GW])
        a_h, a_l = sb("act_h", [P, 2, SB, GW], F32R), sb("act_l", [P, 2, SB, GW], F32R)
        g_mm, u_mm, silu_ready, gated_ready, a_ready, a_hi, a_split = (sem(n) for n in (
            "g_mm", "u_mm", "silu_ready", "gated_ready", "a_ready", "a_hi", "a_split"))
        y_mm, y_added, stored = sem("y_mm"), sem("y_added"), sem("stored")
        block = ctx.enter_context(nc.Block())
        GATED_CREDIT = 2
        A_SPLIT_CREDIT = 2 * SB
        Y_MM_CREDIT = 2 * 2
        Y_ADDED_CREDIT = 2
        UNITS = NG

        @block.sync
        def _(sp):
            with sp.Fori(0, NBLK - 1) as k:
                sp.wait_ge(weights.split_done, k + 1)
                weights.load(sp, k + 1)
            for g in range(NG):
                sp.wait_ge(y_added, ((NBLK - 1) * UNITS + g + 1) * 2 + Y_ADDED_CREDIT)
                sp.dma_start(out[g * GW:(g + 1) * GW, :].rearrange("(n p) d -> p n d", p=P), X[:, g * GT:(g + 1) * GT, :]).then_inc(stored, 16)
            sp.wait_ge(stored, 16 * NG)

        @block.gpsimd
        def _(pool):
            pool.sem_inc(gated_ready, GATED_CREDIT)
            pool.sem_inc(a_split, A_SPLIT_CREDIT)
            pool.sem_inc(y_mm, Y_MM_CREDIT)
            pool.sem_inc(y_added, Y_ADDED_CREDIT)

            def split_activations(k, ks):
                with pool.Fori(0, UNITS // 2) as gg:
                    for gu in range(2):
                        for s in range(SB):
                            pool.wait_ge(a_hi, (k * UNITS + gg * 2 + gu) * SB + s + 1)
                            nc.gpsimd.tensor_tensor(a_l[:, gu, s, :], a[:, gu, s, :], f32(a_h[:, gu, s, :]), ALU.subtract).then_inc(a_split, 1)

            with pool.Fori(0, NBLK // 2 - 1) as kk:
                for ks in range(2):
                    k = kk * 2 + ks
                    pool.wait_ge(y_mm, k * UNITS * 2 + Y_MM_CREDIT)
                    weights.split(pool, k + 1, 1 - ks)
                    split_activations(k, ks)
            k = NBLK - 2
            pool.wait_ge(y_mm, k * UNITS * 2 + Y_MM_CREDIT)
            weights.split(pool, k + 1, 1)
            split_activations(k, 0)
            split_activations(k + 1, 1)

        @block.scalar
        def _(act):
            with act.Fori(0, NBLK * UNITS // 2) as pair:
                for gu in range(2):
                    unit = pair * 2 + gu
                    for s in range(SB):
                        act.wait_ge(g_mm, unit * SB + s + 1)
                        act.activation(silu[:, s % 2, :], ps[:, s % 2, :], ACT.Silu).then_inc(silu_ready, 1)
                        act.wait_ge(a_ready, unit * SB + s + 1)
                        act.wait_ge(y_mm, unit * 2 + 2)
                        act.activation(a_h[:, gu, s, :], a[:, gu, s, :], ACT.Copy).then_inc(a_hi, 1)

        @block.vector
        def _(dve):
            def unit_of(kind, k, gg, gu):
                g = gg * 2 + gu
                unit = k * UNITS + g
                for s in range(SB):
                    n = unit * SB + s + 1
                    dve.wait_ge(silu_ready, n)
                    dve.wait_ge(u_mm, n)
                    nc.vector.tensor_tensor(gated[:, s % 2, :], silu[:, s % 2, :], ps[:, 2 + s % 2, :], ALU.mult).then_inc(gated_ready, 1)
                    dve.wait_ge(gated_ready, n + GATED_CREDIT)
                    dve.wait_ge(a_split, n)
                    nc.vector.tensor_tensor(a[:, gu, s, :], gated[:, s % 2, :], cw[:, kind, bass.ds(g * GW, GW)], ALU.mult).then_inc(a_ready, 1)

            def add_output(k, gg, gu):
                unit = k * UNITS + gg * 2 + gu
                for half in range(2):
                    dve.wait_ge(y_mm, unit * 2 + half + 1 + Y_MM_CREDIT)
                    x = X[:, bass.ds((gg * 2 + gu) * GT + 2 * half, 2), :].rearrange("p n d -> p (n d)")
                    nc.vector.tensor_tensor(x, x, ps[:, 6 + half, :], ALU.add).then_inc(y_added, 1)

            for kind, start, blocks in ((0, 0, LARGE_BLK), (1, LARGE_BLK, NBLK - LARGE_BLK)):
                with dve.Fori(0, blocks) as i:
                    with dve.Fori(0, UNITS // 2) as gg:
                        for gu in range(2):
                            unit_of(kind, i + start, gg, gu)
                        for gu in range(2):
                            add_output(i + start, gg, gu)

        @block.tensor
        def _(pe):
            x2 = (x_h, x_l)
            w2 = {n: (hi[n], lo[n]) for n in lo}
            with pe.Fori(0, NBLK // 2) as kk:
                for ks in range(2):
                    k = kk * 2 + ks
                    with pe.Fori(0, UNITS // 2) as gg:
                        pe.wait_ge(weights.split_done, k + 1)
                        for gu in range(2):
                            cols = bass.ds((gg * 2 + gu) * GW, GW)
                            for s in range(SB):
                                n = (k * UNITS + gg * 2 + gu) * SB + s + 1
                                units = slice(s * P, (s + 1) * P)
                                pe.wait_ge(gated_ready, n)
                                for name, bank, done in (("g", s % 2, g_mm), ("u", 2 + s % 2, u_mm)):
                                    for m, (c, (i, j)) in enumerate((c, x) for c in range(DC) for x in THREE):
                                        last = nc.tensor.matmul(ps[:, bank, :], w2[name][i][:, ks, c, units], x2[j][:, c, cols],
                                                                start=m == 0, stop=m == 3 * DC - 1)
                                    last.then_inc(done, 1)
                        for gu in range(2):
                            unit = k * UNITS + gg * 2 + gu
                            pe.wait_ge(a_split, unit * SB + SB + A_SPLIT_CREDIT)
                            for j in range(GT):
                                if j % 2 == 0:
                                    pe.wait_ge(y_added, unit * 2 + j // 2 + 1)
                                for m, (s, (x, y)) in enumerate((s, x) for s in range(SB) for x in THREE):
                                    last = nc.tensor.matmul(ps[:, 6 + j // 2, j % 2 * D:(j % 2 + 1) * D],
                                                            (a_h, a_l)[x][:, gu, s, j * P:(j + 1) * P], w2["d"][y][:, ks, s, :],
                                                            start=m == 0, stop=m == 3 * SB - 1)
                                if j % 2:
                                    last.then_inc(y_mm, 1)


def kernel(**inputs):
    import numpy as np
    import concourse.bacc as bacc
    from concourse.bass_utils import run_bass_kernel_spmd
    a = {k: np.asarray(v) for k, v in inputs.items()}
    wkvT = a["L0_xattn_wkv"].T
    up = lambda w, n: w.reshape(len(w), D, -1, n).transpose(1, 2, 0, 3).reshape(D, -1)
    down = lambda w, n: w.reshape(len(w), -1, n, D).transpose(1, 0, 2, 3).reshape(-1, D)
    arrays = {
        "x": a["x"].reshape(T, D),
        "ctxT": a["ctx_2048"].transpose(0, 2, 1),
        "clast": a["ctx_2048"][:, NK - 1, :].T,
        "xwq": a["L0_xattn_wq"], "xwp": a["L0_xattn_wp"], "wkvT": wkvT, "wvT": wkvT[:, D:],
        "xbq": a["L0_xattn_bq"], "xbk": a["L0_xattn_bkv"][:D].reshape(DC, P).T, "xbv": a["L0_xattn_bkv"][D:],
        "xbp": a["L0_xattn_bp"],
        "sWqkv": np.concatenate([a["L0_attn_Wq"], a["L0_attn_Wk"], a["L0_attn_Wv"]], axis=1), "sWo": a["L0_attn_Wo"],
        "sbq": a["L0_attn_bq"].reshape(SH, SD).T, "sbk": a["L0_attn_bk"].reshape(KV, SD).T, "sbv": a["L0_attn_bv"],
        "sbo": a["L0_attn_bo"],
        "gateT": a["L0_ffn_gate_w"].T,
        "eWg": np.concatenate([up(a["L0_ffn_Wg"], EP), up(a["L0_ffn_cWg"], CP)], axis=1),
        "eWu": np.concatenate([up(a["L0_ffn_Wu"], EP), up(a["L0_ffn_cWu"], CP)], axis=1),
        "eWd": np.concatenate([down(a["L0_ffn_Wd"], EP), down(a["L0_ffn_cWd"], CP)]),
    }
    arrays = {f"in_{k}": np.ascontiguousarray(v) for k, v in arrays.items()}
    nc = bacc.Bacc("TRN2", target_bir_lowering=False, num_devices=1)
    t = {k[3:]: nc.dram_tensor(k, v.shape, mybir.dt.from_np(v.dtype), kind="ExternalInput").ap() for k, v in arrays.items()}
    out = nc.dram_tensor("out", (T, D), F32, kind="ExternalOutput").ap()
    program(nc, t, out)
    got = run_bass_kernel_spmd(nc, [arrays], core_ids=[0])
    return got.results[0]["out"].reshape(NB, NQ, D)
```
